# Optimizing a Trainium2 kernel written in Bass

```python
import numpy as np
import jax
import jax.numpy as jnp

def _softmax(x, axis=-1):
    return jax.nn.softmax(x, axis=axis)

def _gelu(x):
    return jax.nn.gelu(x, approximate=True)

def _silu(x):
    return jax.nn.silu(x)

def _sigmoid(x):
    return jax.nn.sigmoid(x)

def _layernorm(x, axis=-1, eps=1e-05):
    m = jnp.mean(x, axis=axis, keepdims=True)
    v = jnp.var(x, axis=axis, keepdims=True)
    return (x - m) / jnp.sqrt(v + eps)

def _scatter_add(tgt, idx, src, axis=0):
    return tgt.at[idx].add(src)

def _segment_sum(src, seg, n):
    return jax.ops.segment_sum(src, seg, n)
kernel_name = 'mk_xattn_ffn_d1_seqx_r8_77ffc2'

def setup_inputs(seed: int=0):
    np.random.seed(seed)
    _w = jnp.asarray

    def _rec_inputs():
        import jax
        import jax.numpy as jnp
        _rk = jax.random.key(seed)
        x = -0.0002928 + 1 * jax.random.normal(jax.random.fold_in(_rk, 1), (64, 64, 128), jnp.float32)
        _lenS = 64 - jax.random.randint(jax.random.fold_in(_rk, 7), (64,), 0, max(1, 64 // 4) + 1, jnp.int32)
        _lenS2 = 64 - jax.random.randint(jax.random.fold_in(_rk, 8), (64,), 0, max(1, 64 // 4) + 1, jnp.int32)
        _ctx_1024P = jax.random.normal(jax.random.fold_in(_rk, 11), (64, 16, 128), jnp.float32)
        _ctx_1024c = jax.random.dirichlet(jax.random.fold_in(_rk, 511), 0.3 * jnp.ones((16,), jnp.float32), (64, 64))
        _ctx_1024t = jnp.einsum('bsk,bkd->bsd', _ctx_1024c, _ctx_1024P)
        _ctx_1024t = _ctx_1024t * jax.lax.rsqrt(jnp.mean(jnp.square(_ctx_1024t)) + 1e-12) * 0.953939
        ctx_1024 = -1.39393e-06 + 0.999914 * (_ctx_1024t + 0.3 * jax.random.normal(jax.random.fold_in(_rk, 611), (64, 64, 128), jnp.float32))
        return (x, ctx_1024)
    x, ctx_1024 = _rec_inputs()

    def _L0_xattn_setup():
        import jax, jax.numpy as jnp
        import numpy as np
        B, S, H, NH = (2, 256, 128, 4)
        DH = H // NH
        EPS = 1e-06

        def _parallel_stabilized(qh, kh, vh, ig, fg):
            log_fg = jax.nn.log_sigmoid(fg)
            cs = jnp.cumsum(log_fg, axis=2)
            ltr = jnp.tril(jnp.ones((qh.shape[2], qh.shape[2]), dtype=bool))
            log_fg_mat = jnp.where(ltr, cs - jnp.swapaxes(cs, 2, 3), -jnp.inf)
            log_D = log_fg_mat + jnp.swapaxes(ig, 2, 3)
            max_log_D = jnp.max(log_D, axis=-1, keepdims=True)
            D = jnp.exp(log_D - max_log_D)
            qk = jnp.einsum('bhsd,bhtd->bhst', qh, kh) / jnp.sqrt(jnp.float32(DH))
            C = qk * D
            normalizer = jnp.maximum(jnp.abs(jnp.sum(C, axis=-1, keepdims=True)), jnp.exp(-max_log_D))
            return jnp.einsum('bhst,bhtd->bhsd', C / (normalizer + EPS), vh)
        key = jax.random.key(seed)
        ks = jax.random.split(key, 6)
        q = jax.random.normal(ks[0], (B, S, H), dtype=jnp.float32)
        k = jax.random.normal(ks[1], (B, S, H), dtype=jnp.float32)
        v = jax.random.normal(ks[2], (B, S, H), dtype=jnp.float32)
        igate_kernel = jax.random.normal(ks[3], (3 * H, NH), dtype=jnp.float32) * 0.02
        fgate_kernel = jax.random.normal(ks[4], (3 * H, NH), dtype=jnp.float32) * 0.02
        igate_bias = jax.random.normal(ks[5], (NH,), dtype=jnp.float32) * 0.1
        fgate_bias = jnp.linspace(3.0, 6.0, NH, dtype=jnp.float32)
        outnorm_scale = jnp.ones((H,), dtype=jnp.float32)
        return {'q': q, 'k': k, 'v': v, 'igate_kernel': igate_kernel, 'igate_bias': igate_bias, 'fgate_kernel': fgate_kernel, 'fgate_bias': fgate_bias, 'outnorm_scale': outnorm_scale}
    _L0_xattn_all = _L0_xattn_setup()
    _L0_xattn_in = {k: v for k, v in _L0_xattn_all.items() if k in ('igate_kernel', 'igate_bias', 'fgate_kernel', 'fgate_bias', 'outnorm_scale')}
    del _L0_xattn_all

    def _L0_ffn_setup():
        import jax, jax.numpy as jnp
        import numpy as np
        DIM = 128
        DEPTH = 6
        HEADS = 16
        DIM_HEAD = 64
        WINDOW = 32
        INNER = HEADS * DIM_HEAD
        DIM_INNER = int(DIM * 4 * 2 / 3)
        QK_SCALE = 8.0

        def shift_tokens(t):
            a, s = jnp.split(t, 2, -1)
            s = jnp.pad(s, ((0, 0), (1, 0), (0, 0)))[:, :-1]
            return jnp.concatenate([a, s], -1)

        def l2norm(t):
            return t / jnp.maximum(jnp.linalg.norm(t, axis=-1, keepdims=True), 1e-12)

        def rotate_half(x):
            x1, x2 = jnp.split(x, 2, -1)
            return jnp.concatenate([-x2, x1], -1)

        def rotary_tables(n):
            half = jnp.arange(0, DIM_HEAD, 2, dtype=jnp.float32)
            inv_freq = 1.0 / 10000.0 ** (half / DIM_HEAD)
            t = jnp.arange(n, dtype=jnp.float32)
            freqs = t[:, None] * inv_freq[None, :]
            freqs = jnp.concatenate([freqs, freqs], -1)
            base_scale = (half + 0.4 * DIM_HEAD) / (1.4 * DIM_HEAD)
            power = (t - n // 2) / (WINDOW // 2)
            scale = base_scale[None, :] ** power[:, None]
            scale = jnp.concatenate([scale, scale], -1)
            return (freqs, scale)

        def local_attention(q, k, v):
            b, h, n, d = q.shape
            w = WINDOW
            nw = n // w
            bq = q.reshape(b, h, nw, w, d)
            bk = k.reshape(b, h, nw, w, d)
            bv = v.reshape(b, h, nw, w, d)

            def look(t):
                p = jnp.pad(t, ((0, 0), (0, 0), (1, 0), (0, 0), (0, 0)))
                return jnp.concatenate([p[:, :, :nw], p[:, :, 1:]], axis=3)
            bk2, bv2 = (look(bk), look(bv))
            seq = jnp.arange(n).reshape(nw, w)
            seq_p = jnp.pad(seq, ((1, 0), (0, 0)), constant_values=-1)
            jt = jnp.concatenate([seq_p[:nw], seq_p[1:]], axis=1)
            it = seq[:, :, None]
            jb = jt[:, None, :]
            mask = (it < jb) | (it > jb + w) | (jb == -1)
            sim = jnp.einsum('bhwie,bhwje->bhwij', bq, bk2) * QK_SCALE
            sim = jnp.where(mask, -jnp.finfo(sim.dtype).max, sim)
            attn = jax.nn.softmax(sim, -1)
            out = jnp.einsum('bhwij,bhwje->bhwie', attn, bv2)
            return out.reshape(b, h, n, d)

        def attn_layer(x, Wqkv, qs, ksc, Wo):
            b, n, _ = x.shape
            qkv = x @ Wqkv
            q, k, v = jnp.split(qkv, 3, -1)
            sh = lambda t: t.reshape(b, n, HEADS, DIM_HEAD).transpose(0, 2, 1, 3)
            q, k, v = (sh(q), sh(k), sh(v))
            q = l2norm(q) * qs
            k = l2norm(k) * ksc
            freqs, scale = rotary_tables(n)
            cos, sin = (jnp.cos(freqs), jnp.sin(freqs))
            q = q * cos * scale + rotate_half(q) * sin * scale
            inv = 1.0 / scale
            k = k * cos * inv + rotate_half(k) * sin * inv
            out = local_attention(q, k, v)
            out = out.transpose(0, 2, 1, 3).reshape(b, n, INNER)
            return out @ Wo

        def ffn_layer(x, g, bln, W1, b1, W2, b2):
            mu = x.mean(-1, keepdims=True)
            var = ((x - mu) ** 2).mean(-1, keepdims=True)
            xn = (x - mu) / jnp.sqrt(var + 1e-05) * g + bln
            hg = xn @ W1 + b1
            a, gate = jnp.split(hg, 2, -1)
            return a * jax.nn.gelu(gate, approximate=False) @ W2 + b2
        key = jax.random.key(seed)
        ks = jax.random.split(key, 8)
        B, N = (2, 256)
        init = lambda k, shape: jax.random.normal(k, shape, jnp.float32) * 0.02
        return {'x': jax.random.normal(ks[0], (B, N, DIM), jnp.float32), 'Wqkv': init(ks[1], (DEPTH, DIM, 3 * INNER)), 'q_scale': jnp.ones((DEPTH, DIM_HEAD), jnp.float32), 'k_scale': jnp.ones((DEPTH, DIM_HEAD), jnp.float32), 'Wo': init(ks[2], (DEPTH, INNER, DIM)), 'ln_g': jnp.ones((DEPTH, DIM), jnp.float32), 'ln_b': jnp.zeros((DEPTH, DIM), jnp.float32), 'W1': init(ks[3], (DEPTH, DIM, 2 * DIM_INNER)), 'b1': jnp.zeros((DEPTH, 2 * DIM_INNER), jnp.float32), 'W2': init(ks[4], (DEPTH, DIM_INNER, DIM)), 'b2': jnp.zeros((DEPTH, DIM), jnp.float32)}
    _L0_ffn_all = _L0_ffn_setup()
    _L0_ffn_in = {k: v for k, v in _L0_ffn_all.items() if k in ('Wqkv', 'q_scale', 'k_scale', 'Wo', 'ln_g', 'ln_b', 'W1', 'b1', 'W2', 'b2')}
    del _L0_ffn_all
    return {'x': x, 'ctx_1024': ctx_1024, 'L0_xattn_igate_kernel': _L0_xattn_in['igate_kernel'], 'L0_xattn_igate_bias': _L0_xattn_in['igate_bias'], 'L0_xattn_fgate_kernel': _L0_xattn_in['fgate_kernel'], 'L0_xattn_fgate_bias': _L0_xattn_in['fgate_bias'], 'L0_xattn_outnorm_scale': _L0_xattn_in['outnorm_scale'], 'L0_ffn_Wqkv': _L0_ffn_in['Wqkv'], 'L0_ffn_q_scale': _L0_ffn_in['q_scale'], 'L0_ffn_k_scale': _L0_ffn_in['k_scale'], 'L0_ffn_Wo': _L0_ffn_in['Wo'], 'L0_ffn_ln_g': _L0_ffn_in['ln_g'], 'L0_ffn_ln_b': _L0_ffn_in['ln_b'], 'L0_ffn_W1': _L0_ffn_in['W1'], 'L0_ffn_b1': _L0_ffn_in['b1'], 'L0_ffn_W2': _L0_ffn_in['W2'], 'L0_ffn_b2': _L0_ffn_in['b2']}

def reference(x, ctx_1024, L0_xattn_igate_kernel, L0_xattn_igate_bias, L0_xattn_fgate_kernel, L0_xattn_fgate_bias, L0_xattn_outnorm_scale, L0_ffn_Wqkv, L0_ffn_q_scale, L0_ffn_k_scale, L0_ffn_Wo, L0_ffn_ln_g, L0_ffn_ln_b, L0_ffn_W1, L0_ffn_b1, L0_ffn_W2, L0_ffn_b2):
    import jax
    import jax.numpy as jnp

    def _L0_xattn_ref(q, k, v, igate_kernel, igate_bias, fgate_kernel, fgate_bias, outnorm_scale):
        import jax, jax.numpy as jnp
        import numpy as np
        B, S, H, NH = (2, 256, 128, 4)
        DH = H // NH
        EPS = 1e-06

        def _parallel_stabilized(qh, kh, vh, ig, fg):
            log_fg = jax.nn.log_sigmoid(fg)
            cs = jnp.cumsum(log_fg, axis=2)
            ltr = jnp.tril(jnp.ones((qh.shape[2], qh.shape[2]), dtype=bool))
            log_fg_mat = jnp.where(ltr, cs - jnp.swapaxes(cs, 2, 3), -jnp.inf)
            log_D = log_fg_mat + jnp.swapaxes(ig, 2, 3)
            max_log_D = jnp.max(log_D, axis=-1, keepdims=True)
            D = jnp.exp(log_D - max_log_D)
            qk = jnp.einsum('bhsd,bhtd->bhst', qh, kh) / jnp.sqrt(jnp.float32(DH))
            C = qk * D
            normalizer = jnp.maximum(jnp.abs(jnp.sum(C, axis=-1, keepdims=True)), jnp.exp(-max_log_D))
            return jnp.einsum('bhst,bhtd->bhsd', C / (normalizer + EPS), vh)
        Bq, Sq, Hq = q.shape
        x = jnp.concatenate([q, k, v], axis=-1)
        ig = x @ igate_kernel + igate_bias
        fg = x @ fgate_kernel + fgate_bias
        ig = jnp.transpose(ig, (0, 2, 1))[..., None]
        fg = jnp.transpose(fg, (0, 2, 1))[..., None]
        qh = jnp.transpose(q.reshape(Bq, Sq, NH, DH), (0, 2, 1, 3))
        kh = jnp.transpose(k.reshape(Bq, Sq, NH, DH), (0, 2, 1, 3))
        vh = jnp.transpose(v.reshape(Bq, Sq, NH, DH), (0, 2, 1, 3))
        h = _parallel_stabilized(qh, kh, vh, ig, fg)
        mean = jnp.mean(h, axis=-1, keepdims=True)
        var = jnp.mean((h - mean) ** 2, axis=-1, keepdims=True)
        h_norm = (h - mean) * jax.lax.rsqrt(var + 1e-05)
        h_norm = h_norm * outnorm_scale.reshape(1, NH, 1, DH)
        out = jnp.transpose(h_norm, (0, 2, 1, 3)).reshape(Bq, Sq, Hq)
        return out

    def _L0_ffn_ref(x, Wqkv, q_scale, k_scale, Wo, ln_g, ln_b, W1, b1, W2, b2):
        import jax, jax.numpy as jnp
        import numpy as np
        DIM = 128
        DEPTH = 6
        HEADS = 16
        DIM_HEAD = 64
        WINDOW = 32
        INNER = HEADS * DIM_HEAD
        DIM_INNER = int(DIM * 4 * 2 / 3)
        QK_SCALE = 8.0

        def shift_tokens(t):
            a, s = jnp.split(t, 2, -1)
            s = jnp.pad(s, ((0, 0), (1, 0), (0, 0)))[:, :-1]
            return jnp.concatenate([a, s], -1)

        def l2norm(t):
            return t / jnp.maximum(jnp.linalg.norm(t, axis=-1, keepdims=True), 1e-12)

        def rotate_half(x):
            x1, x2 = jnp.split(x, 2, -1)
            return jnp.concatenate([-x2, x1], -1)

        def rotary_tables(n):
            half = jnp.arange(0, DIM_HEAD, 2, dtype=jnp.float32)
            inv_freq = 1.0 / 10000.0 ** (half / DIM_HEAD)
            t = jnp.arange(n, dtype=jnp.float32)
            freqs = t[:, None] * inv_freq[None, :]
            freqs = jnp.concatenate([freqs, freqs], -1)
            base_scale = (half + 0.4 * DIM_HEAD) / (1.4 * DIM_HEAD)
            power = (t - n // 2) / (WINDOW // 2)
            scale = base_scale[None, :] ** power[:, None]
            scale = jnp.concatenate([scale, scale], -1)
            return (freqs, scale)

        def local_attention(q, k, v):
            b, h, n, d = q.shape
            w = WINDOW
            nw = n // w
            bq = q.reshape(b, h, nw, w, d)
            bk = k.reshape(b, h, nw, w, d)
            bv = v.reshape(b, h, nw, w, d)

            def look(t):
                p = jnp.pad(t, ((0, 0), (0, 0), (1, 0), (0, 0), (0, 0)))
                return jnp.concatenate([p[:, :, :nw], p[:, :, 1:]], axis=3)
            bk2, bv2 = (look(bk), look(bv))
            seq = jnp.arange(n).reshape(nw, w)
            seq_p = jnp.pad(seq, ((1, 0), (0, 0)), constant_values=-1)
            jt = jnp.concatenate([seq_p[:nw], seq_p[1:]], axis=1)
            it = seq[:, :, None]
            jb = jt[:, None, :]
            mask = (it < jb) | (it > jb + w) | (jb == -1)
            sim = jnp.einsum('bhwie,bhwje->bhwij', bq, bk2) * QK_SCALE
            sim = jnp.where(mask, -jnp.finfo(sim.dtype).max, sim)
            attn = jax.nn.softmax(sim, -1)
            out = jnp.einsum('bhwij,bhwje->bhwie', attn, bv2)
            return out.reshape(b, h, n, d)

        def attn_layer(x, Wqkv, qs, ksc, Wo):
            b, n, _ = x.shape
            qkv = x @ Wqkv
            q, k, v = jnp.split(qkv, 3, -1)
            sh = lambda t: t.reshape(b, n, HEADS, DIM_HEAD).transpose(0, 2, 1, 3)
            q, k, v = (sh(q), sh(k), sh(v))
            q = l2norm(q) * qs
            k = l2norm(k) * ksc
            freqs, scale = rotary_tables(n)
            cos, sin = (jnp.cos(freqs), jnp.sin(freqs))
            q = q * cos * scale + rotate_half(q) * sin * scale
            inv = 1.0 / scale
            k = k * cos * inv + rotate_half(k) * sin * inv
            out = local_attention(q, k, v)
            out = out.transpose(0, 2, 1, 3).reshape(b, n, INNER)
            return out @ Wo

        def ffn_layer(x, g, bln, W1, b1, W2, b2):
            mu = x.mean(-1, keepdims=True)
            var = ((x - mu) ** 2).mean(-1, keepdims=True)
            xn = (x - mu) / jnp.sqrt(var + 1e-05) * g + bln
            hg = xn @ W1 + b1
            a, gate = jnp.split(hg, 2, -1)
            return a * jax.nn.gelu(gate, approximate=False) @ W2 + b2
        for i in range(DEPTH):
            x = attn_layer(shift_tokens(x), Wqkv[i], q_scale[i], k_scale[i], Wo[i]) + x
            x = ffn_layer(shift_tokens(x), ln_g[i], ln_b[i], W1[i], b1[i], W2[i], b2[i]) + x
        return x
    x = x + _L0_xattn_ref(_layernorm(x, axis=-1), ctx_1024, ctx_1024, L0_xattn_igate_kernel, L0_xattn_igate_bias, L0_xattn_fgate_kernel, L0_xattn_fgate_bias, L0_xattn_outnorm_scale)
    x = x + _L0_ffn_ref(_layernorm(x, axis=-1), L0_ffn_Wqkv, L0_ffn_q_scale, L0_ffn_k_scale, L0_ffn_Wo, L0_ffn_ln_g, L0_ffn_ln_b, L0_ffn_W1, L0_ffn_b1, L0_ffn_W2, L0_ffn_b2)
    return x

_drawn_inputs = setup_inputs


def setup_inputs(seed=0):
    import zlib

    import numpy as np

    out = dict(_drawn_inputs(seed))
    spreads = {'L0_xattn_outnorm_scale': (1.0, 0.2),
     'L0_ffn_q_scale': (1.0, 0.6),
     'L0_ffn_k_scale': (1.0, 0.6),
     'L0_ffn_ln_g': (1.0, 0.6),
     'L0_ffn_ln_b': (0.0, 0.8),
     'L0_ffn_b1': (0.0, 0.8),
     'L0_ffn_b2': (0.0, 0.1)}
    factors = {'L0_xattn_igate_bias': 8.0,
     'L0_xattn_fgate_kernel': 5.234,
     'L0_ffn_W1': 4.903,
     'L0_ffn_W2': 4.826}
    for name, (base, spread) in spreads.items():
        noise = np.random.default_rng([zlib.crc32(name.encode()), seed]).standard_normal(out[name].shape)
        drawn = base * np.exp(spread * noise) if base else spread * noise
        out[name] = jnp.asarray(drawn.astype(out[name].dtype))
    for name, factor in factors.items():
        out[name] = (out[name] * factor).astype(out[name].dtype)
    return out
```

```python
from contextlib import ExitStack

import numpy as np

import concourse.bass as bass
from concourse import mybir

F32 = mybir.dt.float32
F32R = mybir.dt.float32r
BF16 = mybir.dt.bfloat16
I32 = mybir.dt.int32
ALU = mybir.AluOpType
ACT = mybir.ActivationFunctionType
AX_X = mybir.AxisListType.X

NSEQ, S, D = 64, 64, 128
NPAIR = NSEQ // 2
TOK = 2 * S
NTOK = NSEQ * S
NTILE = NPAIR
NQUAD = NTILE // 2
DEPTH, HEADS, DH = 6, 16, 64
INNER = HEADS * DH
XH = 4
XD = D // XH
FF = 341
FCH = [128, 128, FF - 256]
WINDOW = 32
NVEC = 9
MASKED = -1.0e30
MAGIC = float(0x5F3759DF)
WCOL = [0, INNER, 512, INNER + 512, 2 * INNER, 2 * INNER + 512]
UNITS = 8
GSTEPS, SSTEPS, MSTEPS = 12, 14, 32
SCANS = UNITS * GSTEPS
MIXING = SCANS + SSTEPS


def constants():
    half = np.arange(0, DH, 2, dtype=np.float64)
    inv_freq = 1.0 / 10000.0 ** (half / DH)
    t = np.arange(S, dtype=np.float64)
    freqs = np.concatenate([t[:, None] * inv_freq[None]] * 2, -1)
    base = (half + 0.4 * DH) / (1.4 * DH)
    scale = np.concatenate([base[None] ** ((t - S // 2) / (WINDOW // 2))[:, None]] * 2, -1)
    sign = np.where(np.arange(DH) < DH // 2, -1.0, 1.0)[None]
    rot = np.stack([8 * np.cos(freqs) * scale, 8 * sign * np.sin(freqs) * scale,
                    np.cos(freqs) / scale, sign * np.sin(freqs) / scale], 1)
    rot = np.tile(rot, (2, 1, 1)).astype(np.float32).reshape(TOK, 4 * DH)
    i, j = np.arange(S)[:, None], np.arange(S)[None]
    band = np.where((j <= i) & (j >= i - WINDOW), 0.0, MASKED).astype(np.float32)
    band = np.tile(band, (2, 8))
    causal = np.tile(np.where(i <= j, 0.0, MASKED).astype(np.float32), (2, 1))
    return rot, band, causal


def transformer_program(nc, x, ctx_in, wgate, bgate, outnorm, wqkv, qscale, kscale, wo, w1, w2, vec,
                        rot_c, band_c, causal_c, out):
    with ExitStack() as stack:
        def sb(name, shape, dt=F32):
            return stack.enter_context(nc.sbuf_tensor(name, shape, dt))

        def bank(name):
            return stack.enter_context(nc.psum_tensor(name, [128, 512], F32))

        def sem(name):
            return stack.enter_context(nc.semaphore(name))

        QKV = [bank("qkv0"), bank("qkv1")]
        TP = [bank("tp0"), bank("tp1")]
        SC = [bank("sc0"), bank("sc1")]
        OT = [bank("ot0"), bank("ot1")]

        SCX = [SC[0], SC[1], QKV[0], QKV[1]]

        xtok = sb("xtok", [128, NTOK])
        xT = sb("xT", [128, NTOK])
        ident = sb("ident", [128, 128])
        identb = sb("identb", [128, 128], BF16)
        cst = sb("cst", [128, 4])
        rot_base = sb("rot_base", [128, 4 * DH])
        scales = sb("scales", [128, DEPTH, 4, DH])
        tabs = sb("tabs", [128, 4 * DH])
        band_f = sb("band_f", [128, 512])
        band = sb("band", [128, 512], BF16)
        ones = sb("ones", [128, 128])
        vecs_all = sb("vecs_all", [128, DEPTH * NVEC])
        vecs = sb("vecs", [128, NVEC])
        w_raw = sb("w_raw", [128, 3 * INNER])
        w_hi = sb("w_hi", [128, 3 * INNER], F32R)
        w_lo = sb("w_lo", [128, 3 * INNER], F32R)
        wo_s = sb("wo_s", [128, 8, 128])
        w1_s = sb("w1_s", [128, 2 * FF])
        w2_s = sb("w2_s", [128, 3, 128])
        arena = sb("arena", [128, 4 * 2048])
        raw = arena[:, 0:2048].rearrange("p (c n) -> p c n", c=4)
        qn = arena[:, 2048:4096].rearrange("p (c n) -> p c n", c=4)
        tr = arena[:, 4096:6144].rearrange("p (c n) -> p c n", c=4)
        ur = arena[:, 6144:8192].rearrange("p (c n) -> p c n", c=4)
        xs_hi = sb("xs_hi", [128, 256], F32R)
        xs_lo = sb("xs_lo", [128, 256], F32R)
        sq = sb("sq", [128, 2, 512])
        ss = sb("ss", [128, 32])
        seed = sb("seed", [128, 32], I32)
        nwt = sb("nwt", [128, 3, 32])
        rinv = sb("rinv", [128, 32])
        qT = sb("qT", [128, 2, 4, 128])
        kT = sb("kT", [128, 2, 4, 128])
        vt = sb("vt", [128, 2, INNER])
        es = sb("es", [128, 2, 512])
        smax = sb("smax", [128, 2, 8])
        ssum = sb("ssum", [128, 2, 8])
        sinv = sb("sinv", [128, 2, 8])
        pT = sb("pT", [128, 2, 4, 128])
        oT = sb("oT", [128, 8, 128])
        fx = sb("fx", [128, 256])
        fc = sb("fc", [128, 256])
        fsq = sb("fsq", [128, 256])
        fln = sb("fln", [128, 256])
        frs = sb("frs", [128, 256])
        fxn = sb("fxn", [128, 256])
        fh = sb("fh", [128, 3, 256])
        ctok = arena[:, 0:4096]
        xlT = arena[:, 4096:8192]
        wg = sb("wg", [128, 3, 8])
        wg_kv = sb("wg_kv", [128, 8])
        bg = sb("bg", [128, 8])
        onorm = sb("onorm", [128, D])
        causal = sb("causal", [128, S])
        gtok = sb("gtok", [128, NPAIR, 8])
        gpk = sb("gpk", [128, 8, 128])
        gro = sb("gro", [128, 8, 128])
        a_tok = sb("a_tok", [128, 128])
        em_tok = sb("em_tok", [128, 128])
        st_x = sb("st_x", [128, 512])
        st_c = sb("st_c", [128, 512])
        st_v = sb("st_v", [128, 16, 33])
        st_sel = sb("st_sel", [128, 16])
        st_em = sb("st_em", [128, 16])
        st_a = sb("st_a", [128, 16])
        st_xT = sb("st_xT", [128, 512])
        st_cT = sb("st_cT", [128, 512])
        gexp = sb("gexp", [128, 1024])
        hmix = sb("hmix", [128, 512])
        psq = sb("psq", [128, 512])
        psm = sb("psm", [128, 12, 16])

        ld_x, ld_ctx, ld_small = sem("ld_x"), sem("ld_ctx"), sem("ld_small")
        ld_wqkv, ld_wo, ld_ffn = sem("ld_wqkv"), sem("ld_wo"), sem("ld_ffn")
        stored = sem("stored")
        const_made, const_init = sem("const_made"), sem("const_init")
        small_ready = sem("small_ready")
        chain, mixed = sem("chain_step"), sem("mixed")
        qkv_mm, t_mm, s_mm, pt_mm, pv_mm, wo_mm = map(sem, ("qkv_mm", "t_mm", "s_mm", "pt_mm", "pv_mm", "wo_mm"))
        mean_mm, var_mm, w1_mm, w2_mm = map(sem, ("mean_mm", "var_mm", "w1_mm", "w2_mm"))
        qk_sq, qkv_evac, qkt_evac, e_exp, pt_evac, ot_evac = map(
            sem, ("qk_sq", "qkv_evac", "qkt_evac", "e_exp", "pt_evac", "ot_evac"))
        fsq_done, fln_done, frs_done, gelu_done, whi_done = map(
            sem, ("fsq_done", "fln_done", "frs_done", "gelu_done", "whi_done"))
        ss_red, newton, qn_ready, u_ready, s_max, s_sub, e_sum, e_inv = map(
            sem, ("ss_red", "newton", "qn_ready", "u_ready", "s_max", "s_sub", "e_sum", "e_inv"))
        resid, xs_half, xs_ready, fx_ready, fc_ready, fn_step, fxn_ready, h_ready, ffn_done = map(
            sem, ("resid", "xs_half", "xs_ready", "fx_ready", "fc_ready", "fn_step", "fxn_ready", "h_ready", "ffn_done"))
        wlo_done, tabs_ready, vec_ready = sem("wlo_done"), sem("tabs_ready"), sem("vec_ready")
        t_done, rot_ready, pn_ready = sem("t_done"), sem("rot_ready"), sem("pn_ready")
        end_mm, end_add = sem("end_mm"), sem("end_add")

        ST = [psm[:, k, :] for k in range(12)]
        HALVES = (slice(0, 64), slice(64, 128))

        def bc(ap, n):
            return ap.unsqueeze(2).broadcast_to([ap.shape[0], ap.shape[1], n])

        def mid(ap, n):
            return ap.unsqueeze(1).broadcast_to([ap.shape[0], n, ap.shape[1]])

        def g3(ap, n):
            return ap.rearrange("p (a n) -> p a n", n=n)

        block = stack.enter_context(nc.Block())

        @block.sync
        def _(sp):
            xv = x.rearrange("(p t) d -> t p d", t=TOK)
            cv = ctx_in.rearrange("(p t) d -> t p d", t=TOK)
            for k in range(2):
                sl = slice(k * 2048, (k + 1) * 2048)
                sp.dma_start(g3(xtok[:, sl], D), xv[:, k * 16:(k + 1) * 16, :]).then_inc(ld_x, 16)
                sp.dma_start(g3(ctok[:, sl], D), cv[:, k * 16:(k + 1) * 16, :]).then_inc(ld_ctx, 16)
            sp.dma_start(wg[:], wgate.rearrange("(k p) g -> p k g", p=128)).then_inc(ld_small, 16)
            sp.dma_start(bg[:], bgate.partition_broadcast(128)).then_inc(ld_small, 16)
            sp.dma_start(onorm[:], outnorm.partition_broadcast(128)).then_inc(ld_small, 16)
            sp.dma_start(causal[:], causal_c).then_inc(ld_small, 16)
            sp.dma_start(rot_base[:], rot_c).then_inc(ld_small, 16)
            sp.dma_start(band_f[:], band_c).then_inc(ld_small, 16)
            sp.dma_start(vecs_all[:], vec).then_inc(ld_small, 16)
            for k, src in enumerate((qscale, kscale)):
                rep = src.partition_broadcast(128)
                sp.dma_start(scales[:, :, 2 * k, :], rep).then_inc(ld_small, 16)
                sp.dma_start(scales[:, :, 2 * k + 1, 0:32], rep[:, :, 32:64]).then_inc(ld_small, 16)
                sp.dma_start(scales[:, :, 2 * k + 1, 32:64], rep[:, :, 0:32]).then_inc(ld_small, 16)
            sp.dma_start(w_raw[:], wqkv[0]).then_inc(ld_wqkv, 16)
            sp.dma_start(wo_s[:], wo[0]).then_inc(ld_wo, 16)
            sp.dma_start(w1_s[:], w1[0]).then_inc(ld_ffn, 16)
            sp.dma_start(w2_s[:], w2[0]).then_inc(ld_ffn, 16)
            with sp.Fori(0, DEPTH - 1) as L:
                sp.wait_ge(whi_done, 6 * L + 6)
                sp.wait_ge(wlo_done, 6 * L + 6)
                sp.dma_start(w_raw[:], wqkv[bass.ds(L + 1, 1)].rearrange("o p n -> (o p) n")).then_inc(ld_wqkv, 16)
                sp.wait_ge(wo_mm, NTILE * L + NTILE)
                sp.dma_start(wo_s[:], wo[bass.ds(L + 1, 1)].rearrange("o p k n -> (o p) k n")).then_inc(ld_wo, 16)
                sp.wait_ge(w2_mm, NQUAD * L + NQUAD)
                sp.dma_start(w1_s[:], w1[bass.ds(L + 1, 1)].rearrange("o p n -> (o p) n")).then_inc(ld_ffn, 16)
                sp.dma_start(w2_s[:], w2[bass.ds(L + 1, 1)].rearrange("o p k n -> (o p) k n")).then_inc(ld_ffn, 16)
            ov = out.rearrange("(p t) d -> t p d", t=TOK)
            for k in range(UNITS):
                sp.wait_ge(end_add, k + 1)
                sp.dma_start(ov[:, 4 * k:4 * k + 4, :], g3(xtok[:, k * 512:(k + 1) * 512], D)).then_inc(stored, 16)
            sp.wait_ge(stored, 16 * UNITS)

        @block.gpsimd
        def _(pool):
            gps = nc.gpsimd
            gps.memset(ident[:], 0.0).then_inc(const_init, 1)
            gps.memset(ones[:], 1.0 / D).then_inc(const_made, 1)
            gps.memset(cst[:, 0:1], 1e-5).then_inc(const_made, 1)
            gps.memset(cst[:, 1:2], 1.0).then_inc(const_made, 1)
            gps.memset(st_v[:], 1.0).then_inc(const_made, 1)
            pool.wait_ge(const_init, 1)
            gps.affine_select(out=ident[:], in_=ident[:], compare_op=ALU.not_equal, fill=1.0, base=0,
                              pattern=[[-1, 128]], channel_multiplier=1).then_inc(const_made, 1)

            def rotate(n, i, first=False):
                tab = tabs[:, (i % 2) * 2 * DH:(i % 2) * 2 * DH + DH]
                pool.wait_ge(qn_ready, 4 * n + i + 1)
                if not first:
                    pool.wait_ge(t_mm, 4 * n + i - 3)
                gps.tensor_tensor(g3(tr[:, i, :], DH), g3(qn[:, i, :], DH), mid(tab, 8), ALU.mult).then_inc(t_done, 1)
                pool.wait_ge(t_done, 4 * n + i + 1)
                pool.wait_ge(u_ready, 4 * n + i + 1)
                gps.tensor_tensor(tr[:, i, :], tr[:, i, :], ur[:, i, :], ALU.add).then_inc(rot_ready, 1)

            def normalise(m, g):
                pool.wait_ge(e_inv, 2 * m + g + 1)
                gps.tensor_tensor(g3(es[:, g, :], S), g3(es[:, g, :], S), bc(sinv[:, g, :], S),
                                  ALU.mult).then_inc(pn_ready, 1)

            def step(n, a=True, b=True, first=False):
                if b:
                    normalise(n - 1, 0)
                if a:
                    rotate(n, 0, first)
                if b:
                    normalise(n - 1, 1)
                if a:
                    for i in range(1, 4):
                        rotate(n, i, first)

            step(0, b=False, first=True)
            step(1)
            with pool.Fori(0, DEPTH - 1) as L:
                with pool.Fori(1, NQUAD) as q:
                    n = NTILE * L + 2 * q
                    step(n)
                    step(n + 1)
                n = NTILE * L + NTILE
                step(n)
                step(n + 1)
            with pool.Fori(1, NQUAD) as q:
                n = NTILE * (DEPTH - 1) + 2 * q
                step(n)
                step(n + 1)
            step(DEPTH * NTILE, a=False)

        @block.tensor
        def _(pe):
            mm = nc.tensor.matmul

            def carry_wait(col=0):
                mm(OT[0][:, col:col + 1], identb[:], identb[:, 0:1], start=True, stop=True)

            pe.wait_ge(const_made, 6)
            pe.wait_ge(small_ready, 1)
            with pe.Fori(0, UNITS) as u:
                pe.wait_ge(chain, GSTEPS * u + 8)
                for bk, src in zip(TP, (st_x, st_c)):
                    for k in range(4):
                        last = nc.tensor.transpose(bk[:, k * 128:(k + 1) * 128], src[:, k * 128:(k + 1) * 128], ident[:])
                last.then_inc(chain, 1)
                pe.wait_ge(chain, GSTEPS * u + 10)
                for k in range(4):
                    mm(SC[0][:, 8 * k:8 * k + 8], st_xT[:, k * 128:(k + 1) * 128], wg[:, 0, :], start=True, stop=False)
                    last = mm(SC[0][:, 8 * k:8 * k + 8], st_cT[:, k * 128:(k + 1) * 128], wg_kv[:], start=False, stop=True)
                last.then_inc(chain, 1)
            pe.wait_ge(chain, SCANS + 6)
            nc.tensor.transpose(TP[0][:, 0:128], gpk[:, 3, :], ident[:])
            nc.tensor.transpose(TP[0][:, 128:256], gpk[:, 0, :], ident[:]).then_inc(chain, 1)
            pe.wait_ge(chain, SCANS + 12)
            nc.tensor.transpose(TP[1][:, 0:128], gro[:, 3, :], ident[:])
            nc.tensor.transpose(TP[1][:, 128:256], gro[:, 6, :], ident[:]).then_inc(chain, 1)

            with pe.Fori(0, UNITS) as u:
                pe.wait_ge(chain, MSTEPS * u + (MIXING + 1))
                for k in range(4):
                    for h in range(XH):
                        for b in range(2):
                            c = k * XH + h
                            o = (k % 2) * 256 + h * 64
                            mm(TP[k // 2][HALVES[b], o:o + 64], st_sel[:, c:c + 1].broadcast_to([128, 64]),
                               gro[:, 5, 64 * b:64 * b + 64], start=True, stop=True)
                for k in range(4):
                    for b in range(2):
                        for h in range(XH):
                            c = k * 128 + 64 * b
                            last = mm(SCX[h][HALVES[b], k * 64:k * 64 + 64], st_cT[32 * h:32 * h + 32, c:c + 64],
                                      st_xT[32 * h:32 * h + 32, c:c + 64], start=True, stop=True,
                                      tile_position=(32 * h, 64 * b))
                last.then_inc(chain, 1)
                pe.wait_ge(chain, MSTEPS * u + (MIXING + 6))
                carry_wait()
                for k in range(4):
                    for h in range(XH):
                        for b in range(2):
                            c = k * XH + h
                            o = (k % 2) * 132 + h * 33
                            last = mm(OT[k // 2][HALVES[b], o:o + 33], gexp[HALVES[b], c * 64:(c + 1) * 64],
                                      st_v[HALVES[b], c, :], start=True, stop=True)
                last.then_inc(chain, 1)
                pe.wait_ge(chain, MSTEPS * u + (MIXING + 30))
                for k in range(4):
                    last = nc.tensor.transpose(QKV[0][:, k * 128:(k + 1) * 128], st_x[:, k * 128:(k + 1) * 128], ident[:])
                last.then_inc(chain, 1)

            def project(n, par, i, first=False, layer=None):
                if layer is not None:
                    pe.wait_ge(whi_done, 6 * layer + i + 1)
                    pe.wait_ge(wlo_done, 6 * layer + i + 1)
                if not first or i >= 2:
                    pe.wait_ge(qkv_evac, 6 * n + i - 1)
                bk = QKV[i % 2]
                xh, xl = (t[:, par * 128:(par + 1) * 128] for t in (xs_hi, xs_lo))
                wh, wl = (t[:, WCOL[i]:WCOL[i] + 512] for t in (w_hi, w_lo))
                mm(bk[:], xh, wh, start=True, stop=False)
                mm(bk[:], xh, wl, start=False, stop=False)
                mm(bk[:], xl, wh, start=False, stop=True).then_inc(qkv_mm, 1)

            def transposes(m, i, first):
                if not first and i == 0:
                    pe.wait_ge(pt_evac, 2 * m)
                if i >= 2:
                    pe.wait_ge(qkt_evac, 4 * m + i - 1)
                pe.wait_ge(rot_ready, 4 * m + i + 1)
                for k in range(4):
                    last = nc.tensor.transpose(TP[i % 2][:, k * 128:(k + 1) * 128], tr[:, i, k * 128:(k + 1) * 128], ident[:])
                last.then_inc(t_mm, 1)

            def scores(m, g, first, ffn_before=None):
                if not first:
                    pe.wait_ge(s_sub, 2 * m + g - 1)
                if ffn_before is not None:
                    pe.wait_ge(ffn_done, ffn_before)
                pe.wait_ge(qkt_evac, 4 * m + 2 * g + 2)
                mm(SC[g][:], identb[:], band[:], start=True, stop=True)
                for k in range(4):
                    for s in range(2):
                        for h in range(2):
                            sl, c = HALVES[h], k * 128 + s * 64
                            last = mm(SC[g][sl, c:c + 64], qT[sl, g, k, s * 64:s * 64 + 64],
                                      kT[sl, g, k, s * 64:s * 64 + 64], start=False, stop=True,
                                      skip_group_check=True)
                last.then_inc(s_mm, 1)

            def prob_transposes(m, g, ffn=None):
                if g == 1 and ffn is not None:
                    pe.wait_ge(h_ready, 3 * ffn + 2)
                pe.wait_ge(pn_ready, 2 * m + g + 1)
                for k in range(4):
                    last = nc.tensor.transpose(TP[1 - g][:, k * 128:(k + 1) * 128], es[:, g, k * 128:(k + 1) * 128], ident[:])
                last.then_inc(pt_mm, 1)

            def values(m, g, par, first, ffn=None):
                if g == 0:
                    if not first:
                        pe.wait_ge(resid, m)
                    if ffn is not None:
                        pe.wait_ge(h_ready, 3 * ffn + 3)
                    pe.wait_ge(qkv_evac, 6 * m + 6)
                pe.wait_ge(pt_evac, 2 * m + g + 1)
                if g == 0:
                    carry_wait()
                else:
                    carry_wait(256)
                for k in range(4):
                    for h in range(2):
                        for s in range(2):
                            hd = 8 * g + 2 * k + h
                            last = mm(OT[s][HALVES[h], (4 * g + k) * 64:(4 * g + k) * 64 + 64],
                                      vt[HALVES[s], par, hd * DH:(hd + 1) * DH],
                                      pT[HALVES[s], g, k, h * 64:h * 64 + 64], start=True, stop=True)
                last.then_inc(pv_mm, 1)

            def out_product(w, L):
                pe.wait_ge(ld_wo, 16 * L + 16)
                pe.wait_ge(ot_evac, w + 1)
                for k in range(8):
                    last = mm(OT[0][:, 0:128], wo_s[:, k, :], oT[:, k, :], start=(k == 0), stop=(k == 7))
                last.then_inc(wo_mm, 1)

            def ffn_mean(f):
                pe.wait_ge(fx_ready, f + 1)
                mm(OT[1][:, 0:256], ones[:], fx[:], start=True, stop=True).then_inc(mean_mm, 1)

            def ffn_var(f):
                pe.wait_ge(fsq_done, f + 1)
                mm(OT[1][:, 256:512], ones[:], fsq[:], start=True, stop=True).then_inc(var_mm, 1)

            def ffn_up(f, L):
                pe.wait_ge(ld_ffn, 32 * L + 32)
                pe.wait_ge(fxn_ready, f + 1)
                for bk, parts in ((OT[0], ((1, 0), (1, 1))), (OT[1], ((1, 2), (0, 2))), (TP[0], ((0, 0), (0, 1)))):
                    for k, (gate, c) in enumerate(parts):
                        o = gate * FF + c * 128
                        last = mm(bk[0:FCH[c], k * 256:(k + 1) * 256], w1_s[:, o:o + FCH[c]], fxn[:], start=True, stop=True)
                    last.then_inc(w1_mm, 1)

            def ffn_down(f, m):
                pe.wait_ge(s_sub, 2 * m + 1)
                pe.wait_ge(h_ready, 3 * f + 3)
                for c in range(3):
                    last = mm(SC[0][:, 0:256], w2_s[0:FCH[c], c, :], fh[0:FCH[c], c, :], start=(c == 0), stop=(c == 2))
                last.then_inc(w2_mm, 1)

            def step(n, par, L, a=True, b=True, w=True, f=None, first=False, b_first=False, ffn_before=None, quad=None,
                     layer=None):
                m = n - 1
                if a:
                    if quad is not None:
                        pe.wait_ge(xs_ready, quad + 1)
                    project(n, par, 0, first, layer)
                if w:
                    out_product(n - 2, L)
                if b:
                    transposes(m, 0, b_first)
                    transposes(m, 1, b_first)
                if a:
                    project(n, par, 1, first, layer)
                if b:
                    scores(m, 0, b_first, ffn_before)
                if f is not None:
                    ffn_mean(f)
                if a:
                    project(n, par, 2, first, layer)
                if b:
                    transposes(m, 2, b_first)
                    transposes(m, 3, b_first)
                if a:
                    project(n, par, 3, first, layer)
                if b:
                    scores(m, 1, b_first)
                if f is not None:
                    ffn_var(f)
                if a:
                    project(n, par, 4, first, layer)
                if b:
                    prob_transposes(m, 0)
                if f is not None:
                    ffn_up(f, L)
                if a:
                    project(n, par, 5, first, layer)
                if b:
                    values(m, 0, 1 - par, b_first, f)
                    prob_transposes(m, 1, f)
                    values(m, 1, 1 - par, b_first)
                if f is not None:
                    ffn_down(f, m)

            pe.wait_ge(const_made, 6)
            step(0, 0, 0, b=False, w=False, first=True, quad=0, layer=0)
            step(1, 1, 0, w=False, b_first=True)
            with pe.Fori(0, DEPTH - 1) as L:
                with pe.Fori(1, NQUAD) as q:
                    n, g = NTILE * L + 2 * q, NQUAD * L + q
                    step(n, 0, L, ffn_before=g - 1, quad=g)
                    step(n + 1, 1, L, f=g - 1)
                n, g = NTILE * L + NTILE, NQUAD * L + NQUAD
                step(n, 0, L, ffn_before=g - 1, quad=g, layer=L + 1)
                step(n + 1, 1, L, f=g - 1)
            with pe.Fori(1, NQUAD) as q:
                n, g = NTILE * (DEPTH - 1) + 2 * q, NQUAD * (DEPTH - 1) + q
                step(n, 0, DEPTH - 1, ffn_before=g - 1, quad=g)
                step(n + 1, 1, DEPTH - 1, f=g - 1)
            n, g = DEPTH * NTILE, DEPTH * NQUAD
            step(n, 0, DEPTH - 1, a=False, ffn_before=g - 1)
            out_product(n - 1, DEPTH - 1)
            ffn_mean(g - 1)
            ffn_var(g - 1)
            ffn_up(g - 1, DEPTH - 1)
            ffn_down(g - 1, n - 1)
            for k in range(UNITS):
                pe.wait_ge(ffn_done, g)
                if k >= 2:
                    pe.wait_ge(end_add, k - 1)
                for j in range(4):
                    o = (4 * k + j) * 128
                    last = nc.tensor.transpose(QKV[k % 2][:, j * 128:(j + 1) * 128], xT[:, o:o + 128], ident[:])
                last.then_inc(end_mm, 1)

        @block.scalar
        def _(act):
            fn = nc.scalar.activation
            EPS = cst[:, 0:1]
            ONE = cst[:, 1:2]
            act.wait_ge(const_made, 6)
            act.wait_ge(ld_ctx, 32)

            def ln_act(base, meanwhile=None):
                act.wait_ge(chain, base + 3)
                fn(psq[:], st_x[:], ACT.Square).then_inc(chain, 1)
                if meanwhile is not None:
                    meanwhile()
                act.wait_ge(chain, base + 5)
                fn(ST[2][:, 0:4], ST[2][:, 0:4], ACT.Ln, bias=EPS, scale=1.0 / D).then_inc(chain, 1)
                act.wait_ge(chain, base + 6)
                fn(ST[2][:, 0:4], ST[2][:, 0:4], ACT.Exp, scale=-0.5).then_inc(chain, 1)

            with act.Fori(0, UNITS) as u:
                ln_act(GSTEPS * u, lambda: nc.scalar.copy(st_c[:], ctok[:, bass.ds(u * 512, 512)]))
                act.wait_ge(chain, GSTEPS * u + 9)
                nc.scalar.copy(st_xT[:], TP[0][:])
                nc.scalar.copy(xlT[:, bass.ds(u * 512, 512)], TP[0][:])
                nc.scalar.copy(xT[:, bass.ds(u * 512, 512)], TP[1][:])
                nc.scalar.copy(st_cT[:], TP[1][:]).then_inc(chain, 1)
            act.wait_ge(chain, SCANS + 3)
            fn(gpk[:, 2, :], gpk[:, 2, :], ACT.Exp).then_inc(chain, 1)
            act.wait_ge(chain, SCANS + 4)
            fn(gpk[:, 2, :], gpk[:, 2, :], ACT.Ln, bias=ONE).then_inc(chain, 1)
            act.wait_ge(chain, SCANS + 13)
            nc.scalar.copy(a_tok[:], TP[1][:, 0:128])
            fn(em_tok[:], TP[1][:, 128:256], ACT.Exp).then_inc(chain, 1)

            with act.Fori(0, UNITS) as u:
                base = MSTEPS * u + MIXING
                act.wait_ge(chain, base)
                nc.scalar.copy(ST[7][:, 0:1], ident[:, 0:1])
                nc.scalar.copy(st_xT[:], xlT[:, bass.ds(u * 512, 512)])
                nc.scalar.copy(st_cT[:], xT[:, bass.ds(u * 512, 512)])
                nc.scalar.copy(st_v[:, :, 0:XD], g3(ctok[:, bass.ds(u * 512, 512)], XD))
                nc.scalar.copy(st_a[:], a_tok[:, bass.ds(u * 16, 16)])
                nc.scalar.copy(st_em[:], em_tok[:, bass.ds(u * 16, 16)])
                nc.scalar.copy(st_sel[:], ident[:, bass.ds(u * 16, 16)]).then_inc(chain, 1)
                act.wait_ge(chain, base + 4)
                fn(gexp[:], gexp[:], ACT.Exp).then_inc(chain, 1)
                act.wait_ge(chain, base + 15)
                fn(psq[:], hmix[:], ACT.Square).then_inc(chain, 1)
                act.wait_ge(chain, base + 17)
                fn(ST[5][:], ST[5][:], ACT.Ln, bias=EPS, scale=1.0 / XD).then_inc(chain, 1)
                act.wait_ge(chain, base + 18)
                fn(ST[5][:], ST[5][:], ACT.Exp, scale=-0.5).then_inc(chain, 1)
                ln_act(base + 22)
                act.wait_ge(chain, base + 31)
                nc.scalar.copy(ST[7][:, 0:1], ident[:, 0:1])
                nc.scalar.copy(xT[:, bass.ds(u * 512, 512)], QKV[0][:]).then_inc(chain, 1)

            def split_hi(L, first=False):
                act.wait_ge(ld_wqkv, 16 * L + 16)
                for i in range(6):
                    if not first:
                        act.wait_ge(qkv_mm, 6 * NTILE * L - 5 + i)
                    sl = slice(WCOL[i], WCOL[i] + 512)
                    nc.scalar.copy(w_hi[:, sl], w_raw[:, sl]).then_inc(whi_done, 1)

            def evacuate_qk(n, i, first):
                act.wait_ge(qkv_mm, 6 * n + i + 1)
                if not first or i >= 2:
                    act.wait_ge(ss_red, 4 * n + i - 1)
                fn(sq[:, i % 2, :], QKV[i % 2][:], ACT.Square).then_inc(qk_sq, 1)
                if not first:
                    act.wait_ge(qn_ready, 4 * n + i - 3)
                nc.scalar.copy(raw[:, i, :], QKV[i % 2][:]).then_inc(qkv_evac, 1)

            def evacuate_v(n, i, par, early):
                act.wait_ge(qkv_mm, 6 * n + i + 1)
                if not early and i == 4:
                    act.wait_ge(pv_mm, 2 * n - 2)
                nc.scalar.copy(vt[:, par, (i - 4) * 512:(i - 3) * 512], QKV[i % 2][:]).then_inc(qkv_evac, 1)

            def evacuate_t(m, i, first):
                act.wait_ge(t_mm, 4 * m + i + 1)
                if not first:
                    act.wait_ge(s_mm, 2 * m - 1 + i // 2)
                dst = (qT, kT)[i % 2]
                nc.scalar.copy(dst[:, i // 2, :, :].rearrange("p k n -> p (k n)"), TP[i % 2][:]).then_inc(qkt_evac, 1)

            def exponent(m, g):
                act.wait_ge(s_sub, 2 * m + g + 1)
                fn(es[:, g, :], es[:, g, :], ACT.Exp).then_inc(e_exp, 1)

            def evacuate_pt(m, g, first):
                act.wait_ge(pt_mm, 2 * m + g + 1)
                if not first:
                    act.wait_ge(pv_mm, 2 * m - 1 + g)
                nc.scalar.copy(pT[:, g, :, :].rearrange("p k n -> p (k n)"), TP[1 - g][:]).then_inc(pt_evac, 1)

            def evacuate_ot(m, first):
                act.wait_ge(pv_mm, 2 * m + 2)
                if not first:
                    act.wait_ge(wo_mm, m)
                for s in range(2):
                    last = nc.scalar.copy(oT[:, :, s * 64:s * 64 + 64], g3(OT[s][:], 64))
                last.then_inc(ot_evac, 1)

            def ffn_square(f):
                act.wait_ge(fc_ready, f + 1)
                fn(fsq[:], fc[:], ACT.Square).then_inc(fsq_done, 1)

            def ffn_rstd(f):
                act.wait_ge(var_mm, f + 1)
                fn(fln[:], OT[1][:, 256:512], ACT.Ln, bias=EPS).then_inc(fln_done, 1)
                act.wait_ge(fln_done, f + 1)
                act.wait_ge(fn_step, f)
                fn(frs[:], fln[:], ACT.Exp, scale=-0.5).then_inc(frs_done, 1)

            def ffn_gelu(f, L):
                act.wait_ge(vec_ready, L + 1)
                act.wait_ge(w2_mm, f)
                for c in range(3):
                    if c != 1:
                        act.wait_ge(w1_mm, 3 * f + 1 + c // 2)
                    src = OT[0][:, c * 256:(c + 1) * 256] if c < 2 else OT[1][0:FCH[2], 0:256]
                    fn(fh[0:FCH[c], c, :], src, ACT.Gelu, bias=vecs[0:FCH[c], 6 + c:7 + c]).then_inc(gelu_done, 1)

            def step(n, par, L, a=True, b=True, f=None, first=False, b_first=False, early=False):
                m = n - 1
                if a:
                    evacuate_qk(n, 0, first)
                if b:
                    evacuate_t(m, 0, b_first)
                    evacuate_t(m, 1, b_first)
                if a:
                    evacuate_qk(n, 1, first)
                if f is not None:
                    ffn_square(f)
                if a:
                    evacuate_qk(n, 2, first)
                if b:
                    evacuate_t(m, 2, b_first)
                    evacuate_t(m, 3, b_first)
                if b:
                    exponent(m, 0)
                if a:
                    evacuate_qk(n, 3, first)
                if f is not None:
                    ffn_rstd(f)
                if a:
                    evacuate_v(n, 4, par, early)
                if b:
                    exponent(m, 1)
                    evacuate_pt(m, 0, b_first)
                if f is not None:
                    ffn_gelu(f, L)
                if a:
                    evacuate_v(n, 5, par, early)
                if b:
                    evacuate_pt(m, 1, b_first)
                    evacuate_ot(m, b_first)

            act.wait_ge(small_ready, 1)
            split_hi(0, first=True)
            step(0, 0, 0, b=False, first=True, early=True)
            step(1, 1, 0, b_first=True, early=True)
            with act.Fori(0, DEPTH - 1) as L:
                with act.Fori(1, NQUAD) as q:
                    n, g = NTILE * L + 2 * q, NQUAD * L + q
                    step(n, 0, L)
                    step(n + 1, 1, L, f=g - 1)
                n, g = NTILE * L + NTILE, NQUAD * L + NQUAD
                split_hi(L + 1)
                step(n, 0, L)
                step(n + 1, 1, L, f=g - 1)
            with act.Fori(1, NQUAD) as q:
                n, g = NTILE * (DEPTH - 1) + 2 * q, NQUAD * (DEPTH - 1) + q
                step(n, 0, DEPTH - 1)
                step(n + 1, 1, DEPTH - 1, f=g - 1)
            n, g = DEPTH * NTILE, DEPTH * NQUAD
            step(n, 0, DEPTH - 1, a=False)
            ffn_square(g - 1)
            ffn_rstd(g - 1)
            ffn_gelu(g - 1, DEPTH - 1)

        @block.vector
        def _(dve):
            v = nc.vector
            tt, ts, stt = v.tensor_tensor, v.tensor_scalar, v.scalar_tensor_tensor

            v.memset(xs_hi[:].bitcast(F32), 0.0)
            v.memset(xs_lo[:].bitcast(F32), 0.0)
            v.memset(fx[:], 0.0)
            v.memset(gro[:, 7, :], 0.0).then_inc(const_made, 1)
            dve.wait_ge(ld_small, 16 * 13)
            dve.wait_ge(const_made, 6)
            v.tensor_copy(band[:], band_f[:])
            v.tensor_copy(identb[:], ident[:])
            v.tensor_copy(vecs[:], vecs_all[:, 0:NVEC]).then_inc(vec_ready, 1)
            tt(tabs[:], rot_base[:], scales[:, 0, :, :].rearrange("p a b -> p (a b)"), ALU.mult).then_inc(tabs_ready, 1)
            tt(wg_kv[:], wg[:, 1, :], wg[:, 2, :], ALU.add).then_inc(small_ready, 1)

            def ln_dve(base, xs):
                dve.wait_ge(chain, base)
                v.memset(ST[8][:, 0:1], 0.0)
                v.tensor_reduce(ST[0][:, 0:4], g3(xs, D), AX_X, ALU.add).then_inc(chain, 1)
                dve.wait_ge(chain, base + 1)
                ts(ST[1][:, 0:4], ST[0][:, 0:4], 1.0 / D, None, ALU.mult).then_inc(chain, 1)
                dve.wait_ge(chain, base + 2)
                tt(g3(st_x[:], D), g3(xs, D), bc(ST[1][:, 0:4], D), ALU.subtract).then_inc(chain, 1)
                dve.wait_ge(chain, base + 4)
                v.tensor_reduce(ST[2][:, 0:4], g3(psq[:], D), AX_X, ALU.add).then_inc(chain, 1)
                dve.wait_ge(chain, base + 7)
                tt(g3(st_x[:], D), g3(st_x[:], D), bc(ST[2][:, 0:4], D), ALU.mult).then_inc(chain, 1)

            dve.wait_ge(ld_x, 32)
            with dve.Fori(0, UNITS) as u:
                ln_dve(GSTEPS * u, xtok[:, bass.ds(u * 512, 512)])
                dve.wait_ge(chain, GSTEPS * u + 11)
                ts(gtok[:, bass.ds(u * 4, 4), :], g3(SC[0][:, 0:32], 8), 1.0, None, ALU.mult).then_inc(chain, 1)
            dve.wait_ge(chain, SCANS)
            tt(g3(gpk[:, 0, :], XH), gtok[:, :, 0:4], mid(bg[:, 0:4], NPAIR), ALU.add)
            tt(g3(gpk[:, 1, :], XH), gtok[:, :, 4:8], mid(bg[:, 4:8], NPAIR), ALU.add).then_inc(chain, 1)
            dve.wait_ge(chain, SCANS + 1)
            ts(gpk[:, 2, :], gpk[:, 1, :], -1.0, None, ALU.mult).then_inc(chain, 1)
            dve.wait_ge(chain, SCANS + 2)
            tt(gpk[:, 2, :], gpk[:, 2, :], gpk[:, 1, :], ALU.min).then_inc(chain, 1)
            dve.wait_ge(chain, SCANS + 5)
            stt(gpk[:, 3, :], gpk[:, 1, :], 0.0, gpk[:, 2, :], ALU.min, ALU.subtract).then_inc(chain, 1)
            dve.wait_ge(chain, SCANS + 7)
            v.tensor_copy(gro[:, 0:2, :], g3(TP[0][:, 0:256], 128)).then_inc(chain, 1)
            dve.wait_ge(chain, SCANS + 8)
            for sl in HALVES:
                last = v.tensor_tensor_scan(gro[:, 2, sl], gro[:, 0, sl], gro[:, 7, sl], 0.0, ALU.add, ALU.add)
            last.then_inc(chain, 1)
            dve.wait_ge(chain, SCANS + 9)
            tt(gro[:, 3, :], gro[:, 1, :], gro[:, 2, :], ALU.subtract).then_inc(chain, 1)
            dve.wait_ge(chain, SCANS + 10)
            for sl in HALVES:
                last = v.tensor_tensor_scan(gro[:, 4, sl], gro[:, 3, sl], gro[:, 7, sl], -3.0e38, ALU.max, ALU.add)
            last.then_inc(chain, 1)
            dve.wait_ge(chain, SCANS + 11)
            ts(gro[:, 5, :], gro[:, 4, :], -1.0, None, ALU.mult)
            stt(gro[:, 6, :], gro[:, 2, :], -1.0, gro[:, 4, :], ALU.mult, ALU.subtract).then_inc(chain, 1)

            with dve.Fori(0, UNITS) as u:
                base = MSTEPS * u + MIXING
                dve.wait_ge(chain, base + 2)
                for k in range(2):
                    last = tt(g3(gexp[:, k * 512:(k + 1) * 512], S), g3(TP[k][:], S), bc(st_a[:, k * 8:(k + 1) * 8], S), ALU.add)
                last.then_inc(chain, 1)
                dve.wait_ge(chain, base + 3)
                stt(g3(gexp[:], S), g3(gexp[:], S), 0.0, mid(causal[:], 16), ALU.min, ALU.add).then_inc(chain, 1)
                dve.wait_ge(chain, base + 5)
                for h in range(XH):
                    e = gexp[:].rearrange("p (k h s) -> p k h s", k=4, h=XH)[:, :, h, :]
                    last = stt(e, g3(SCX[h][:, 0:256], S), float(XD) ** -0.5, e, ALU.mult, ALU.mult)
                last.then_inc(chain, 1)
                dve.wait_ge(chain, base + 7)
                for k in range(2):
                    last = ts(ST[3][:, k * 8:(k + 1) * 8], g3(OT[k][:, 0:264], 33)[:, :, 32], -1.0, None, ALU.mult)
                last.then_inc(chain, 1)
                dve.wait_ge(chain, base + 8)
                for k in range(2):
                    last = tt(ST[3][:, k * 8:(k + 1) * 8], g3(OT[k][:, 0:264], 33)[:, :, 32], ST[3][:, k * 8:(k + 1) * 8], ALU.max)
                last.then_inc(chain, 1)
                dve.wait_ge(chain, base + 9)
                tt(ST[3], ST[3], st_em[:], ALU.max).then_inc(chain, 1)
                dve.wait_ge(chain, base + 10)
                ts(ST[3], ST[3], 1e-6, None, ALU.add).then_inc(chain, 1)
                dve.wait_ge(chain, base + 11)
                v.reciprocal(ST[3], ST[3]).then_inc(chain, 1)
                dve.wait_ge(chain, base + 12)
                for k in range(2):
                    last = tt(g3(hmix[:, k * 256:(k + 1) * 256], XD), g3(OT[k][:, 0:264], 33)[:, :, 0:32],
                              bc(ST[3][:, k * 8:(k + 1) * 8], XD), ALU.mult)
                last.then_inc(chain, 1)
                dve.wait_ge(chain, base + 13)
                v.tensor_reduce(ST[4], g3(hmix[:], XD), AX_X, ALU.add).then_inc(chain, 1)
                dve.wait_ge(chain, base + 14)
                ts(ST[4], ST[4], 1.0 / XD, None, ALU.mult).then_inc(mixed, 1)
                dve.wait_ge(mixed, u + 1)
                tt(g3(hmix[:], XD), g3(hmix[:], XD), bc(ST[4], XD), ALU.subtract).then_inc(chain, 1)
                dve.wait_ge(chain, base + 16)
                v.tensor_reduce(ST[5], g3(psq[:], XD), AX_X, ALU.add).then_inc(chain, 1)
                dve.wait_ge(chain, base + 19)
                tt(g3(hmix[:], XD), g3(hmix[:], XD), bc(ST[5], XD), ALU.mult).then_inc(chain, 1)
                dve.wait_ge(chain, base + 20)
                tt(g3(hmix[:], D), g3(hmix[:], D), mid(onorm[:], 4), ALU.mult).then_inc(chain, 1)
                x1 = xtok[:, bass.ds(u * 512, 512)]
                dve.wait_ge(chain, base + 21)
                tt(x1, x1, hmix[:], ALU.add).then_inc(chain, 1)
                ln_dve(base + 22, x1)

            def split_lo(L, first=False):
                for i in range(6):
                    dve.wait_ge(whi_done, 6 * L + i + 1)
                    sl = slice(WCOL[i], WCOL[i] + 512)
                    tt(w_lo[:, sl], w_raw[:, sl], w_hi[:, sl].bitcast(F32), ALU.subtract).then_inc(wlo_done, 1)

            def quad_views(q):
                cols = bass.ds(q * 256, 256) if not isinstance(q, int) else slice(q * 256, q * 256 + 256)
                return xT[0:64, cols], g3(xT[64:128, cols], S)[:, :, 0:S - 1]

            def late(t):
                return g3(t[64:128, :], S)[:, :, 1:S]

            def stationary(q, count, last_tile=None):
                if last_tile is not None:
                    dve.wait_ge(qkv_mm, 6 * last_tile + 6)
                lo, hi = quad_views(q)
                ts(xs_hi[0:64, :], lo, 1.0, None, ALU.mult)
                ts(late(xs_hi), hi, 1.0, None, ALU.mult).then_inc(xs_half, 1)
                dve.wait_ge(xs_half, count + 1)
                tt(xs_lo[0:64, :], lo, xs_hi[0:64, :].bitcast(F32), ALU.subtract)
                tt(late(xs_lo), hi, late(xs_hi[:].bitcast(F32)), ALU.subtract).then_inc(xs_ready, 1)

            def sum_squares(n, i, first):
                dve.wait_ge(qk_sq, 4 * n + i + 1)
                if i == 0 and not first:
                    dve.wait_ge(newton, 12 * n)
                v.tensor_reduce(ss[:, 8 * i:8 * i + 8], g3(sq[:, i % 2, :], DH), AX_X, ALU.add).then_inc(ss_red, 1)

            def norms(n, first):
                y, a, b = nwt[:, 0, :], nwt[:, 1, :], nwt[:, 2, :]
                dve.wait_ge(ss_red, 4 * n + 4)
                ts(ss[:], ss[:], 1e-24, None, ALU.max).then_inc(newton, 1)
                dve.wait_ge(newton, 12 * n + 1)
                ts(seed[:], ss[:].bitcast(I32), 1, None, ALU.logical_shift_right).then_inc(newton, 1)
                dve.wait_ge(newton, 12 * n + 2)
                if not first:
                    dve.wait_ge(qn_ready, 4 * n)
                ts(y.bitcast(I32), seed[:], -1.0, MAGIC, ALU.mult, ALU.add).then_inc(newton, 1)
                for k in range(3):
                    dve.wait_ge(newton, 12 * n + 3 + 3 * k)
                    tt(a, y, y, ALU.mult).then_inc(newton, 1)
                    dve.wait_ge(newton, 12 * n + 4 + 3 * k)
                    stt(b, a, -0.5, ss[:], ALU.mult, ALU.mult).then_inc(newton, 1)
                    dve.wait_ge(newton, 12 * n + 5 + 3 * k)
                    dst = rinv[:] if k == 2 else y
                    stt(dst, b, 1.5, y, ALU.add, ALU.mult).then_inc(newton, 1)

            def scale_qk(n, i, first):
                dve.wait_ge(newton, 12 * n + 12)
                dve.wait_ge(qkv_evac, 6 * n + i + 1)
                if not first:
                    dve.wait_ge(t_done, 4 * n + i - 3)
                tt(g3(qn[:, i, :], DH), g3(raw[:, i, :], DH), bc(rinv[:, 8 * i:8 * i + 8], DH), ALU.mult).then_inc(qn_ready, 1)
                dve.wait_ge(qn_ready, 4 * n + i + 1)
                if not first:
                    dve.wait_ge(rot_ready, 4 * n + i - 3)
                o = (2 * (i % 2) + 1) * DH
                swapped = qn[:, i, :].rearrange("p (h t d) -> p h t d", t=2, d=32)[:, :, ::-1, :]
                tab = tabs[:, o:o + DH].rearrange("p (t d) -> p t d", t=2).unsqueeze(1).broadcast_to([128, 8, 2, 32])
                tt(ur[:, i, :].rearrange("p (h t d) -> p h t d", t=2, d=32), swapped, tab, ALU.mult).then_inc(u_ready, 1)

            def softmax_shift(m, g, first):
                dve.wait_ge(s_mm, 2 * m + g + 1)
                v.tensor_reduce(smax[:, g, :], g3(SC[g][:], S), AX_X, ALU.max).then_inc(s_max, 1)
                dve.wait_ge(s_max, 2 * m + g + 1)
                if not first:
                    dve.wait_ge(pt_mm, 2 * m + g - 1)
                tt(g3(es[:, g, :], S), g3(SC[g][:], S), bc(smax[:, g, :], S), ALU.subtract).then_inc(s_sub, 1)

            def softmax_sum(m, g, first):
                dve.wait_ge(e_exp, 2 * m + g + 1)
                v.tensor_reduce(ssum[:, g, :], g3(es[:, g, :], S), AX_X, ALU.add).then_inc(e_sum, 1)
                dve.wait_ge(e_sum, 2 * m + g + 1)
                if not first:
                    dve.wait_ge(pn_ready, 2 * m + g - 1)
                v.reciprocal(sinv[:, g, :], ssum[:, g, :]).then_inc(e_inv, 1)

            def residual(w, local):
                dve.wait_ge(wo_mm, w + 1)
                cols = bass.ds(local * 128, 128) if not isinstance(local, int) else slice(local * 128, local * 128 + 128)
                tt(xT[:, cols], OT[0][:, 0:128], xT[:, cols], ALU.add).then_inc(resid, 1)

            def ffn_input(f, q):
                dve.wait_ge(resid, 2 * f + 2)
                dve.wait_ge(fc_ready, f)
                lo, hi = quad_views(q)
                ts(fx[0:64, :], lo, 1.0, None, ALU.mult)
                ts(late(fx), hi, 1.0, None, ALU.mult).then_inc(fx_ready, 1)

            def ffn_centre(f):
                dve.wait_ge(mean_mm, f + 1)
                dve.wait_ge(fn_step, f)
                tt(fc[:], OT[1][:, 0:256], fx[:], ALU.subtract).then_inc(fc_ready, 1)

            def ffn_norm(f, L):
                dve.wait_ge(frs_done, f + 1)
                dve.wait_ge(w1_mm, 3 * f)
                stt(fxn[:], fc[:], -1.0, frs[:], ALU.mult, ALU.mult).then_inc(fn_step, 1)
                dve.wait_ge(fn_step, f + 1)
                ts(fxn[:], fxn[:], vecs[:, 0:1], vecs[:, 1:2], ALU.mult, ALU.add).then_inc(fxn_ready, 1)

            def ffn_hidden(f):
                for c in (0, 1, 2):
                    dve.wait_ge(gelu_done, 3 * f + c + 1)
                    if c == 0:
                        dve.wait_ge(w1_mm, 3 * f + 3)
                    rows = slice(0, FCH[c])
                    src = TP[0][rows, c * 256:(c + 1) * 256] if c < 2 else OT[1][rows, 256:512]
                    stt(fh[rows, c, :], src, vecs[rows, 3 + c:4 + c], fh[rows, c, :], ALU.add, ALU.mult).then_inc(h_ready, 1)

            def ffn_residual(f, q):
                dve.wait_ge(w2_mm, f + 1)
                cols = bass.ds(q * 256, 256) if not isinstance(q, int) else slice(q * 256, q * 256 + 256)
                stt(xT[:, cols], SC[0][:, 0:256], vecs[:, 2:3], xT[:, cols], ALU.add, ALU.add).then_inc(ffn_done, 1)

            def new_tables(L, n):
                dve.wait_ge(t_done, 4 * n)
                tt(tabs[:], rot_base[:], scales[:, bass.ds(L, 1), :, :].rearrange("p o a b -> p (o a b)"),
                   ALU.mult).then_inc(tabs_ready, 1)
                dve.wait_ge(tabs_ready, L + 1)

            def step(n, a=True, b=True, w=None, f=None, fq=None, first=False, b_first=False, tables=None, nxt=None):
                m = n - 1
                if a:
                    sum_squares(n, 0, first)
                if w is not None:
                    residual(n - 2, w)
                if f is not None:
                    ffn_input(f, fq)
                if a:
                    sum_squares(n, 1, first)
                if b:
                    softmax_shift(m, 0, b_first)
                if f is not None:
                    ffn_centre(f)
                if a:
                    sum_squares(n, 2, first)
                    sum_squares(n, 3, first)
                if b:
                    softmax_sum(m, 0, b_first)
                if f is not None:
                    ffn_norm(f, None)
                if a:
                    norms(n, first)
                if tables is not None:
                    new_tables(tables, n)
                if b:
                    softmax_shift(m, 1, b_first)
                if a:
                    scale_qk(n, 0, first)
                if b:
                    softmax_sum(m, 1, b_first)
                if a:
                    scale_qk(n, 1, first)
                if f is not None:
                    ffn_hidden(f)
                if a:
                    scale_qk(n, 2, first)
                    scale_qk(n, 3, first)
                if nxt is not None:
                    stationary(*nxt, n)
                if f is not None:
                    ffn_residual(f, fq)

            dve.wait_ge(chain, MIXING + UNITS * MSTEPS)
            dve.wait_ge(tabs_ready, 1)
            stationary(0, 0)
            split_lo(0)
            step(0, b=False, first=True)
            step(1, b_first=True, nxt=(1, 1))
            with dve.Fori(0, DEPTH - 1) as L:
                with dve.Fori(1, NQUAD) as q:
                    n, g = NTILE * L + 2 * q, NQUAD * L + q
                    step(n, w=2 * q - 2)
                    step(n + 1, w=2 * q - 1, f=g - 1, fq=q - 1, nxt=((q + 1) % NQUAD, g + 1))
                n, g = NTILE * L + NTILE, NQUAD * L + NQUAD
                split_lo(L + 1)
                step(n, w=NTILE - 2, tables=L + 1)
                step(n + 1, w=NTILE - 1, f=g - 1, fq=NQUAD - 1, nxt=(1, g + 1))
                dve.wait_ge(ffn_done, g)
                ts(vecs[:], vecs_all[:, bass.ds(L * NVEC + NVEC, NVEC)], 1.0, None, ALU.mult).then_inc(vec_ready, 1)
            with dve.Fori(1, NQUAD - 1) as q:
                n, g = NTILE * (DEPTH - 1) + 2 * q, NQUAD * (DEPTH - 1) + q
                step(n, w=2 * q - 2)
                step(n + 1, w=2 * q - 1, f=g - 1, fq=q - 1, nxt=(q + 1, g + 1))
            n, g = DEPTH * NTILE - 2, DEPTH * NQUAD - 1
            step(n, w=NTILE - 4)
            step(n + 1, w=NTILE - 3, f=g - 1, fq=NQUAD - 2)
            step(n + 2, a=False, w=NTILE - 2)
            residual(n + 1, NTILE - 1)
            ffn_input(g, NQUAD - 1)
            ffn_centre(g)
            ffn_norm(g, None)
            ffn_hidden(g)
            ffn_residual(g, NQUAD - 1)
            for k in range(UNITS):
                dve.wait_ge(end_mm, k + 1)
                sl = slice(k * 512, (k + 1) * 512)
                tt(xtok[:, sl], QKV[k % 2][:], xtok[:, sl], ALU.add).then_inc(end_add, 1)


_ARRAYS = ["x", "ctx", "wgate", "bgate", "outnorm", "wqkv", "qscale", "kscale", "wo", "w1", "w2", "vec", "rot", "band", "causal"]


def kernel(**inputs):
    import numpy as _np
    import concourse.bacc as _bacc
    from concourse import mybir as _mybir
    from concourse.bass_utils import run_bass_kernel_spmd as _run

    i = {k: _np.asarray(v) for k, v in inputs.items()}
    f32 = _np.float32
    a = {"x": i["x"].reshape(NTOK, D), "ctx": i["ctx_1024"].reshape(NTOK, D)}
    a["wgate"] = _np.concatenate([i["L0_xattn_igate_kernel"], i["L0_xattn_fgate_kernel"]], 1)
    a["bgate"] = _np.concatenate([i["L0_xattn_igate_bias"], i["L0_xattn_fgate_bias"]])
    a["outnorm"] = i["L0_xattn_outnorm_scale"]
    a["wqkv"] = i["L0_ffn_Wqkv"]
    a["qscale"], a["kscale"] = i["L0_ffn_q_scale"], i["L0_ffn_k_scale"]
    a["wo"] = i["L0_ffn_Wo"].reshape(DEPTH, 8, 128, D).transpose(0, 2, 1, 3)
    a["w1"] = i["L0_ffn_W1"]
    w2 = _np.zeros((DEPTH, 384, D), f32)
    w2[:, :FF] = i["L0_ffn_W2"]
    a["w2"] = w2.reshape(DEPTH, 3, 128, D).transpose(0, 2, 1, 3)
    vec = _np.zeros((DEPTH, NVEC, 128), f32)
    vec[:, 0], vec[:, 1], vec[:, 2] = i["L0_ffn_ln_g"], i["L0_ffn_ln_b"], i["L0_ffn_b2"]
    for part in range(2):
        for c in range(3):
            vec[:, 3 + 3 * part + c, :FCH[c]] = i["L0_ffn_b1"][:, part * FF + c * 128:part * FF + c * 128 + FCH[c]]
    a["vec"] = vec.transpose(2, 0, 1).reshape(128, DEPTH * NVEC)
    a["rot"], a["band"], a["causal"] = constants()

    nc = _bacc.Bacc("TRN2", target_bir_lowering=False, num_devices=1)
    arrays, args = {}, []
    for name in _ARRAYS:
        arr = _np.ascontiguousarray(a[name])
        arrays[f"in_{name}"] = arr
        args.append(nc.dram_tensor(f"in_{name}", arr.shape, _mybir.dt.from_np(arr.dtype), kind="ExternalInput").ap())
    args.append(nc.dram_tensor("out_x", (NTOK, D), _mybir.dt.float32, kind="ExternalOutput").ap())
    transformer_program(nc, *args)
    r = _run(nc, [arrays], core_ids=[0])
    return r.results[0]["out_x"].reshape(NSEQ, S, D)
```

```python
from contextlib import ExitStack

import numpy as np

import concourse.bass as bass
from concourse import mybir

F32 = mybir.dt.float32
F32R = mybir.dt.float32r
BF16 = mybir.dt.bfloat16
I32 = mybir.dt.int32
ALU = mybir.AluOpType
ACT = mybir.ActivationFunctionType
AX_X = mybir.AxisListType.X

NSEQ, S, D = 64, 64, 128
NPAIR = NSEQ // 2
TOK = 2 * S
NTOK = NSEQ * S
NTILE = NPAIR
NQUAD = NTILE // 2
DEPTH, HEADS, DH = 6, 16, 64
INNER = HEADS * DH
XH = 4
XD = D // XH
FF = 341
FCH = [128, 128, FF - 256]
WINDOW = 32
NVEC = 9
MASKED = -1.0e30
MAGIC = float(0x5F3759DF)
WCOL = [0, INNER, 512, INNER + 512, 2 * INNER, 2 * INNER + 512]
UNITS = 8
GSTEPS, SSTEPS, MSTEPS = 12, 14, 32
SCANS = UNITS * GSTEPS
MIXING = SCANS + SSTEPS


def constants():
    half = np.arange(0, DH, 2, dtype=np.float64)
    inv_freq = 1.0 / 10000.0 ** (half / DH)
    t = np.arange(S, dtype=np.float64)
    freqs = np.concatenate([t[:, None] * inv_freq[None]] * 2, -1)
    base = (half + 0.4 * DH) / (1.4 * DH)
    scale = np.concatenate([base[None] ** ((t - S // 2) / (WINDOW // 2))[:, None]] * 2, -1)
    sign = np.where(np.arange(DH) < DH // 2, -1.0, 1.0)[None]
    rot = np.stack([8 * np.cos(freqs) * scale, 8 * sign * np.sin(freqs) * scale,
                    np.cos(freqs) / scale, sign * np.sin(freqs) / scale], 1)
    rot = np.tile(rot, (2, 1, 1)).astype(np.float32).reshape(TOK, 4 * DH)
    i, j = np.arange(S)[:, None], np.arange(S)[None]
    band = np.where((j <= i) & (j >= i - WINDOW), 0.0, MASKED).astype(np.float32)
    band = np.tile(band, (2, 8))
    causal = np.tile(np.where(i <= j, 0.0, MASKED).astype(np.float32), (2, 1))
    return rot, band, causal


def transformer_program(nc, x, ctx_in, wgate, bgate, outnorm, wqkv, qscale, kscale, wo, w1, w2, vec,
                        rot_c, band_c, causal_c, out):
    with ExitStack() as stack:
        def sb(name, shape, dt=F32):
            return stack.enter_context(nc.sbuf_tensor(name, shape, dt))

        def bank(name):
            return stack.enter_context(nc.psum_tensor(name, [128, 512], F32))

        def sem(name):
            return stack.enter_context(nc.semaphore(name))

        QKV = [bank("qkv0"), bank("qkv1")]
        TP = [bank("tp0"), bank("tp1")]
        SC = [bank("sc0"), bank("sc1")]
        OT = [bank("ot0"), bank("ot1")]

        SCX = [SC[0], SC[1], QKV[0], QKV[1]]

        xtok = sb("xtok", [128, NTOK])
        xT = sb("xT", [128, NTOK])
        ident = sb("ident", [128, 128])
        identb = sb("identb", [128, 128], BF16)
        cst = sb("cst", [128, 4])
        rot_base = sb("rot_base", [128, 4 * DH])
        scales = sb("scales", [128, DEPTH, 4, DH])
        tabs = sb("tabs", [128, 4 * DH])
        band_f = sb("band_f", [128, 512])
        band = sb("band", [128, 512], BF16)
        ones = sb("ones", [128, 128])
        centring = sb("centring", [128, 128])
        vecs_all = sb("vecs_all", [128, DEPTH * NVEC])
        vecs = sb("vecs", [128, NVEC])
        w_raw = sb("w_raw", [128, 3 * INNER])
        w_hi = sb("w_hi", [128, 3 * INNER], F32R)
        w_lo = sb("w_lo", [128, 3 * INNER], F32R)
        wo_s = sb("wo_s", [128, 8, 128])
        w1_s = sb("w1_s", [128, 2 * FF])
        w2_s = sb("w2_s", [128, 3, 128])
        arena = sb("arena", [128, 4 * 2048])
        raw = arena[:, 0:2048].rearrange("p (c n) -> p c n", c=4)
        qn = arena[:, 2048:4096].rearrange("p (c n) -> p c n", c=4)
        tr = arena[:, 4096:6144].rearrange("p (c n) -> p c n", c=4)
        ur = arena[:, 6144:8192].rearrange("p (c n) -> p c n", c=4)
        xs_hi = sb("xs_hi", [128, 256], F32R)
        xs_lo = sb("xs_lo", [128, 256], F32R)
        sq = sb("sq", [128, 2, 512])
        ss = sb("ss", [128, 32])
        seed = sb("seed", [128, 32], I32)
        nwt = sb("nwt", [128, 3, 32])
        rinv = sb("rinv", [128, 32])
        qT = sb("qT", [128, 2, 4, 128])
        kT = sb("kT", [128, 2, 4, 128])
        vt = sb("vt", [128, 2, INNER])
        es = sb("es", [128, 2, 512])
        smax = sb("smax", [128, 2, 8])
        ssum = sb("ssum", [128, 2, 8])
        sinv = sb("sinv", [128, 2, 8])
        pT = sb("pT", [128, 2, 4, 128])
        oT = sb("oT", [128, 8, 128])
        fx = sb("fx", [128, 256])
        fsq = sb("fsq", [128, 256])
        fln = sb("fln", [128, 256])
        frs = sb("frs", [128, 256])
        fxn = sb("fxn", [128, 256])
        fh = sb("fh", [128, 3, 256])
        ctok = arena[:, 0:4096]
        xlT = arena[:, 4096:8192]
        wg = sb("wg", [128, 3, 8])
        wg_kv = sb("wg_kv", [128, 8])
        bg = sb("bg", [128, 8])
        onorm = sb("onorm", [128, D])
        causal = sb("causal", [128, S])
        gtok = sb("gtok", [128, NPAIR, 8])
        gpk = sb("gpk", [128, 8, 128])
        gro = sb("gro", [128, 8, 128])
        a_tok = sb("a_tok", [128, 128])
        em_tok = sb("em_tok", [128, 128])
        st_x = sb("st_x", [128, 512])
        st_c = sb("st_c", [128, 512])
        st_v = sb("st_v", [128, 16, 33])
        st_sel = sb("st_sel", [128, 16])
        st_em = sb("st_em", [128, 16])
        st_a = sb("st_a", [128, 16])
        st_xT = sb("st_xT", [128, 512])
        st_cT = sb("st_cT", [128, 512])
        gexp = sb("gexp", [128, 1024])
        hmix = sb("hmix", [128, 512])
        psq = sb("psq", [128, 512])
        psm = sb("psm", [128, 12, 16])

        ld_x, ld_ctx, ld_small = sem("ld_x"), sem("ld_ctx"), sem("ld_small")
        ld_wqkv, ld_wo, ld_ffn = sem("ld_wqkv"), sem("ld_wo"), sem("ld_ffn")
        stored = sem("stored")
        const_made, const_init = sem("const_made"), sem("const_init")
        small_ready = sem("small_ready")
        chain, mixed = sem("chain_step"), sem("mixed")
        qkv_mm, t_mm, s_mm, pt_mm, pv_mm, wo_mm = map(sem, ("qkv_mm", "t_mm", "s_mm", "pt_mm", "pv_mm", "wo_mm"))
        centre_mm, var_mm, w1_mm, w2_mm = map(sem, ("centre_mm", "var_mm", "w1_mm", "w2_mm"))
        qk_sq, qkv_evac, qkt_evac, e_exp, pt_evac, ot_evac = map(
            sem, ("qk_sq", "qkv_evac", "qkt_evac", "e_exp", "pt_evac", "ot_evac"))
        fsq_done, fln_done, frs_done, gelu_done, whi_done = map(
            sem, ("fsq_done", "fln_done", "frs_done", "gelu_done", "whi_done"))
        ss_red, newton, qn_ready, u_ready, s_max, s_sub, e_sum, e_inv = map(
            sem, ("ss_red", "newton", "qn_ready", "u_ready", "s_max", "s_sub", "e_sum", "e_inv"))
        resid, xs_half, xs_ready, fx_ready, fn_step, fxn_ready, h_ready, ffn_done = map(
            sem, ("resid", "xs_half", "xs_ready", "fx_ready", "fn_step", "fxn_ready", "h_ready", "ffn_done"))
        wlo_done, tabs_ready, vec_ready = sem("wlo_done"), sem("tabs_ready"), sem("vec_ready")
        t_done, rot_ready, pn_ready = sem("t_done"), sem("rot_ready"), sem("pn_ready")
        end_mm, end_add = sem("end_mm"), sem("end_add")

        ST = [psm[:, k, :] for k in range(12)]
        HALVES = (slice(0, 64), slice(64, 128))

        def bc(ap, n):
            return ap.unsqueeze(2).broadcast_to([ap.shape[0], ap.shape[1], n])

        def mid(ap, n):
            return ap.unsqueeze(1).broadcast_to([ap.shape[0], n, ap.shape[1]])

        def g3(ap, n):
            return ap.rearrange("p (a n) -> p a n", n=n)

        def views(k, width):
            cols = bass.ds(k * width, width) if not isinstance(k, int) else slice(k * width, k * width + width)
            return xT[0:64, cols], g3(xT[64:128, cols], S)[:, :, 0:S - 1]

        def late(t):
            return g3(t[64:128, :], S)[:, :, 1:S]

        block = stack.enter_context(nc.Block())

        @block.sync
        def _(sp):
            xv = x.rearrange("(p t) d -> t p d", t=TOK)
            cv = ctx_in.rearrange("(p t) d -> t p d", t=TOK)
            for k in range(2):
                sl = slice(k * 2048, (k + 1) * 2048)
                sp.dma_start(g3(xtok[:, sl], D), xv[:, k * 16:(k + 1) * 16, :]).then_inc(ld_x, 16)
                sp.dma_start(g3(ctok[:, sl], D), cv[:, k * 16:(k + 1) * 16, :]).then_inc(ld_ctx, 16)
            sp.dma_start(wg[:], wgate.rearrange("(k p) g -> p k g", p=128)).then_inc(ld_small, 16)
            sp.dma_start(bg[:], bgate.partition_broadcast(128)).then_inc(ld_small, 16)
            sp.dma_start(onorm[:], outnorm.partition_broadcast(128)).then_inc(ld_small, 16)
            sp.dma_start(causal[:], causal_c).then_inc(ld_small, 16)
            sp.dma_start(rot_base[:], rot_c).then_inc(ld_small, 16)
            sp.dma_start(band_f[:], band_c).then_inc(ld_small, 16)
            sp.dma_start(vecs_all[:], vec).then_inc(ld_small, 16)
            for k, src in enumerate((qscale, kscale)):
                rep = src.partition_broadcast(128)
                sp.dma_start(scales[:, :, 2 * k, :], rep).then_inc(ld_small, 16)
                sp.dma_start(scales[:, :, 2 * k + 1, 0:32], rep[:, :, 32:64]).then_inc(ld_small, 16)
                sp.dma_start(scales[:, :, 2 * k + 1, 32:64], rep[:, :, 0:32]).then_inc(ld_small, 16)
            sp.dma_start(w_raw[:], wqkv[0]).then_inc(ld_wqkv, 16)
            sp.dma_start(wo_s[:], wo[0]).then_inc(ld_wo, 16)
            sp.dma_start(w1_s[:], w1[0]).then_inc(ld_ffn, 16)
            sp.dma_start(w2_s[:], w2[0]).then_inc(ld_ffn, 16)
            with sp.Fori(0, DEPTH - 1) as L:
                sp.wait_ge(whi_done, 6 * L + 6)
                sp.wait_ge(wlo_done, 6 * L + 6)
                sp.dma_start(w_raw[:], wqkv[bass.ds(L + 1, 1)].rearrange("o p n -> (o p) n")).then_inc(ld_wqkv, 16)
                sp.wait_ge(wo_mm, NTILE * L + NTILE)
                sp.dma_start(wo_s[:], wo[bass.ds(L + 1, 1)].rearrange("o p k n -> (o p) k n")).then_inc(ld_wo, 16)
                sp.wait_ge(w2_mm, NQUAD * L + NQUAD)
                sp.dma_start(w1_s[:], w1[bass.ds(L + 1, 1)].rearrange("o p n -> (o p) n")).then_inc(ld_ffn, 16)
                sp.dma_start(w2_s[:], w2[bass.ds(L + 1, 1)].rearrange("o p k n -> (o p) k n")).then_inc(ld_ffn, 16)
            ov = out.rearrange("(p t) d -> t p d", t=TOK)
            for k in range(UNITS):
                sp.wait_ge(end_add, k + 1)
                sp.dma_start(ov[:, 4 * k:4 * k + 4, :], g3(xtok[:, k * 512:(k + 1) * 512], D)).then_inc(stored, 16)
            sp.wait_ge(stored, 16 * UNITS)

        @block.gpsimd
        def _(pool):
            gps = nc.gpsimd
            gps.memset(ident[:], 0.0).then_inc(const_init, 1)
            gps.memset(ones[:], 1.0 / D).then_inc(const_made, 1)
            gps.memset(cst[:, 0:1], 1e-5).then_inc(const_made, 1)
            gps.memset(cst[:, 1:2], 1.0).then_inc(const_made, 1)
            gps.memset(st_v[:], 1.0).then_inc(const_made, 1)
            pool.wait_ge(const_init, 1)
            gps.affine_select(out=ident[:], in_=ident[:], compare_op=ALU.not_equal, fill=1.0, base=0,
                              pattern=[[-1, 128]], channel_multiplier=1).then_inc(const_made, 1)

            def rotate(n, i, first=False):
                tab = tabs[:, (i % 2) * 2 * DH:(i % 2) * 2 * DH + DH]
                pool.wait_ge(qn_ready, 4 * n + i + 1)
                if not first:
                    pool.wait_ge(t_mm, 4 * n + i - 3)
                gps.tensor_tensor(g3(tr[:, i, :], DH), g3(qn[:, i, :], DH), mid(tab, 8), ALU.mult).then_inc(t_done, 1)
                pool.wait_ge(t_done, 4 * n + i + 1)
                pool.wait_ge(u_ready, 4 * n + i + 1)
                gps.tensor_tensor(tr[:, i, :], tr[:, i, :], ur[:, i, :], ALU.add).then_inc(rot_ready, 1)

            def normalise(m, g):
                pool.wait_ge(e_inv, 2 * m + g + 1)
                gps.tensor_tensor(g3(es[:, g, :], S), g3(es[:, g, :], S), bc(sinv[:, g, :], S),
                                  ALU.mult).then_inc(pn_ready, 1)

            def step(n, a=True, b=True, first=False):
                if b:
                    normalise(n - 1, 0)
                if a:
                    rotate(n, 0, first)
                    rotate(n, 1, first)
                if b:
                    normalise(n - 1, 1)
                if a:
                    rotate(n, 2, first)
                    rotate(n, 3, first)

            step(0, b=False, first=True)
            step(1)
            with pool.Fori(1, DEPTH * NQUAD) as q:
                step(2 * q)
                step(2 * q + 1)
            step(DEPTH * NTILE, a=False)

        @block.tensor
        def _(pe):
            mm = nc.tensor.matmul

            def carry_wait(col=0):
                mm(OT[0][:, col:col + 1], identb[:], identb[:, 0:1], start=True, stop=True)

            pe.wait_ge(const_made, 6)
            pe.wait_ge(small_ready, 1)
            with pe.Fori(0, UNITS) as u:
                pe.wait_ge(chain, GSTEPS * u + 8)
                for bk, src in zip(TP, (st_x, st_c)):
                    for k in range(4):
                        last = nc.tensor.transpose(bk[:, k * 128:(k + 1) * 128], src[:, k * 128:(k + 1) * 128], ident[:])
                last.then_inc(chain, 1)
                pe.wait_ge(chain, GSTEPS * u + 10)
                for k in range(4):
                    mm(SC[0][:, 8 * k:8 * k + 8], st_xT[:, k * 128:(k + 1) * 128], wg[:, 0, :], start=True, stop=False)
                    last = mm(SC[0][:, 8 * k:8 * k + 8], st_cT[:, k * 128:(k + 1) * 128], wg_kv[:], start=False, stop=True)
                last.then_inc(chain, 1)
            pe.wait_ge(chain, SCANS + 6)
            nc.tensor.transpose(TP[0][:, 0:128], gpk[:, 3, :], ident[:])
            nc.tensor.transpose(TP[0][:, 128:256], gpk[:, 0, :], ident[:]).then_inc(chain, 1)
            pe.wait_ge(chain, SCANS + 12)
            nc.tensor.transpose(TP[1][:, 0:128], gro[:, 3, :], ident[:])
            nc.tensor.transpose(TP[1][:, 128:256], gro[:, 6, :], ident[:]).then_inc(chain, 1)

            with pe.Fori(0, UNITS) as u:
                pe.wait_ge(chain, MSTEPS * u + (MIXING + 1))
                for k in range(4):
                    for h in range(XH):
                        for b in range(2):
                            c = k * XH + h
                            o = (k % 2) * 256 + h * 64
                            mm(TP[k // 2][HALVES[b], o:o + 64], st_sel[:, c:c + 1].broadcast_to([128, 64]),
                               gro[:, 5, 64 * b:64 * b + 64], start=True, stop=True)
                for k in range(4):
                    for b in range(2):
                        for h in range(XH):
                            c = k * 128 + 64 * b
                            last = mm(SCX[h][HALVES[b], k * 64:k * 64 + 64], st_cT[32 * h:32 * h + 32, c:c + 64],
                                      st_xT[32 * h:32 * h + 32, c:c + 64], start=True, stop=True,
                                      tile_position=(32 * h, 64 * b))
                last.then_inc(chain, 1)
                pe.wait_ge(chain, MSTEPS * u + (MIXING + 6))
                carry_wait()
                for k in range(4):
                    for h in range(XH):
                        for b in range(2):
                            c = k * XH + h
                            o = (k % 2) * 132 + h * 33
                            last = mm(OT[k // 2][HALVES[b], o:o + 33], gexp[HALVES[b], c * 64:(c + 1) * 64],
                                      st_v[HALVES[b], c, :], start=True, stop=True)
                last.then_inc(chain, 1)
                pe.wait_ge(chain, MSTEPS * u + (MIXING + 30))
                for k in range(4):
                    last = nc.tensor.transpose(QKV[0][:, k * 128:(k + 1) * 128], st_x[:, k * 128:(k + 1) * 128], ident[:])
                last.then_inc(chain, 1)

            def project(n, par, i, first=False, layer=None):
                if layer is not None:
                    pe.wait_ge(whi_done, 6 * layer + i + 1)
                    pe.wait_ge(wlo_done, 6 * layer + i + 1)
                if not first or i >= 2:
                    pe.wait_ge(qkv_evac, 6 * n + i - 1)
                bk = QKV[i % 2]
                xh, xl = (t[:, par * 128:(par + 1) * 128] for t in (xs_hi, xs_lo))
                wh, wl = (t[:, WCOL[i]:WCOL[i] + 512] for t in (w_hi, w_lo))
                mm(bk[:], xh, wh, start=True, stop=False)
                mm(bk[:], xh, wl, start=False, stop=False)
                mm(bk[:], xl, wh, start=False, stop=True).then_inc(qkv_mm, 1)

            def transposes(m, i, first):
                if not first and i in (0, 3):
                    pe.wait_ge(pt_evac, 2 * m - 1 + i // 3)
                if i >= 2:
                    pe.wait_ge(qkt_evac, 4 * m + i - 1)
                pe.wait_ge(rot_ready, 4 * m + i + 1)
                for k in range(4):
                    last = nc.tensor.transpose(TP[i % 2][:, k * 128:(k + 1) * 128], tr[:, i, k * 128:(k + 1) * 128], ident[:])
                last.then_inc(t_mm, 1)

            def scores(m, g, first, up=None, down=None):
                if down is not None and g == 0:
                    pe.wait_ge(ffn_done, down + 1)
                if up is not None and g == 1:
                    pe.wait_ge(fn_step, up + 1)
                if not first:
                    pe.wait_ge(s_sub, 2 * m + g - 1)
                pe.wait_ge(qkt_evac, 4 * m + 2 * g + 2)
                mm(SC[g][:], identb[:], band[:], start=True, stop=True)
                for k in range(4):
                    for s in range(2):
                        for h in range(2):
                            sl, c = HALVES[h], k * 128 + s * 64
                            last = mm(SC[g][sl, c:c + 64], qT[sl, g, k, s * 64:s * 64 + 64],
                                      kT[sl, g, k, s * 64:s * 64 + 64], start=False, stop=True,
                                      skip_group_check=True)
                last.then_inc(s_mm, 1)

            def prob_transposes(m, g, b=True):
                if g == 1 and b:
                    pe.wait_ge(qkt_evac, 4 * m + 6)
                pe.wait_ge(pn_ready, 2 * m + g + 1)
                for k in range(4):
                    last = nc.tensor.transpose(TP[g][:, k * 128:(k + 1) * 128], es[:, g, k * 128:(k + 1) * 128], ident[:])
                last.then_inc(pt_mm, 1)

            def values(m, g, par, first):
                if g == 0:
                    if not first:
                        pe.wait_ge(resid, m)
                    pe.wait_ge(qkv_evac, 6 * m + 6)
                pe.wait_ge(pt_evac, 2 * m + g + 1)
                if g == 0:
                    carry_wait()
                else:
                    carry_wait(256)
                for k in range(4):
                    for h in range(2):
                        for s in range(2):
                            hd = 8 * g + 2 * k + h
                            last = mm(OT[s][HALVES[h], (4 * g + k) * 64:(4 * g + k) * 64 + 64],
                                      vt[HALVES[s], par, hd * DH:(hd + 1) * DH],
                                      pT[HALVES[s], g, k, h * 64:h * 64 + 64], start=True, stop=True)
                last.then_inc(pv_mm, 1)

            def out_product(w, L):
                pe.wait_ge(ld_wo, 16 * L + 16)
                pe.wait_ge(ot_evac, w + 1)
                for k in range(8):
                    last = mm(OT[0][:, 0:128], wo_s[:, k, :], oT[:, k, :], start=(k == 0), stop=(k == 7))
                last.then_inc(wo_mm, 1)

            def ffn_centre(f, scored):
                pe.wait_ge(s_sub, scored)
                pe.wait_ge(fx_ready, f + 1)
                mm(SC[1][:, 0:256], centring[:], fx[:], start=True, stop=True).then_inc(centre_mm, 1)

            def ffn_var(f):
                pe.wait_ge(fsq_done, f + 1)
                mm(SC[1][:, 256:512], ones[:], fsq[:], start=True, stop=True).then_inc(var_mm, 1)

            def ffn_up(f, L, t):
                pe.wait_ge(resid, t + 1)
                pe.wait_ge(ld_ffn, 32 * L + 32)
                pe.wait_ge(fxn_ready, f + 1)
                for bk, parts in ((OT[0], ((1, 0), (1, 1))), (OT[1], ((1, 2), (0, 2))), (TP[1], ((0, 0), (0, 1)))):
                    for k, (gate, c) in enumerate(parts):
                        o = gate * FF + c * 128
                        last = mm(bk[0:FCH[c], k * 256:(k + 1) * 256], w1_s[:, o:o + FCH[c]], fxn[:], start=True, stop=True)
                    last.then_inc(w1_mm, 1)

            def ffn_down(f, scored):
                pe.wait_ge(s_sub, scored)
                pe.wait_ge(h_ready, 3 * f + 3)
                for c in range(3):
                    last = mm(SC[0][:, 0:256], w2_s[0:FCH[c], c, :], fh[0:FCH[c], c, :], start=(c == 0), stop=(c == 2))
                last.then_inc(w2_mm, 1)

            def step(n, par, L, a=True, b=True, c=True, up=None, down=None, first=False, b_first=False, c_first=False,
                     layer=None, ffn_layer=None):
                m, t = n - 1, n - 2
                if a:
                    pe.wait_ge(xs_ready, n + 1)
                    project(n, par, 0, first, layer)
                if c:
                    prob_transposes(t, 0)
                if a:
                    project(n, par, 1, first, layer)
                if b:
                    transposes(m, 0, b_first)
                if a:
                    project(n, par, 2, first, layer)
                if down is not None:
                    ffn_down(down, 2 * m - 1)
                if b:
                    transposes(m, 1, b_first)
                if a:
                    project(n, par, 3, first, layer)
                if c:
                    values(t, 0, par, c_first)
                if up is not None:
                    ffn_centre(up, 2 * m)
                if c:
                    prob_transposes(t, 1, b)
                if b:
                    scores(m, 0, b_first, down=down)
                if up is not None:
                    ffn_var(up)
                if b:
                    transposes(m, 2, b_first)
                if c:
                    values(t, 1, par, c_first)
                if b:
                    transposes(m, 3, b_first)
                if a:
                    project(n, par, 4, first, layer)
                if b:
                    scores(m, 1, b_first, up=up)
                if c:
                    out_product(t, L)
                if a:
                    project(n, par, 5, first, layer)
                if up is not None:
                    ffn_up(up, L if ffn_layer is None else ffn_layer, t)

            pe.wait_ge(const_made, 6)
            step(0, 0, 0, b=False, c=False, first=True, layer=0)
            step(1, 1, 0, c=False, b_first=True)
            step(2, 0, 0, c_first=True)
            step(3, 1, 0)
            with pe.Fori(2, NQUAD) as q:
                step(2 * q, 0, 0, up=q - 2)
                step(2 * q + 1, 1, 0, down=q - 2)
            with pe.Fori(1, DEPTH) as L:
                n, g = NTILE * L, NQUAD * L
                step(n, 0, L - 1, up=g - 2, layer=L)
                step(n + 1, 1, L - 1, down=g - 2)
                step(n + 2, 0, L, up=g - 1, ffn_layer=L - 1)
                step(n + 3, 1, L, down=g - 1)
                with pe.Fori(2, NQUAD) as q:
                    n, g = NTILE * L + 2 * q, NQUAD * L + q
                    step(n, 0, L, up=g - 2)
                    step(n + 1, 1, L, down=g - 2)
            n, g = DEPTH * NTILE, DEPTH * NQUAD
            step(n, 0, DEPTH - 1, a=False, up=g - 2)
            step(n + 1, 1, DEPTH - 1, a=False, b=False, down=g - 2)
            ffn_centre(g - 1, 2 * n)
            ffn_var(g - 1)
            ffn_up(g - 1, DEPTH - 1, n - 1)
            ffn_down(g - 1, 2 * n)
            for k in range(UNITS):
                pe.wait_ge(ffn_done, g)
                if k >= 2:
                    pe.wait_ge(end_add, k - 1)
                for j in range(4):
                    o = (4 * k + j) * 128
                    last = nc.tensor.transpose(QKV[k % 2][:, j * 128:(j + 1) * 128], xT[:, o:o + 128], ident[:])
                last.then_inc(end_mm, 1)

        @block.scalar
        def _(act):
            fn = nc.scalar.activation
            EPS = cst[:, 0:1]
            ONE = cst[:, 1:2]
            act.wait_ge(const_made, 6)
            act.wait_ge(ld_ctx, 32)

            def exp_ln_tables():
                nc.scalar.preload_act_table_set("natural_log_exp_and_others")

            exp_ln_tables()

            def ln_act(base, meanwhile=None):
                act.wait_ge(chain, base + 3)
                fn(psq[:], st_x[:], ACT.Square).then_inc(chain, 1)
                if meanwhile is not None:
                    meanwhile()
                act.wait_ge(chain, base + 5)
                fn(ST[2][:, 0:4], ST[2][:, 0:4], ACT.Ln, bias=EPS, scale=1.0 / D).then_inc(chain, 1)
                act.wait_ge(chain, base + 6)
                fn(ST[2][:, 0:4], ST[2][:, 0:4], ACT.Exp, scale=-0.5).then_inc(chain, 1)

            with act.Fori(0, UNITS) as u:
                ln_act(GSTEPS * u, lambda: nc.scalar.copy(st_c[:], ctok[:, bass.ds(u * 512, 512)]))
                act.wait_ge(chain, GSTEPS * u + 9)
                nc.scalar.copy(st_xT[:], TP[0][:])
                nc.scalar.copy(xlT[:, bass.ds(u * 512, 512)], TP[0][:])
                nc.scalar.copy(xT[:, bass.ds(u * 512, 512)], TP[1][:])
                nc.scalar.copy(st_cT[:], TP[1][:]).then_inc(chain, 1)
            act.wait_ge(chain, SCANS + 3)
            fn(gpk[:, 2, :], gpk[:, 2, :], ACT.Exp).then_inc(chain, 1)
            act.wait_ge(chain, SCANS + 4)
            fn(gpk[:, 2, :], gpk[:, 2, :], ACT.Ln, bias=ONE).then_inc(chain, 1)
            act.wait_ge(chain, SCANS + 13)
            nc.scalar.copy(a_tok[:], TP[1][:, 0:128])
            fn(em_tok[:], TP[1][:, 128:256], ACT.Exp).then_inc(chain, 1)

            with act.Fori(0, UNITS) as u:
                base = MSTEPS * u + MIXING
                act.wait_ge(chain, base)
                nc.scalar.copy(ST[7][:, 0:1], ident[:, 0:1])
                nc.scalar.copy(st_xT[:], xlT[:, bass.ds(u * 512, 512)])
                nc.scalar.copy(st_cT[:], xT[:, bass.ds(u * 512, 512)])
                nc.scalar.copy(st_v[:, :, 0:XD], g3(ctok[:, bass.ds(u * 512, 512)], XD))
                nc.scalar.copy(st_a[:], a_tok[:, bass.ds(u * 16, 16)])
                nc.scalar.copy(st_em[:], em_tok[:, bass.ds(u * 16, 16)])
                nc.scalar.copy(st_sel[:], ident[:, bass.ds(u * 16, 16)]).then_inc(chain, 1)
                act.wait_ge(chain, base + 4)
                fn(gexp[:], gexp[:], ACT.Exp).then_inc(chain, 1)
                act.wait_ge(chain, base + 15)
                fn(psq[:], hmix[:], ACT.Square).then_inc(chain, 1)
                act.wait_ge(chain, base + 17)
                fn(ST[5][:], ST[5][:], ACT.Ln, bias=EPS, scale=1.0 / XD).then_inc(chain, 1)
                act.wait_ge(chain, base + 18)
                fn(ST[5][:], ST[5][:], ACT.Exp, scale=-0.5).then_inc(chain, 1)
                ln_act(base + 22)
                act.wait_ge(chain, base + 31)
                nc.scalar.copy(ST[7][:, 0:1], ident[:, 0:1])
                nc.scalar.copy(xT[:, bass.ds(u * 512, 512)], QKV[0][:]).then_inc(chain, 1)

            def split_hi(L, i, first=False):
                if i == 0:
                    act.wait_ge(ld_wqkv, 16 * L + 16)
                if not first:
                    act.wait_ge(qkv_mm, 6 * NTILE * L - 5 + i)
                sl = slice(WCOL[i], WCOL[i] + 512)
                nc.scalar.copy(w_hi[:, sl], w_raw[:, sl]).then_inc(whi_done, 1)

            def stationary_hi(n, par, local, early=False):
                if not early:
                    act.wait_ge(qkv_mm, 6 * n - 6)
                    act.wait_ge(xs_ready, n - 1)
                lo, hi = views(local, 128)
                half = slice(par * 128, par * 128 + 128)
                nc.scalar.copy(xs_hi[0:64, half], lo)
                nc.scalar.copy(late(xs_hi[:, half]), hi).then_inc(xs_half, 1)

            def ffn_input(f, q):
                act.wait_ge(resid, 2 * f + 2)
                lo, hi = views(q, 256)
                nc.scalar.copy(fx[0:64, :], lo)
                nc.scalar.copy(late(fx), hi).then_inc(fx_ready, 1)

            def square_qk(n, i, first):
                act.wait_ge(qkv_mm, 6 * n + i + 1)
                if not first or i >= 2:
                    act.wait_ge(ss_red, 4 * n + i - 1)
                fn(sq[:, i % 2, :], QKV[i % 2][:], ACT.Square).then_inc(qk_sq, 1)

            def evacuate_qk(n, i, first):
                if not first:
                    act.wait_ge(qn_ready, 4 * n + i - 3)
                nc.scalar.copy(raw[:, i, :], QKV[i % 2][:]).then_inc(qkv_evac, 1)

            def evacuate_v(n, i, par, early):
                act.wait_ge(qkv_mm, 6 * n + i + 1)
                if not early and i == 4:
                    act.wait_ge(pv_mm, 2 * n - 2)
                nc.scalar.copy(vt[:, par, (i - 4) * 512:(i - 3) * 512], QKV[i % 2][:]).then_inc(qkv_evac, 1)

            def evacuate_t(m, i, first):
                act.wait_ge(t_mm, 4 * m + i + 1)
                if not first:
                    act.wait_ge(s_mm, 2 * m - 1 + i // 2)
                dst = (qT, kT)[i % 2]
                nc.scalar.copy(dst[:, i // 2, :, :].rearrange("p k n -> p (k n)"), TP[i % 2][:]).then_inc(qkt_evac, 1)

            def exponent(m, g):
                act.wait_ge(s_sub, 2 * m + g + 1)
                fn(es[:, g, :], es[:, g, :], ACT.Exp).then_inc(e_exp, 1)

            def evacuate_pt(m, g, first):
                act.wait_ge(pt_mm, 2 * m + g + 1)
                if not first:
                    act.wait_ge(pv_mm, 2 * m - 1 + g)
                nc.scalar.copy(pT[:, g, :, :].rearrange("p k n -> p (k n)"), TP[g][:]).then_inc(pt_evac, 1)

            def evacuate_ot(m, first):
                act.wait_ge(pv_mm, 2 * m + 2)
                if not first:
                    act.wait_ge(wo_mm, m)
                for s in range(2):
                    last = nc.scalar.copy(oT[:, :, s * 64:s * 64 + 64], g3(OT[s][:], 64))
                last.then_inc(ot_evac, 1)

            def ffn_square(f):
                act.wait_ge(centre_mm, f + 1)
                fn(fsq[:], SC[1][:, 0:256], ACT.Square).then_inc(fsq_done, 1)

            def ffn_rstd(f):
                act.wait_ge(var_mm, f + 1)
                fn(fln[:], SC[1][:, 256:512], ACT.Ln, bias=EPS).then_inc(fln_done, 1)
                act.wait_ge(fln_done, f + 1)
                fn(frs[:], fln[:], ACT.Exp, scale=-0.5).then_inc(frs_done, 1)

            def ffn_gelu(f, L):
                act.wait_ge(vec_ready, L + 1)
                for c in range(3):
                    if c != 1:
                        act.wait_ge(w1_mm, 3 * f + 1 + c // 2)
                    src = OT[0][:, c * 256:(c + 1) * 256] if c < 2 else OT[1][0:FCH[2], 0:256]
                    fn(fh[0:FCH[c], c, :], src, ACT.Gelu, bias=vecs[0:FCH[c], 6 + c:7 + c]).then_inc(gelu_done, 1)

            def step(n, par, L, a=True, b=True, c=True, up=None, first=False, b_first=False, c_first=False,
                     early=False, split=None, nxt=None, up_q=None):
                m, t = n - 1, n - 2

                def hi(*chunks):
                    if split is not None:
                        for i in chunks:
                            split_hi(split, i, first)

                hi(0, 1)
                if a:
                    square_qk(n, 0, first)
                if c:
                    evacuate_pt(t, 0, c_first)
                hi(2)
                if a:
                    evacuate_qk(n, 0, first)
                    square_qk(n, 1, first)
                    evacuate_qk(n, 1, first)
                hi(3)
                if b:
                    evacuate_t(m, 0, b_first)
                if a:
                    square_qk(n, 2, first)
                if b:
                    evacuate_t(m, 1, b_first)
                if a:
                    square_qk(n, 3, first)
                if up is not None:
                    ffn_input(up, up_q)
                hi(4)
                if a:
                    evacuate_qk(n, 2, first)
                hi(5)
                if up is not None:
                    ffn_square(up)
                if c:
                    evacuate_pt(t, 1, c_first)
                if a:
                    evacuate_qk(n, 3, first)
                if nxt is not None:
                    stationary_hi(n + 1, 1 - par, nxt, early=first)
                if up is not None:
                    ffn_rstd(up)
                if par == 1:
                    exp_ln_tables()
                if b:
                    evacuate_t(m, 2, b_first)
                    exponent(m, 0)
                    evacuate_t(m, 3, b_first)
                if c:
                    evacuate_ot(t, c_first)
                if a:
                    evacuate_v(n, 4, par, early)
                    evacuate_v(n, 5, par, early)
                if b:
                    exponent(m, 1)
                if up is not None:
                    ffn_gelu(up, L)

            act.wait_ge(small_ready, 1)
            stationary_hi(0, 0, 0, early=True)
            step(0, 0, 0, b=False, c=False, first=True, early=True, split=0, nxt=1)
            step(1, 1, 0, c=False, b_first=True, early=True, nxt=2)
            step(2, 0, 0, c_first=True, nxt=3)
            step(3, 1, 0, nxt=4)
            with act.Fori(2, NQUAD) as q:
                step(2 * q, 0, 0, up=q - 2, up_q=q - 2, nxt=2 * q + 1)
                step(2 * q + 1, 1, 0, nxt=(2 * q + 2) % NTILE)
            with act.Fori(1, DEPTH) as L:
                n, g = NTILE * L, NQUAD * L
                step(n, 0, L - 1, up=g - 2, up_q=NQUAD - 2, split=L, nxt=1)
                step(n + 1, 1, L - 1, nxt=2)
                step(n + 2, 0, L - 1, up=g - 1, up_q=NQUAD - 1, nxt=3)
                step(n + 3, 1, L, nxt=4)
                with act.Fori(2, NQUAD) as q:
                    n, g = NTILE * L + 2 * q, NQUAD * L + q
                    step(n, 0, L, up=g - 2, up_q=q - 2, nxt=2 * q + 1)
                    step(n + 1, 1, L, nxt=(2 * q + 2) % NTILE)
            n, g = DEPTH * NTILE, DEPTH * NQUAD
            step(n, 0, DEPTH - 1, a=False, up=g - 2, up_q=NQUAD - 2)
            step(n + 1, 1, DEPTH - 1, a=False, b=False)
            ffn_input(g - 1, NQUAD - 1)
            ffn_square(g - 1)
            ffn_rstd(g - 1)
            ffn_gelu(g - 1, DEPTH - 1)

        @block.vector
        def _(dve):
            v = nc.vector
            tt, ts, stt = v.tensor_tensor, v.tensor_scalar, v.scalar_tensor_tensor

            v.memset(xs_hi[:].bitcast(F32), 0.0)
            v.memset(xs_lo[:].bitcast(F32), 0.0)
            v.memset(fx[:], 0.0)
            v.memset(gro[:, 7, :], 0.0).then_inc(const_made, 1)
            dve.wait_ge(ld_small, 16 * 13)
            dve.wait_ge(const_made, 6)
            v.tensor_copy(band[:], band_f[:])
            v.tensor_copy(identb[:], ident[:])
            tt(centring[:], ident[:], ones[:], ALU.subtract)
            v.tensor_copy(vecs[:], vecs_all[:, 0:NVEC]).then_inc(vec_ready, 1)
            tt(tabs[:], rot_base[:], scales[:, 0, :, :].rearrange("p a b -> p (a b)"), ALU.mult).then_inc(tabs_ready, 1)
            tt(wg_kv[:], wg[:, 1, :], wg[:, 2, :], ALU.add).then_inc(small_ready, 1)

            def ln_dve(base, xs):
                dve.wait_ge(chain, base)
                v.memset(ST[8][:, 0:1], 0.0)
                v.tensor_reduce(ST[0][:, 0:4], g3(xs, D), AX_X, ALU.add).then_inc(chain, 1)
                dve.wait_ge(chain, base + 1)
                ts(ST[1][:, 0:4], ST[0][:, 0:4], 1.0 / D, None, ALU.mult).then_inc(chain, 1)
                dve.wait_ge(chain, base + 2)
                tt(g3(st_x[:], D), g3(xs, D), bc(ST[1][:, 0:4], D), ALU.subtract).then_inc(chain, 1)
                dve.wait_ge(chain, base + 4)
                v.tensor_reduce(ST[2][:, 0:4], g3(psq[:], D), AX_X, ALU.add).then_inc(chain, 1)
                dve.wait_ge(chain, base + 7)
                tt(g3(st_x[:], D), g3(st_x[:], D), bc(ST[2][:, 0:4], D), ALU.mult).then_inc(chain, 1)

            dve.wait_ge(ld_x, 32)
            with dve.Fori(0, UNITS) as u:
                ln_dve(GSTEPS * u, xtok[:, bass.ds(u * 512, 512)])
                dve.wait_ge(chain, GSTEPS * u + 11)
                ts(gtok[:, bass.ds(u * 4, 4), :], g3(SC[0][:, 0:32], 8), 1.0, None, ALU.mult).then_inc(chain, 1)
            dve.wait_ge(chain, SCANS)
            tt(g3(gpk[:, 0, :], XH), gtok[:, :, 0:4], mid(bg[:, 0:4], NPAIR), ALU.add)
            tt(g3(gpk[:, 1, :], XH), gtok[:, :, 4:8], mid(bg[:, 4:8], NPAIR), ALU.add).then_inc(chain, 1)
            dve.wait_ge(chain, SCANS + 1)
            ts(gpk[:, 2, :], gpk[:, 1, :], -1.0, None, ALU.mult).then_inc(chain, 1)
            dve.wait_ge(chain, SCANS + 2)
            tt(gpk[:, 2, :], gpk[:, 2, :], gpk[:, 1, :], ALU.min).then_inc(chain, 1)
            dve.wait_ge(chain, SCANS + 5)
            stt(gpk[:, 3, :], gpk[:, 1, :], 0.0, gpk[:, 2, :], ALU.min, ALU.subtract).then_inc(chain, 1)
            dve.wait_ge(chain, SCANS + 7)
            v.tensor_copy(gro[:, 0:2, :], g3(TP[0][:, 0:256], 128)).then_inc(chain, 1)
            dve.wait_ge(chain, SCANS + 8)
            for sl in HALVES:
                last = v.tensor_tensor_scan(gro[:, 2, sl], gro[:, 0, sl], gro[:, 7, sl], 0.0, ALU.add, ALU.add)
            last.then_inc(chain, 1)
            dve.wait_ge(chain, SCANS + 9)
            tt(gro[:, 3, :], gro[:, 1, :], gro[:, 2, :], ALU.subtract).then_inc(chain, 1)
            dve.wait_ge(chain, SCANS + 10)
            for sl in HALVES:
                last = v.tensor_tensor_scan(gro[:, 4, sl], gro[:, 3, sl], gro[:, 7, sl], -3.0e38, ALU.max, ALU.add)
            last.then_inc(chain, 1)
            dve.wait_ge(chain, SCANS + 11)
            ts(gro[:, 5, :], gro[:, 4, :], -1.0, None, ALU.mult)
            stt(gro[:, 6, :], gro[:, 2, :], -1.0, gro[:, 4, :], ALU.mult, ALU.subtract).then_inc(chain, 1)

            with dve.Fori(0, UNITS) as u:
                base = MSTEPS * u + MIXING
                dve.wait_ge(chain, base + 2)
                for k in range(2):
                    last = tt(g3(gexp[:, k * 512:(k + 1) * 512], S), g3(TP[k][:], S), bc(st_a[:, k * 8:(k + 1) * 8], S), ALU.add)
                last.then_inc(chain, 1)
                dve.wait_ge(chain, base + 3)
                stt(g3(gexp[:], S), g3(gexp[:], S), 0.0, mid(causal[:], 16), ALU.min, ALU.add).then_inc(chain, 1)
                dve.wait_ge(chain, base + 5)
                for h in range(XH):
                    e = gexp[:].rearrange("p (k h s) -> p k h s", k=4, h=XH)[:, :, h, :]
                    last = stt(e, g3(SCX[h][:, 0:256], S), float(XD) ** -0.5, e, ALU.mult, ALU.mult)
                last.then_inc(chain, 1)
                dve.wait_ge(chain, base + 7)
                for k in range(2):
                    last = ts(ST[3][:, k * 8:(k + 1) * 8], g3(OT[k][:, 0:264], 33)[:, :, 32], -1.0, None, ALU.mult)
                last.then_inc(chain, 1)
                dve.wait_ge(chain, base + 8)
                for k in range(2):
                    last = tt(ST[3][:, k * 8:(k + 1) * 8], g3(OT[k][:, 0:264], 33)[:, :, 32], ST[3][:, k * 8:(k + 1) * 8], ALU.max)
                last.then_inc(chain, 1)
                dve.wait_ge(chain, base + 9)
                tt(ST[3], ST[3], st_em[:], ALU.max).then_inc(chain, 1)
                dve.wait_ge(chain, base + 10)
                ts(ST[3], ST[3], 1e-6, None, ALU.add).then_inc(chain, 1)
                dve.wait_ge(chain, base + 11)
                v.reciprocal(ST[3], ST[3]).then_inc(chain, 1)
                dve.wait_ge(chain, base + 12)
                for k in range(2):
                    last = tt(g3(hmix[:, k * 256:(k + 1) * 256], XD), g3(OT[k][:, 0:264], 33)[:, :, 0:32],
                              bc(ST[3][:, k * 8:(k + 1) * 8], XD), ALU.mult)
                last.then_inc(chain, 1)
                dve.wait_ge(chain, base + 13)
                v.tensor_reduce(ST[4], g3(hmix[:], XD), AX_X, ALU.add).then_inc(chain, 1)
                dve.wait_ge(chain, base + 14)
                ts(ST[4], ST[4], 1.0 / XD, None, ALU.mult).then_inc(mixed, 1)
                dve.wait_ge(mixed, u + 1)
                tt(g3(hmix[:], XD), g3(hmix[:], XD), bc(ST[4], XD), ALU.subtract).then_inc(chain, 1)
                dve.wait_ge(chain, base + 16)
                v.tensor_reduce(ST[5], g3(psq[:], XD), AX_X, ALU.add).then_inc(chain, 1)
                dve.wait_ge(chain, base + 19)
                tt(g3(hmix[:], XD), g3(hmix[:], XD), bc(ST[5], XD), ALU.mult).then_inc(chain, 1)
                dve.wait_ge(chain, base + 20)
                tt(g3(hmix[:], D), g3(hmix[:], D), mid(onorm[:], 4), ALU.mult).then_inc(chain, 1)
                x1 = xtok[:, bass.ds(u * 512, 512)]
                dve.wait_ge(chain, base + 21)
                tt(x1, x1, hmix[:], ALU.add).then_inc(chain, 1)
                ln_dve(base + 22, x1)

            def split_lo(L, *chunks):
                for i in chunks:
                    dve.wait_ge(whi_done, 6 * L + i + 1)
                    sl = slice(WCOL[i], WCOL[i] + 512)
                    tt(w_lo[:, sl], w_raw[:, sl], w_hi[:, sl].bitcast(F32), ALU.subtract).then_inc(wlo_done, 1)

            def stationary_lo(n, par, local):
                dve.wait_ge(xs_half, n + 1)
                lo, hi = views(local, 128)
                half = slice(par * 128, par * 128 + 128)
                tt(xs_lo[0:64, half], lo, xs_hi[0:64, half].bitcast(F32), ALU.subtract)
                tt(late(xs_lo[:, half]), hi, late(xs_hi[:, half].bitcast(F32)), ALU.subtract).then_inc(xs_ready, 1)

            def sum_squares(n, i, first):
                dve.wait_ge(qk_sq, 4 * n + i + 1)
                if i == 0 and not first:
                    dve.wait_ge(newton, 12 * n)
                v.tensor_reduce(ss[:, 8 * i:8 * i + 8], g3(sq[:, i % 2, :], DH), AX_X, ALU.add).then_inc(ss_red, 1)

            def norm_op(n, k, first):
                y, a, b = nwt[:, 0, :], nwt[:, 1, :], nwt[:, 2, :]
                if k == 0:
                    dve.wait_ge(ss_red, 4 * n + 4)
                    op = ts(ss[:], ss[:], 1e-24, None, ALU.max)
                else:
                    dve.wait_ge(newton, 12 * n + k)
                    if k == 1:
                        op = ts(seed[:], ss[:].bitcast(I32), 1, None, ALU.logical_shift_right)
                    elif k == 2:
                        op = ts(y.bitcast(I32), seed[:], -1.0, MAGIC, ALU.mult, ALU.add)
                    elif k % 3 == 0:
                        op = tt(a, y, y, ALU.mult)
                    elif k % 3 == 1:
                        op = stt(b, a, -0.5, ss[:], ALU.mult, ALU.mult)
                    else:
                        op = stt(rinv[:] if k == 11 else y, b, 1.5, y, ALU.add, ALU.mult)
                op.then_inc(newton, 1)

            def unit_qk(n, i, first):
                if i == 0:
                    dve.wait_ge(newton, 12 * n + 12)
                    dve.wait_ge(qkv_evac, 6 * n + 4)
                if i == 0 and not first:
                    dve.wait_ge(t_done, 4 * n)
                tt(g3(qn[:, i, :], DH), g3(raw[:, i, :], DH), bc(rinv[:, 8 * i:8 * i + 8], DH), ALU.mult).then_inc(qn_ready, 1)

            def sine_qk(n, i, first):
                dve.wait_ge(qn_ready, 4 * n + i + 1)
                if i == 0 and not first:
                    dve.wait_ge(rot_ready, 4 * n)
                o = (2 * (i % 2) + 1) * DH
                swapped = qn[:, i, :].rearrange("p (h t d) -> p h t d", t=2, d=32)[:, :, ::-1, :]
                tab = tabs[:, o:o + DH].rearrange("p (t d) -> p t d", t=2).unsqueeze(1).broadcast_to([128, 8, 2, 32])
                tt(ur[:, i, :].rearrange("p (h t d) -> p h t d", t=2, d=32), swapped, tab, ALU.mult).then_inc(u_ready, 1)

            def row_max(m, g):
                dve.wait_ge(s_mm, 2 * m + g + 1)
                v.tensor_reduce(smax[:, g, :], g3(SC[g][:], S), AX_X, ALU.max).then_inc(s_max, 1)

            def row_shift(m, g, first):
                dve.wait_ge(s_max, 2 * m + g + 1)
                if not first:
                    dve.wait_ge(pt_mm, 2 * m + g - 1)
                tt(g3(es[:, g, :], S), g3(SC[g][:], S), bc(smax[:, g, :], S), ALU.subtract).then_inc(s_sub, 1)

            def row_sum(m, g):
                dve.wait_ge(e_exp, 2 * m + g + 1)
                v.tensor_reduce(ssum[:, g, :], g3(es[:, g, :], S), AX_X, ALU.add).then_inc(e_sum, 1)

            def row_inverse(m, g, first):
                dve.wait_ge(e_sum, 2 * m + g + 1)
                if not first:
                    dve.wait_ge(pn_ready, 2 * m + g - 1)
                v.reciprocal(sinv[:, g, :], ssum[:, g, :]).then_inc(e_inv, 1)

            def residual(w, local):
                dve.wait_ge(wo_mm, w + 1)
                cols = bass.ds(local * 128, 128) if not isinstance(local, int) else slice(local * 128, local * 128 + 128)
                tt(xT[:, cols], OT[0][:, 0:128], xT[:, cols], ALU.add).then_inc(resid, 1)

            def ffn_scale(f):
                dve.wait_ge(frs_done, f + 1)
                tt(fxn[:], SC[1][:, 0:256], frs[:], ALU.mult).then_inc(fn_step, 1)

            def ffn_gain(f):
                dve.wait_ge(fn_step, f + 1)
                ts(fxn[:], fxn[:], vecs[:, 0:1], vecs[:, 1:2], ALU.mult, ALU.add).then_inc(fxn_ready, 1)

            def ffn_hidden(f):
                for c in (0, 1, 2):
                    dve.wait_ge(gelu_done, 3 * f + c + 1)
                    if c == 0:
                        dve.wait_ge(w1_mm, 3 * f + 3)
                    rows = slice(0, FCH[c])
                    src = TP[1][rows, c * 256:(c + 1) * 256] if c < 2 else OT[1][rows, 256:512]
                    stt(fh[rows, c, :], src, vecs[rows, 3 + c:4 + c], fh[rows, c, :], ALU.add, ALU.mult).then_inc(h_ready, 1)

            def ffn_residual(f, q):
                dve.wait_ge(w2_mm, f + 1)
                cols = bass.ds(q * 256, 256) if not isinstance(q, int) else slice(q * 256, q * 256 + 256)
                stt(xT[:, cols], SC[0][:, 0:256], vecs[:, 2:3], xT[:, cols], ALU.add, ALU.add).then_inc(ffn_done, 1)

            def new_tables(L, n):
                dve.wait_ge(t_done, 4 * n)
                tt(tabs[:], rot_base[:], scales[:, bass.ds(L, 1), :, :].rearrange("p o a b -> p (o a b)"),
                   ALU.mult).then_inc(tabs_ready, 1)
                dve.wait_ge(tabs_ready, L + 1)

            def step(n, par, a=True, b=True, w=None, up=None, down=None, down_q=None, nxt=None, first=False, b_first=False,
                     tables=None):
                m = n - 1

                def norm_ops(*ops):
                    if a:
                        for k in ops:
                            norm_op(n, k, first)

                if tables is not None:
                    split_lo(tables, 0, 1)
                if down is not None:
                    ffn_hidden(down)
                if a:
                    sum_squares(n, 0, first)
                if tables is not None:
                    split_lo(tables, 2)
                if a:
                    sum_squares(n, 1, first)
                if tables is not None:
                    split_lo(tables, 3)
                if down is not None:
                    ffn_residual(down, down_q)
                if a:
                    sum_squares(n, 2, first)
                if tables is not None:
                    split_lo(tables, 4)
                if a:
                    sum_squares(n, 3, first)
                if tables is not None:
                    split_lo(tables, 5)
                norm_ops(0, 1, 2, 3, 4, 5, 6, 7, 8)
                if b:
                    row_max(m, 0)
                norm_ops(9)
                if b:
                    row_shift(m, 0, b_first)
                norm_ops(10, 11)
                if tables is not None and not first:
                    new_tables(tables, n)
                if a:
                    unit_qk(n, 0, first)
                    unit_qk(n, 1, first)
                if up is not None:
                    ffn_scale(up)
                if b:
                    row_sum(m, 0)
                if up is not None:
                    ffn_gain(up)
                if a:
                    sine_qk(n, 0, first)
                if b:
                    row_inverse(m, 0, b_first)
                if nxt is not None:
                    stationary_lo(n + 1, 1 - par, nxt)
                if b:
                    row_max(m, 1)
                if b:
                    row_shift(m, 1, b_first)
                if w is not None:
                    residual(n - 2, w)
                if a:
                    sine_qk(n, 1, first)
                    unit_qk(n, 2, first)
                if b:
                    row_sum(m, 1)
                if a:
                    unit_qk(n, 3, first)
                if b:
                    row_inverse(m, 1, b_first)
                if a:
                    sine_qk(n, 2, first)
                    sine_qk(n, 3, first)

            dve.wait_ge(chain, MIXING + UNITS * MSTEPS)
            dve.wait_ge(tabs_ready, 1)
            stationary_lo(0, 0, 0)
            step(0, 0, b=False, first=True, tables=0, nxt=1)
            step(1, 1, b_first=True, nxt=2)
            step(2, 0, w=0, nxt=3)
            step(3, 1, w=1, nxt=4)
            with dve.Fori(2, NQUAD) as q:
                step(2 * q, 0, w=2 * q - 2, up=q - 2, nxt=2 * q + 1)
                step(2 * q + 1, 1, w=2 * q - 1, down=q - 2, down_q=q - 2, nxt=(2 * q + 2) % NTILE)
            with dve.Fori(1, DEPTH) as L:
                n, g = NTILE * L, NQUAD * L
                step(n, 0, w=NTILE - 2, up=g - 2, tables=L, nxt=1)
                step(n + 1, 1, w=NTILE - 1, down=g - 2, down_q=NQUAD - 2, nxt=2)
                step(n + 2, 0, w=0, up=g - 1, nxt=3)
                step(n + 3, 1, w=1, down=g - 1, down_q=NQUAD - 1, nxt=4)
                dve.wait_ge(ffn_done, g)
                ts(vecs[:], vecs_all[:, bass.ds(L * NVEC, NVEC)], 1.0, None, ALU.mult).then_inc(vec_ready, 1)
                with dve.Fori(2, NQUAD) as q:
                    n, g = NTILE * L + 2 * q, NQUAD * L + q
                    step(n, 0, w=2 * q - 2, up=g - 2, nxt=2 * q + 1)
                    step(n + 1, 1, w=2 * q - 1, down=g - 2, down_q=q - 2, nxt=(2 * q + 2) % NTILE)
            n, g = DEPTH * NTILE, DEPTH * NQUAD
            step(n, 0, a=False, w=NTILE - 2, up=g - 2)
            step(n + 1, 1, a=False, b=False, w=NTILE - 1, down=g - 2, down_q=NQUAD - 2)
            ffn_scale(g - 1)
            ffn_gain(g - 1)
            ffn_hidden(g - 1)
            ffn_residual(g - 1, NQUAD - 1)
            for k in range(UNITS):
                dve.wait_ge(end_mm, k + 1)
                sl = slice(k * 512, (k + 1) * 512)
                tt(xtok[:, sl], QKV[k % 2][:], xtok[:, sl], ALU.add).then_inc(end_add, 1)


_ARRAYS = ["x", "ctx", "wgate", "bgate", "outnorm", "wqkv", "qscale", "kscale", "wo", "w1", "w2", "vec", "rot", "band", "causal"]


def kernel(**inputs):
    import numpy as _np
    import concourse.bacc as _bacc
    from concourse import mybir as _mybir
    from concourse.bass_utils import run_bass_kernel_spmd as _run

    i = {k: _np.asarray(v) for k, v in inputs.items()}
    f32 = _np.float32
    a = {"x": i["x"].reshape(NTOK, D), "ctx": i["ctx_1024"].reshape(NTOK, D)}
    a["wgate"] = _np.concatenate([i["L0_xattn_igate_kernel"], i["L0_xattn_fgate_kernel"]], 1)
    a["bgate"] = _np.concatenate([i["L0_xattn_igate_bias"], i["L0_xattn_fgate_bias"]])
    a["outnorm"] = i["L0_xattn_outnorm_scale"]
    a["wqkv"] = i["L0_ffn_Wqkv"]
    a["qscale"], a["kscale"] = i["L0_ffn_q_scale"], i["L0_ffn_k_scale"]
    a["wo"] = i["L0_ffn_Wo"].reshape(DEPTH, 8, 128, D).transpose(0, 2, 1, 3)
    a["w1"] = i["L0_ffn_W1"]
    w2 = _np.zeros((DEPTH, 384, D), f32)
    w2[:, :FF] = i["L0_ffn_W2"]
    a["w2"] = w2.reshape(DEPTH, 3, 128, D).transpose(0, 2, 1, 3)
    vec = _np.zeros((DEPTH, NVEC, 128), f32)
    vec[:, 0], vec[:, 1], vec[:, 2] = i["L0_ffn_ln_g"], i["L0_ffn_ln_b"], i["L0_ffn_b2"]
    for part in range(2):
        for c in range(3):
            vec[:, 3 + 3 * part + c, :FCH[c]] = i["L0_ffn_b1"][:, part * FF + c * 128:part * FF + c * 128 + FCH[c]]
    a["vec"] = vec.transpose(2, 0, 1).reshape(128, DEPTH * NVEC)
    a["rot"], a["band"], a["causal"] = constants()

    nc = _bacc.Bacc("TRN2", target_bir_lowering=False, num_devices=1)
    arrays, args = {}, []
    for name in _ARRAYS:
        arr = _np.ascontiguousarray(a[name])
        arrays[f"in_{name}"] = arr
        args.append(nc.dram_tensor(f"in_{name}", arr.shape, _mybir.dt.from_np(arr.dtype), kind="ExternalInput").ap())
    args.append(nc.dram_tensor("out_x", (NTOK, D), _mybir.dt.float32, kind="ExternalOutput").ap())
    transformer_program(nc, *args)
    r = _run(nc, [arrays], core_ids=[0])
    return r.results[0]["out_x"].reshape(NSEQ, S, D)
```

```python
from contextlib import ExitStack

import numpy as np

import concourse.bass as bass
from concourse import mybir

F32 = mybir.dt.float32
F32R = mybir.dt.float32r
BF16 = mybir.dt.bfloat16
I32 = mybir.dt.int32
ALU = mybir.AluOpType
ACT = mybir.ActivationFunctionType
AX_X = mybir.AxisListType.X

NSEQ, S, D = 64, 64, 128
NPAIR = NSEQ // 2
TOK = 2 * S
NTOK = NSEQ * S
NTILE = NPAIR
NQUAD = NTILE // 2
DEPTH, HEADS, DH = 6, 16, 64
INNER = HEADS * DH
XH = 4
XD = D // XH
FF = 341
FCH = [128, 128, FF - 256]
WINDOW = 32
NVEC = 9
MASKED = -1.0e30
MAGIC = float(0x5F3759DF)
WCOL = [0, INNER, 512, INNER + 512, 2 * INNER, 2 * INNER + 512]
UNITS = 8
LSTEPS, GSTEPS, ASTEPS, BSTEPS, BNORM = 8, 4, 6, 23, 15
SSTEPS = 14


def constants():
    half = np.arange(0, DH, 2, dtype=np.float64)
    inv_freq = 1.0 / 10000.0 ** (half / DH)
    t = np.arange(S, dtype=np.float64)
    freqs = np.concatenate([t[:, None] * inv_freq[None]] * 2, -1)
    base = (half + 0.4 * DH) / (1.4 * DH)
    scale = np.concatenate([base[None] ** ((t - S // 2) / (WINDOW // 2))[:, None]] * 2, -1)
    sign = np.where(np.arange(DH) < DH // 2, -1.0, 1.0)[None]
    rot = np.stack([8 * np.cos(freqs) * scale, 8 * sign * np.sin(freqs) * scale,
                    np.cos(freqs) / scale, sign * np.sin(freqs) / scale], 1)
    rot = np.tile(rot, (2, 1, 1)).astype(np.float32).reshape(TOK, 4 * DH)
    i, j = np.arange(S)[:, None], np.arange(S)[None]
    band = np.where((j <= i) & (j >= i - WINDOW), 0.0, MASKED).astype(np.float32)
    band = np.tile(band, (2, 8))
    causal = np.tile(np.where(i <= j, 0.0, MASKED).astype(np.float32), (2, 1))
    return rot, band, causal


def transformer_program(nc, x, ctx_in, wgate, bgate, outnorm, wqkv, qscale, kscale, wo, w1, w2, vec,
                        rot_c, band_c, causal_c, out):
    with ExitStack() as stack:
        def sb(name, shape, dt=F32):
            return stack.enter_context(nc.sbuf_tensor(name, shape, dt))

        def bank(name):
            return stack.enter_context(nc.psum_tensor(name, [128, 512], F32))

        def sem(name):
            return stack.enter_context(nc.semaphore(name))

        QKV = [bank("qkv0"), bank("qkv1")]
        TP = [bank("tp0"), bank("tp1")]
        SC = [bank("sc0"), bank("sc1")]
        OT = [bank("ot0"), bank("ot1")]

        SCX = [SC[0], SC[1], QKV[0], QKV[1]]

        xtok = sb("xtok", [128, NTOK])
        xT = sb("xT", [128, NTOK])
        ident = sb("ident", [128, 128])
        identb = sb("identb", [128, 128], BF16)
        cst = sb("cst", [128, 4])
        rot_base = sb("rot_base", [128, 4 * DH])
        scales = sb("scales", [128, DEPTH, 4, DH])
        tabs = sb("tabs", [128, 4 * DH])
        band_f = sb("band_f", [128, 512])
        band = sb("band", [128, 512], BF16)
        ones = sb("ones", [128, 128])
        centring = sb("centring", [128, 128])
        vecs_all = sb("vecs_all", [128, DEPTH * NVEC])
        vecs = sb("vecs", [128, NVEC])
        w_raw = sb("w_raw", [128, 3 * INNER])
        w_hi = sb("w_hi", [128, 3 * INNER], F32R)
        w_lo = sb("w_lo", [128, 3 * INNER], F32R)
        wo_s = sb("wo_s", [128, 8, 128])
        w1_s = sb("w1_s", [128, 2 * FF])
        w2_s = sb("w2_s", [128, 3, 128])
        arena = sb("arena", [128, 4 * 2048])
        raw = arena[:, 0:2048].rearrange("p (c n) -> p c n", c=4)
        qn = arena[:, 2048:4096].rearrange("p (c n) -> p c n", c=4)
        tr = arena[:, 4096:6144].rearrange("p (c n) -> p c n", c=4)
        ur = arena[:, 6144:8192].rearrange("p (c n) -> p c n", c=4)
        xs_hi = sb("xs_hi", [128, 256], F32R)
        xs_lo = sb("xs_lo", [128, 256], F32R)
        sq = sb("sq", [128, 2, 512])
        ss = sb("ss", [128, 32])
        seed = sb("seed", [128, 32], I32)
        nwt = sb("nwt", [128, 3, 32])
        rinv = sb("rinv", [128, 32])
        qT = sb("qT", [128, 2, 4, 128])
        kT = sb("kT", [128, 2, 4, 128])
        vt = sb("vt", [128, 2, INNER])
        es = sb("es", [128, 2, 512])
        smax = sb("smax", [128, 2, 8])
        ssum = sb("ssum", [128, 2, 8])
        sinv = sb("sinv", [128, 2, 8])
        pT = sb("pT", [128, 2, 4, 128])
        oT = sb("oT", [128, 8, 128])
        fx = sb("fx", [128, 256])
        fsq = sb("fsq", [128, 256])
        fln = sb("fln", [128, 256])
        frs = sb("frs", [128, 256])
        fxn = sb("fxn", [128, 256])
        fh = sb("fh", [128, 3, 256])
        ctok = arena[:, 0:4096]
        xlT = arena[:, 4096:8192]
        wg = sb("wg", [128, 3, 8])
        wg_kv = sb("wg_kv", [128, 8])
        bg = sb("bg", [128, 8])
        onorm = sb("onorm", [128, D])
        causal = sb("causal", [128, S])
        gtok = sb("gtok", [128, NPAIR, 8])
        gpk = sb("gpk", [128, 8, 128])
        gro = sb("gro", [128, 8, 128])
        a_tok = sb("a_tok", [128, 128])
        em_tok = sb("em_tok", [128, 128])
        st_x = sb("st_x", [128, 512])
        st_c = sb("st_c", [128, 512])
        st_v = sb("st_v", [128, 16, 33])
        st_sel = sb("st_sel", [128, 16])
        st_em = sb("st_em", [128, 16])
        st_a = sb("st_a", [128, 16])
        st_xT = sb("st_xT", [128, 512])
        st_cT = sb("st_cT", [128, 512])
        gexp = sb("gexp", [128, 1024])
        hmix = sb("hmix", [128, 512])
        psq = sb("psq", [128, 512])
        psm = sb("psm", [128, 12, 16])

        ld_x, ld_ctx, ld_small = sem("ld_x"), sem("ld_ctx"), sem("ld_small")
        ld_wqkv, ld_wo, ld_ffn = sem("ld_wqkv"), sem("ld_wo"), sem("ld_ffn")
        stored = sem("stored")
        const_made, const_init = sem("const_made"), sem("const_init")
        small_ready = sem("small_ready")
        norm_step, gate_step, scan_step, first_step, second_step = map(
            sem, ("norm_step", "gate_step", "scan_step", "first_step", "second_step"))
        ctx_staged, kept, scored, staged, mixed = map(sem, ("ctx_staged", "kept", "scored", "staged", "mixed"))
        mixed_mm, x1_mm, x1_kept = sem("mixed_mm"), sem("x1_mm"), sem("x1_kept")
        qkv_mm, t_mm, s_mm, pt_mm, pv_mm, wo_mm = map(sem, ("qkv_mm", "t_mm", "s_mm", "pt_mm", "pv_mm", "wo_mm"))
        centre_mm, var_mm, w1_mm, w2_mm = map(sem, ("centre_mm", "var_mm", "w1_mm", "w2_mm"))
        qk_sq, qkv_evac, qkt_evac, e_exp, pt_evac, ot_evac = map(
            sem, ("qk_sq", "qkv_evac", "qkt_evac", "e_exp", "pt_evac", "ot_evac"))
        fsq_done, fln_done, frs_done, gelu_done, whi_done = map(
            sem, ("fsq_done", "fln_done", "frs_done", "gelu_done", "whi_done"))
        ss_red, newton, qn_ready, u_ready, s_max, s_sub, e_sum, e_inv = map(
            sem, ("ss_red", "newton", "qn_ready", "u_ready", "s_max", "s_sub", "e_sum", "e_inv"))
        resid, xs_half, xs_ready, fx_ready, fn_step, fxn_ready, h_ready, ffn_done = map(
            sem, ("resid", "xs_half", "xs_ready", "fx_ready", "fn_step", "fxn_ready", "h_ready", "ffn_done"))
        wlo_done, tabs_ready, vec_ready = sem("wlo_done"), sem("tabs_ready"), sem("vec_ready")
        t_done, rot_ready, pn_ready = sem("t_done"), sem("rot_ready"), sem("pn_ready")
        end_mm, end_add = sem("end_mm"), sem("end_add")

        ST = [psm[:, k, :] for k in range(12)]
        HALVES = (slice(0, 64), slice(64, 128))

        def bc(ap, n):
            return ap.unsqueeze(2).broadcast_to([ap.shape[0], ap.shape[1], n])

        def mid(ap, n):
            return ap.unsqueeze(1).broadcast_to([ap.shape[0], n, ap.shape[1]])

        def g3(ap, n):
            return ap.rearrange("p (a n) -> p a n", n=n)

        def views(k, width):
            cols = bass.ds(k * width, width) if not isinstance(k, int) else slice(k * width, k * width + width)
            return xT[0:64, cols], g3(xT[64:128, cols], S)[:, :, 0:S - 1]

        def late(t):
            return g3(t[64:128, :], S)[:, :, 1:S]

        block = stack.enter_context(nc.Block())

        @block.sync
        def _(sp):
            xv = x.rearrange("(p t) d -> t p d", t=TOK)
            cv = ctx_in.rearrange("(p t) d -> t p d", t=TOK)
            for k in range(2):
                sl = slice(k * 2048, (k + 1) * 2048)
                sp.dma_start(g3(xtok[:, sl], D), xv[:, k * 16:(k + 1) * 16, :]).then_inc(ld_x, 16)
                sp.dma_start(g3(ctok[:, sl], D), cv[:, k * 16:(k + 1) * 16, :]).then_inc(ld_ctx, 16)
            sp.dma_start(wg[:], wgate.rearrange("(k p) g -> p k g", p=128)).then_inc(ld_small, 16)
            sp.dma_start(bg[:], bgate.partition_broadcast(128)).then_inc(ld_small, 16)
            sp.dma_start(onorm[:], outnorm.partition_broadcast(128)).then_inc(ld_small, 16)
            sp.dma_start(causal[:], causal_c).then_inc(ld_small, 16)
            sp.dma_start(rot_base[:], rot_c).then_inc(ld_small, 16)
            sp.dma_start(band_f[:], band_c).then_inc(ld_small, 16)
            sp.dma_start(vecs_all[:], vec).then_inc(ld_small, 16)
            for k, src in enumerate((qscale, kscale)):
                rep = src.partition_broadcast(128)
                sp.dma_start(scales[:, :, 2 * k, :], rep).then_inc(ld_small, 16)
                sp.dma_start(scales[:, :, 2 * k + 1, 0:32], rep[:, :, 32:64]).then_inc(ld_small, 16)
                sp.dma_start(scales[:, :, 2 * k + 1, 32:64], rep[:, :, 0:32]).then_inc(ld_small, 16)
            sp.dma_start(w_raw[:], wqkv[0]).then_inc(ld_wqkv, 16)
            sp.dma_start(wo_s[:], wo[0]).then_inc(ld_wo, 16)
            sp.dma_start(w1_s[:], w1[0]).then_inc(ld_ffn, 16)
            sp.dma_start(w2_s[:], w2[0]).then_inc(ld_ffn, 16)
            with sp.Fori(0, DEPTH - 1) as L:
                sp.wait_ge(whi_done, 6 * L + 6)
                sp.wait_ge(wlo_done, 6 * L + 6)
                sp.dma_start(w_raw[:], wqkv[bass.ds(L + 1, 1)].rearrange("o p n -> (o p) n")).then_inc(ld_wqkv, 16)
                sp.wait_ge(wo_mm, NTILE * L + NTILE)
                sp.dma_start(wo_s[:], wo[bass.ds(L + 1, 1)].rearrange("o p k n -> (o p) k n")).then_inc(ld_wo, 16)
                sp.wait_ge(w2_mm, NQUAD * L + NQUAD)
                sp.dma_start(w1_s[:], w1[bass.ds(L + 1, 1)].rearrange("o p n -> (o p) n")).then_inc(ld_ffn, 16)
                sp.dma_start(w2_s[:], w2[bass.ds(L + 1, 1)].rearrange("o p k n -> (o p) k n")).then_inc(ld_ffn, 16)
            ov = out.rearrange("(p t) d -> t p d", t=TOK)
            for k in range(UNITS):
                sp.wait_ge(end_add, k + 1)
                sp.dma_start(ov[:, 4 * k:4 * k + 4, :], g3(xtok[:, k * 512:(k + 1) * 512], D)).then_inc(stored, 16)
            sp.wait_ge(stored, 16 * UNITS)

        @block.gpsimd
        def _(pool):
            gps = nc.gpsimd
            gps.memset(ident[:], 0.0).then_inc(const_init, 1)
            gps.memset(ones[:], 1.0 / D).then_inc(const_made, 1)
            gps.memset(cst[:, 0:1], 1e-5).then_inc(const_made, 1)
            gps.memset(cst[:, 1:2], 1.0).then_inc(const_made, 1)
            gps.memset(st_v[:], 1.0).then_inc(const_made, 1)
            pool.wait_ge(const_init, 1)
            gps.affine_select(out=ident[:], in_=ident[:], compare_op=ALU.not_equal, fill=1.0, base=0,
                              pattern=[[-1, 128]], channel_multiplier=1).then_inc(const_made, 1)

            def cosine_qk(n, i, first):
                tab = tabs[:, (i % 2) * 2 * DH:(i % 2) * 2 * DH + DH]
                pool.wait_ge(qn_ready, 4 * n + i + 1)
                if not first:
                    pool.wait_ge(t_mm, 4 * n + i - 3)
                gps.tensor_tensor(g3(tr[:, i, :], DH), g3(qn[:, i, :], DH), mid(tab, 8), ALU.mult).then_inc(t_done, 1)

            def rotate(n, i):
                pool.wait_ge(t_done, 4 * n + i + 1)
                pool.wait_ge(u_ready, 4 * n + i + 1)
                gps.tensor_tensor(tr[:, i, :], tr[:, i, :], ur[:, i, :], ALU.add).then_inc(rot_ready, 1)

            def normalise(m, g):
                pool.wait_ge(e_inv, 2 * m + g + 1)
                gps.tensor_tensor(g3(es[:, g, :], S), g3(es[:, g, :], S), bc(sinv[:, g, :], S),
                                  ALU.mult).then_inc(pn_ready, 1)

            def step(n, a=True, b=True, first=False):
                if a:
                    cosine_qk(n, 0, first)
                if b:
                    normalise(n - 1, 0)
                if a:
                    cosine_qk(n, 1, first)
                    rotate(n, 0)
                    rotate(n, 1)
                if b:
                    normalise(n - 1, 1)
                if a:
                    cosine_qk(n, 2, first)
                    cosine_qk(n, 3, first)
                    rotate(n, 2)
                    rotate(n, 3)

            step(0, b=False, first=True)
            step(1)
            with pool.Fori(1, DEPTH * NQUAD) as q:
                step(2 * q)
                step(2 * q + 1)
            step(DEPTH * NTILE, a=False)

        @block.tensor
        def _(pe):
            mm = nc.tensor.matmul

            def carry_wait(col=0):
                mm(OT[0][:, col:col + 1], identb[:], identb[:, 0:1], start=True, stop=True)

            def stage_transposes(u, first=False):
                pe.wait_ge(norm_step, LSTEPS * u + LSTEPS)
                pe.wait_ge(ctx_staged, u + 1)
                if not first:
                    pe.wait_ge(kept, u)
                for bk, src in zip(TP, (st_x, st_c)):
                    for k in range(4):
                        last = nc.tensor.transpose(bk[:, k * 128:(k + 1) * 128], src[:, k * 128:(k + 1) * 128], ident[:])
                last.then_inc(gate_step, 1)

            def gate_products(u):
                pe.wait_ge(gate_step, GSTEPS * u + 2)
                for k in range(4):
                    mm(SC[0][:, 8 * k:8 * k + 8], st_xT[:, k * 128:(k + 1) * 128], wg[:, 0, :], start=True, stop=False)
                    last = mm(SC[0][:, 8 * k:8 * k + 8], st_cT[:, k * 128:(k + 1) * 128], wg_kv[:], start=False, stop=True)
                last.then_inc(gate_step, 1)

            pe.wait_ge(const_made, 6)
            pe.wait_ge(small_ready, 1)
            stage_transposes(0, first=True)
            with pe.Fori(0, UNITS - 1) as u:
                gate_products(u)
                stage_transposes(u + 1)
            gate_products(UNITS - 1)
            pe.wait_ge(scan_step, 6)
            nc.tensor.transpose(TP[0][:, 0:128], gpk[:, 3, :], ident[:])
            nc.tensor.transpose(TP[0][:, 128:256], gpk[:, 0, :], ident[:]).then_inc(scan_step, 1)
            pe.wait_ge(scan_step, 12)
            nc.tensor.transpose(TP[1][:, 0:128], gro[:, 3, :], ident[:])
            nc.tensor.transpose(TP[1][:, 128:256], gro[:, 6, :], ident[:]).then_inc(scan_step, 1)

            def gate_rows_and_scores(u, first=False):
                pe.wait_ge(first_step, ASTEPS * u + 1)
                for k in range(4):
                    for h in range(XH):
                        for b in range(2):
                            c = k * XH + h
                            o = (k % 2) * 256 + h * 64
                            last = mm(TP[k // 2][HALVES[b], o:o + 64], st_sel[:, c:c + 1].broadcast_to([128, 64]),
                                      gro[:, 5, 64 * b:64 * b + 64], start=True, stop=True)
                last.then_inc(first_step, 1)
                if not first:
                    pe.wait_ge(x1_kept, u - 1)
                for k in range(4):
                    for b in range(2):
                        for h in range(XH):
                            c = k * 128 + 64 * b
                            last = mm(SCX[h][HALVES[b], k * 64:k * 64 + 64], st_cT[32 * h:32 * h + 32, c:c + 64],
                                      st_xT[32 * h:32 * h + 32, c:c + 64], start=True, stop=True,
                                      tile_position=(32 * h, 64 * b))
                last.then_inc(scored, 1)

            def mixed_values(u):
                pe.wait_ge(first_step, ASTEPS * u + ASTEPS)
                pe.wait_ge(staged, u + 1)
                carry_wait()
                for k in range(4):
                    for h in range(XH):
                        for b in range(2):
                            c = k * XH + h
                            o = (k % 2) * 132 + h * 33
                            last = mm(OT[k // 2][HALVES[b], o:o + 33], gexp[HALVES[b], c * 64:(c + 1) * 64],
                                      st_v[HALVES[b], c, :], start=True, stop=True)
                last.then_inc(mixed_mm, 1)

            def mixed_transposes(u, last_unit=False):
                pe.wait_ge(second_step, BSTEPS * u + BSTEPS)
                if last_unit:
                    pe.wait_ge(x1_kept, u)
                for k in range(4):
                    last = nc.tensor.transpose(QKV[0][:, k * 128:(k + 1) * 128], st_x[:, k * 128:(k + 1) * 128], ident[:])
                last.then_inc(x1_mm, 1)

            gate_rows_and_scores(0, first=True)
            mixed_values(0)
            gate_rows_and_scores(1, first=True)
            with pe.Fori(1, UNITS - 1) as u:
                mixed_values(u)
                mixed_transposes(u - 1)
                gate_rows_and_scores(u + 1)
            mixed_values(UNITS - 1)
            mixed_transposes(UNITS - 2)
            mixed_transposes(UNITS - 1, last_unit=True)

            def project(n, par, i, first=False, layer=None):
                if layer is not None:
                    pe.wait_ge(whi_done, 6 * layer + i + 1)
                    pe.wait_ge(wlo_done, 6 * layer + i + 1)
                if not first or i >= 2:
                    pe.wait_ge(qkv_evac, 6 * n + i - 1)
                bk = QKV[i % 2]
                xh, xl = (t[:, par * 128:(par + 1) * 128] for t in (xs_hi, xs_lo))
                wh, wl = (t[:, WCOL[i]:WCOL[i] + 512] for t in (w_hi, w_lo))
                mm(bk[:], xh, wh, start=True, stop=False)
                mm(bk[:], xh, wl, start=False, stop=False)
                mm(bk[:], xl, wh, start=False, stop=True).then_inc(qkv_mm, 1)

            def transposes(m, i, first):
                if not first and i in (0, 3):
                    pe.wait_ge(pt_evac, 2 * m - 1 + i // 3)
                if i >= 2:
                    pe.wait_ge(qkt_evac, 4 * m + i - 1)
                pe.wait_ge(rot_ready, 4 * m + i + 1)
                for k in range(4):
                    last = nc.tensor.transpose(TP[i % 2][:, k * 128:(k + 1) * 128], tr[:, i, k * 128:(k + 1) * 128], ident[:])
                last.then_inc(t_mm, 1)

            def scores(m, g, first, up=None, down=None):
                if down is not None and g == 0:
                    pe.wait_ge(ffn_done, down + 1)
                if up is not None and g == 1:
                    pe.wait_ge(fn_step, up + 1)
                if not first:
                    pe.wait_ge(s_sub, 2 * m + g - 1)
                pe.wait_ge(qkt_evac, 4 * m + 2 * g + 2)
                mm(SC[g][:], identb[:], band[:], start=True, stop=True)
                for k in range(4):
                    for s in range(2):
                        for h in range(2):
                            sl, c = HALVES[h], k * 128 + s * 64
                            last = mm(SC[g][sl, c:c + 64], qT[sl, g, k, s * 64:s * 64 + 64],
                                      kT[sl, g, k, s * 64:s * 64 + 64], start=False, stop=True,
                                      skip_group_check=True)
                last.then_inc(s_mm, 1)

            def prob_transposes(m, g, b=True):
                if g == 1 and b:
                    pe.wait_ge(qkt_evac, 4 * m + 6)
                pe.wait_ge(pn_ready, 2 * m + g + 1)
                for k in range(4):
                    last = nc.tensor.transpose(TP[g][:, k * 128:(k + 1) * 128], es[:, g, k * 128:(k + 1) * 128], ident[:])
                last.then_inc(pt_mm, 1)

            def values(m, g, par, first):
                if g == 0:
                    if not first:
                        pe.wait_ge(resid, m)
                    pe.wait_ge(qkv_evac, 6 * m + 6)
                pe.wait_ge(pt_evac, 2 * m + g + 1)
                if g == 0:
                    carry_wait()
                else:
                    carry_wait(256)
                for k in range(4):
                    for h in range(2):
                        for s in range(2):
                            hd = 8 * g + 2 * k + h
                            last = mm(OT[s][HALVES[h], (4 * g + k) * 64:(4 * g + k) * 64 + 64],
                                      vt[HALVES[s], par, hd * DH:(hd + 1) * DH],
                                      pT[HALVES[s], g, k, h * 64:h * 64 + 64], start=True, stop=True)
                last.then_inc(pv_mm, 1)

            def out_product(w, L, down=None):
                if down is not None:
                    pe.wait_ge(gelu_done, 3 * down + 2)
                pe.wait_ge(ld_wo, 16 * L + 16)
                pe.wait_ge(ot_evac, w + 1)
                for k in range(8):
                    last = mm(OT[0][:, 0:128], wo_s[:, k, :], oT[:, k, :], start=(k == 0), stop=(k == 7))
                last.then_inc(wo_mm, 1)

            def ffn_centre(f, scored):
                pe.wait_ge(s_sub, scored)
                pe.wait_ge(fx_ready, f + 1)
                mm(SC[1][:, 0:256], centring[:], fx[:], start=True, stop=True).then_inc(centre_mm, 1)

            def ffn_var(f):
                pe.wait_ge(fsq_done, f + 1)
                mm(SC[1][:, 256:512], ones[:], fsq[:], start=True, stop=True).then_inc(var_mm, 1)

            def ffn_up(f, L, t):
                pe.wait_ge(ot_evac, t + 1)
                pe.wait_ge(ld_ffn, 32 * L + 32)
                pe.wait_ge(fxn_ready, f + 1)
                for bk, parts in ((OT[0], ((1, 0), (1, 1))), (OT[1], ((1, 2), (0, 2))), (TP[1], ((0, 0), (0, 1)))):
                    for k, (gate, c) in enumerate(parts):
                        o = gate * FF + c * 128
                        last = mm(bk[0:FCH[c], k * 256:(k + 1) * 256], w1_s[:, o:o + FCH[c]], fxn[:], start=True, stop=True)
                    last.then_inc(w1_mm, 1)

            def ffn_down(f, scored):
                pe.wait_ge(s_sub, scored)
                pe.wait_ge(h_ready, 3 * f + 3)
                for c in range(3):
                    last = mm(SC[0][:, 0:256], w2_s[0:FCH[c], c, :], fh[0:FCH[c], c, :], start=(c == 0), stop=(c == 2))
                last.then_inc(w2_mm, 1)

            def step(n, par, L, a=True, b=True, c=True, up=None, down=None, first=False, b_first=False, c_first=False,
                     layer=None):
                m, t = n - 1, n - 2
                if a:
                    pe.wait_ge(xs_ready, n + 1)
                    project(n, par, 0, first, layer)
                if c:
                    prob_transposes(t, 0)
                if a:
                    project(n, par, 1, first, layer)
                if c and not c_first:
                    out_product(t - 1, L, down)
                if b:
                    transposes(m, 0, b_first)
                if a:
                    project(n, par, 2, first, layer)
                if down is not None:
                    ffn_down(down, 2 * m - 1)
                if b:
                    transposes(m, 1, b_first)
                if a:
                    project(n, par, 3, first, layer)
                if c:
                    values(t, 0, par, c_first)
                if up is not None:
                    ffn_centre(up, 2 * m)
                if c:
                    prob_transposes(t, 1, b)
                if b:
                    scores(m, 0, b_first, down=down)
                if up is not None:
                    ffn_var(up)
                if b:
                    transposes(m, 2, b_first)
                if c:
                    values(t, 1, par, c_first)
                if b:
                    transposes(m, 3, b_first)
                if a:
                    project(n, par, 4, first, layer)
                if b:
                    scores(m, 1, b_first, up=up)
                if a:
                    project(n, par, 5, first, layer)
                if up is not None:
                    ffn_up(up, L, t)

            pe.wait_ge(const_made, 6)
            step(0, 0, 0, b=False, c=False, first=True, layer=0)
            step(1, 1, 0, c=False, b_first=True)
            step(2, 0, 0, c_first=True)
            step(3, 1, 0)
            with pe.Fori(2, NQUAD) as q:
                step(2 * q, 0, 0, up=q - 2)
                step(2 * q + 1, 1, 0, down=q - 2)
            with pe.Fori(1, DEPTH) as L:
                n, g = NTILE * L, NQUAD * L
                step(n, 0, L - 1, up=g - 2, layer=L)
                step(n + 1, 1, L - 1, down=g - 2)
                step(n + 2, 0, L - 1, up=g - 1)
                step(n + 3, 1, L, down=g - 1)
                with pe.Fori(2, NQUAD) as q:
                    n, g = NTILE * L + 2 * q, NQUAD * L + q
                    step(n, 0, L, up=g - 2)
                    step(n + 1, 1, L, down=g - 2)
            n, g = DEPTH * NTILE, DEPTH * NQUAD
            step(n, 0, DEPTH - 1, a=False, up=g - 2)
            step(n + 1, 1, DEPTH - 1, a=False, b=False, down=g - 2)
            out_product(n - 1, DEPTH - 1)
            ffn_centre(g - 1, 2 * n)
            ffn_var(g - 1)
            ffn_up(g - 1, DEPTH - 1, n - 1)
            ffn_down(g - 1, 2 * n)
            for k in range(UNITS):
                pe.wait_ge(ffn_done, g)
                if k >= 2:
                    pe.wait_ge(end_add, k - 1)
                for j in range(4):
                    o = (4 * k + j) * 128
                    last = nc.tensor.transpose(QKV[k % 2][:, j * 128:(j + 1) * 128], xT[:, o:o + 128], ident[:])
                last.then_inc(end_mm, 1)

        @block.scalar
        def _(act):
            fn = nc.scalar.activation
            EPS = cst[:, 0:1]
            ONE = cst[:, 1:2]
            act.wait_ge(const_made, 6)
            act.wait_ge(ld_ctx, 32)

            def exp_ln_tables():
                nc.scalar.preload_act_table_set("natural_log_exp_and_others")

            exp_ln_tables()

            def ln_square(step, base):
                act.wait_ge(step, base + 3)
                fn(psq[:], st_x[:], ACT.Square).then_inc(step, 1)

            def ln_rstd(step, base):
                act.wait_ge(step, base + 5)
                fn(ST[2][:, 0:4], ST[2][:, 0:4], ACT.Ln, bias=EPS, scale=1.0 / D).then_inc(step, 1)
                act.wait_ge(step, base + 6)
                fn(ST[2][:, 0:4], ST[2][:, 0:4], ACT.Exp, scale=-0.5).then_inc(step, 1)

            def to_products(u):
                act.wait_ge(gate_step, GSTEPS * u + 1)
                nc.scalar.copy(st_xT[:], TP[0][:])
                nc.scalar.copy(st_cT[:], TP[1][:]).then_inc(gate_step, 1)

            def keep(u):
                nc.scalar.copy(xlT[:, bass.ds(u * 512, 512)], TP[0][:])
                nc.scalar.copy(xT[:, bass.ds(u * 512, 512)], TP[1][:]).then_inc(kept, 1)

            nc.scalar.copy(st_c[:], ctok[:, 0:512]).then_inc(ctx_staged, 1)
            ln_square(norm_step, 0)
            ln_rstd(norm_step, 0)
            with act.Fori(0, UNITS - 1) as u:
                to_products(u)
                ln_square(norm_step, LSTEPS * u + LSTEPS)
                nc.scalar.copy(st_c[:], ctok[:, bass.ds(u * 512 + 512, 512)]).then_inc(ctx_staged, 1)
                ln_rstd(norm_step, LSTEPS * u + LSTEPS)
                keep(u)
            to_products(UNITS - 1)
            keep(UNITS - 1)
            act.wait_ge(scan_step, 3)
            fn(gpk[:, 2, :], gpk[:, 2, :], ACT.Exp).then_inc(scan_step, 1)
            act.wait_ge(scan_step, 4)
            fn(gpk[:, 2, :], gpk[:, 2, :], ACT.Ln, bias=ONE).then_inc(scan_step, 1)
            act.wait_ge(scan_step, 13)
            nc.scalar.copy(a_tok[:], TP[1][:, 0:128])
            fn(em_tok[:], TP[1][:, 128:256], ACT.Exp).then_inc(scan_step, 1)

            def first_operands(u):
                act.wait_ge(first_step, ASTEPS * u)
                nc.scalar.copy(ST[7][:, 0:1], ident[:, 0:1])
                nc.scalar.copy(st_xT[:], xlT[:, bass.ds(u * 512, 512)])
                nc.scalar.copy(st_cT[:], xT[:, bass.ds(u * 512, 512)])
                nc.scalar.copy(st_a[:], a_tok[:, bass.ds(u * 16, 16)])
                nc.scalar.copy(st_sel[:], ident[:, bass.ds(u * 16, 16)]).then_inc(first_step, 1)

            def second_operands(u):
                nc.scalar.copy(st_v[:, :, 0:XD], g3(ctok[:, bass.ds(u * 512, 512)], XD))
                nc.scalar.copy(st_em[:], em_tok[:, bass.ds(u * 16, 16)]).then_inc(staged, 1)

            def weights_exp(u):
                act.wait_ge(first_step, ASTEPS * u + 4)
                fn(gexp[:], gexp[:], ACT.Exp).then_inc(first_step, 1)

            def second_part(u, meanwhile=None):
                base = BSTEPS * u
                act.wait_ge(second_step, base + 8)
                fn(psq[:], hmix[:], ACT.Square).then_inc(second_step, 1)
                if meanwhile is not None:
                    weights_exp(meanwhile)
                act.wait_ge(second_step, base + 10)
                fn(ST[5][:], ST[5][:], ACT.Ln, bias=EPS, scale=1.0 / XD).then_inc(second_step, 1)
                act.wait_ge(second_step, base + 11)
                fn(ST[5][:], ST[5][:], ACT.Exp, scale=-0.5).then_inc(second_step, 1)
                if meanwhile is not None:
                    second_operands(meanwhile)
                ln_square(second_step, base + BNORM)
                ln_rstd(second_step, base + BNORM)

            def keep_x1(u):
                act.wait_ge(x1_mm, u + 1)
                nc.scalar.copy(ST[9][:, 0:1], ident[:, 0:1])
                nc.scalar.copy(xT[:, bass.ds(u * 512, 512)], QKV[0][:]).then_inc(x1_kept, 1)

            act.wait_ge(scan_step, SSTEPS)
            nc.scalar.copy(st_xT[:], xlT[:, 0:512])
            nc.scalar.copy(st_cT[:], xT[:, 0:512])
            nc.scalar.copy(st_a[:], a_tok[:, 0:16])
            nc.scalar.copy(st_sel[:], ident[:, 0:16]).then_inc(first_step, 1)
            second_operands(0)
            weights_exp(0)
            first_operands(1)
            second_part(0, meanwhile=1)
            with act.Fori(1, UNITS - 1) as u:
                first_operands(u + 1)
                keep_x1(u - 1)
                second_part(u, meanwhile=u + 1)
            keep_x1(UNITS - 2)
            second_part(UNITS - 1)
            keep_x1(UNITS - 1)

            def split_hi(L, i, first=False):
                if i == 0:
                    act.wait_ge(ld_wqkv, 16 * L + 16)
                if not first:
                    act.wait_ge(qkv_mm, 6 * NTILE * L - 5 + i)
                sl = slice(WCOL[i], WCOL[i] + 512)
                nc.scalar.copy(w_hi[:, sl], w_raw[:, sl]).then_inc(whi_done, 1)

            def stationary_hi(n, par, local, early=False):
                if not early:
                    act.wait_ge(qkv_mm, 6 * n - 6)
                    act.wait_ge(xs_ready, n - 1)
                lo, hi = views(local, 128)
                half = slice(par * 128, par * 128 + 128)
                nc.scalar.copy(xs_hi[0:64, half], lo)
                nc.scalar.copy(late(xs_hi[:, half]), hi).then_inc(xs_half, 1)

            def ffn_input(f, q):
                act.wait_ge(resid, 2 * f + 2)
                lo, hi = views(q, 256)
                nc.scalar.copy(fx[0:64, :], lo)
                nc.scalar.copy(late(fx), hi).then_inc(fx_ready, 1)

            def square_qk(n, i, first):
                act.wait_ge(qkv_mm, 6 * n + i + 1)
                if not first or i >= 2:
                    act.wait_ge(ss_red, 4 * n + i - 1)
                fn(sq[:, i % 2, :], QKV[i % 2][:], ACT.Square).then_inc(qk_sq, 1)

            def evacuate_qk(n, i, first):
                if not first:
                    act.wait_ge(qn_ready, 4 * n + i - 3)
                nc.scalar.copy(raw[:, i, :], QKV[i % 2][:]).then_inc(qkv_evac, 1)

            def evacuate_v(n, i, par, early):
                act.wait_ge(qkv_mm, 6 * n + i + 1)
                if not early and i == 4:
                    act.wait_ge(pv_mm, 2 * n - 2)
                nc.scalar.copy(vt[:, par, (i - 4) * 512:(i - 3) * 512], QKV[i % 2][:]).then_inc(qkv_evac, 1)

            def evacuate_t(m, i, first):
                act.wait_ge(t_mm, 4 * m + i + 1)
                if not first:
                    act.wait_ge(s_mm, 2 * m - 1 + i // 2)
                dst = (qT, kT)[i % 2]
                nc.scalar.copy(dst[:, i // 2, :, :].rearrange("p k n -> p (k n)"), TP[i % 2][:]).then_inc(qkt_evac, 1)

            def exponent(m, g):
                act.wait_ge(s_sub, 2 * m + g + 1)
                fn(es[:, g, :], es[:, g, :], ACT.Exp).then_inc(e_exp, 1)

            def evacuate_pt(m, g, first):
                act.wait_ge(pt_mm, 2 * m + g + 1)
                if not first:
                    act.wait_ge(pv_mm, 2 * m - 1 + g)
                nc.scalar.copy(pT[:, g, :, :].rearrange("p k n -> p (k n)"), TP[g][:]).then_inc(pt_evac, 1)

            def evacuate_ot(m, first):
                act.wait_ge(pv_mm, 2 * m + 2)
                if not first:
                    act.wait_ge(wo_mm, m)
                for s in range(2):
                    last = nc.scalar.copy(oT[:, :, s * 64:s * 64 + 64], g3(OT[s][:], 64))
                last.then_inc(ot_evac, 1)

            def ffn_square(f):
                act.wait_ge(centre_mm, f + 1)
                fn(fsq[:], SC[1][:, 0:256], ACT.Square).then_inc(fsq_done, 1)

            def ffn_rstd(f):
                act.wait_ge(var_mm, f + 1)
                fn(fln[:], SC[1][:, 256:512], ACT.Ln, bias=EPS).then_inc(fln_done, 1)
                act.wait_ge(fln_done, f + 1)
                fn(frs[:], fln[:], ACT.Exp, scale=-0.5).then_inc(frs_done, 1)

            def ffn_gelu(f, L):
                act.wait_ge(vec_ready, L + 1)
                for c in range(3):
                    if c != 1:
                        act.wait_ge(w1_mm, 3 * f + 1 + c // 2)
                    src = OT[0][:, c * 256:(c + 1) * 256] if c < 2 else OT[1][0:FCH[2], 0:256]
                    fn(fh[0:FCH[c], c, :], src, ACT.Gelu, bias=vecs[0:FCH[c], 6 + c:7 + c]).then_inc(gelu_done, 1)

            def step(n, par, L, a=True, b=True, c=True, up=None, first=False, b_first=False, c_first=False,
                     early=False, split=None, nxt=None, up_q=None):
                m, t = n - 1, n - 2

                def hi(*chunks):
                    if split is not None:
                        for i in chunks:
                            split_hi(split, i)

                if a:
                    square_qk(n, 0, first)
                if c:
                    evacuate_pt(t, 0, c_first)
                if a:
                    evacuate_qk(n, 0, first)
                    square_qk(n, 1, first)
                    evacuate_qk(n, 1, first)
                if b:
                    evacuate_t(m, 0, b_first)
                if a:
                    square_qk(n, 2, first)
                if b:
                    evacuate_t(m, 1, b_first)
                if up is not None:
                    ffn_input(up, up_q)
                if a:
                    square_qk(n, 3, first)
                if a:
                    evacuate_qk(n, 2, first)
                hi(0, 1)
                if up is not None:
                    ffn_square(up)
                if c:
                    evacuate_pt(t, 1, c_first)
                if a:
                    evacuate_qk(n, 3, first)
                if nxt is not None:
                    stationary_hi(n + 1, 1 - par, nxt, early=first)
                if up is not None:
                    ffn_rstd(up)
                if par == 1:
                    exp_ln_tables()
                if b:
                    evacuate_t(m, 2, b_first)
                    exponent(m, 0)
                    evacuate_t(m, 3, b_first)
                if c:
                    evacuate_ot(t, c_first)
                hi(2, 3)
                if a:
                    evacuate_v(n, 4, par, early)
                    evacuate_v(n, 5, par, early)
                if b:
                    exponent(m, 1)
                hi(4, 5)
                if up is not None:
                    ffn_gelu(up, L)

            act.wait_ge(small_ready, 1)
            for i in range(6):
                split_hi(0, i, first=True)
            act.wait_ge(x1_kept, UNITS)
            stationary_hi(0, 0, 0, early=True)
            step(0, 0, 0, b=False, c=False, first=True, early=True, nxt=1)
            step(1, 1, 0, c=False, b_first=True, early=True, nxt=2)
            step(2, 0, 0, c_first=True, nxt=3)
            step(3, 1, 0, nxt=4)
            with act.Fori(2, NQUAD - 1) as q:
                step(2 * q, 0, 0, up=q - 2, up_q=q - 2, nxt=2 * q + 1)
                step(2 * q + 1, 1, 0, nxt=2 * q + 2)
            with act.Fori(1, DEPTH) as L:
                n, g = NTILE * L, NQUAD * L
                step(n - 2, 0, L - 1, up=g - 3, up_q=NQUAD - 3, nxt=NTILE - 1)
                step(n - 1, 1, L - 1, split=L, nxt=0)
                step(n, 0, L - 1, up=g - 2, up_q=NQUAD - 2, nxt=1)
                step(n + 1, 1, L - 1, nxt=2)
                step(n + 2, 0, L - 1, up=g - 1, up_q=NQUAD - 1, nxt=3)
                step(n + 3, 1, L, nxt=4)
                with act.Fori(2, NQUAD - 1) as q:
                    n, g = NTILE * L + 2 * q, NQUAD * L + q
                    step(n, 0, L, up=g - 2, up_q=q - 2, nxt=2 * q + 1)
                    step(n + 1, 1, L, nxt=2 * q + 2)
            n, g = DEPTH * NTILE, DEPTH * NQUAD
            step(n - 2, 0, DEPTH - 1, up=g - 3, up_q=NQUAD - 3, nxt=NTILE - 1)
            step(n - 1, 1, DEPTH - 1)
            step(n, 0, DEPTH - 1, a=False, up=g - 2, up_q=NQUAD - 2)
            step(n + 1, 1, DEPTH - 1, a=False, b=False)
            ffn_input(g - 1, NQUAD - 1)
            ffn_square(g - 1)
            ffn_rstd(g - 1)
            ffn_gelu(g - 1, DEPTH - 1)

        @block.vector
        def _(dve):
            v = nc.vector
            tt, ts, stt = v.tensor_tensor, v.tensor_scalar, v.scalar_tensor_tensor

            v.memset(xs_hi[:].bitcast(F32), 0.0)
            v.memset(xs_lo[:].bitcast(F32), 0.0)
            v.memset(fx[:], 0.0)
            v.memset(gro[:, 7, :], 0.0).then_inc(const_made, 1)
            dve.wait_ge(ld_small, 16 * 13)
            dve.wait_ge(const_made, 6)
            v.tensor_copy(band[:], band_f[:])
            v.tensor_copy(identb[:], ident[:])
            tt(centring[:], ident[:], ones[:], ALU.subtract)
            v.tensor_copy(vecs[:], vecs_all[:, 0:NVEC]).then_inc(vec_ready, 1)
            tt(tabs[:], rot_base[:], scales[:, 0, :, :].rearrange("p a b -> p (a b)"), ALU.mult).then_inc(tabs_ready, 1)
            tt(wg_kv[:], wg[:, 1, :], wg[:, 2, :], ALU.add).then_inc(small_ready, 1)

            def ln_sums(step, base, xs, free=None):
                if base is not None:
                    dve.wait_ge(step, base)
                    v.memset(ST[8][:, 0:1], 0.0)
                else:
                    base = 0
                v.tensor_reduce(ST[0][:, 0:4], g3(xs, D), AX_X, ALU.add).then_inc(step, 1)
                dve.wait_ge(step, base + 1)
                ts(ST[1][:, 0:4], ST[0][:, 0:4], 1.0 / D, None, ALU.mult).then_inc(step, 1)
                dve.wait_ge(step, base + 2)
                if free is not None:
                    dve.wait_ge(*free)
                    v.memset(ST[8][:, 0:1], 0.0)
                tt(g3(st_x[:], D), g3(xs, D), bc(ST[1][:, 0:4], D), ALU.subtract).then_inc(step, 1)
                dve.wait_ge(step, base + 4)
                v.tensor_reduce(ST[2][:, 0:4], g3(psq[:], D), AX_X, ALU.add).then_inc(step, 1)

            def ln_scale(step, base):
                dve.wait_ge(step, base + 7)
                tt(g3(st_x[:], D), g3(st_x[:], D), bc(ST[2][:, 0:4], D), ALU.mult).then_inc(step, 1)

            def keep_gates(u):
                dve.wait_ge(gate_step, GSTEPS * u + 3)
                ts(gtok[:, bass.ds(u * 4, 4), :], g3(SC[0][:, 0:32], 8), 1.0, None, ALU.mult).then_inc(gate_step, 1)

            dve.wait_ge(ld_x, 32)
            ln_sums(norm_step, None, xtok[:, 0:512])
            ln_scale(norm_step, 0)
            with dve.Fori(0, UNITS - 1) as u:
                ln_sums(norm_step, LSTEPS * u + LSTEPS, xtok[:, bass.ds(u * 512 + 512, 512)], free=(gate_step, GSTEPS * u + 1))
                ln_scale(norm_step, LSTEPS * u + LSTEPS)
                keep_gates(u)
            keep_gates(UNITS - 1)
            dve.wait_ge(gate_step, UNITS * GSTEPS)
            tt(g3(gpk[:, 0, :], XH), gtok[:, :, 0:4], mid(bg[:, 0:4], NPAIR), ALU.add)
            tt(g3(gpk[:, 1, :], XH), gtok[:, :, 4:8], mid(bg[:, 4:8], NPAIR), ALU.add).then_inc(scan_step, 1)
            dve.wait_ge(scan_step, 1)
            ts(gpk[:, 2, :], gpk[:, 1, :], -1.0, None, ALU.mult).then_inc(scan_step, 1)
            dve.wait_ge(scan_step, 2)
            tt(gpk[:, 2, :], gpk[:, 2, :], gpk[:, 1, :], ALU.min).then_inc(scan_step, 1)
            dve.wait_ge(scan_step, 5)
            stt(gpk[:, 3, :], gpk[:, 1, :], 0.0, gpk[:, 2, :], ALU.min, ALU.subtract).then_inc(scan_step, 1)
            dve.wait_ge(scan_step, 7)
            v.tensor_copy(gro[:, 0:2, :], g3(TP[0][:, 0:256], 128)).then_inc(scan_step, 1)
            dve.wait_ge(scan_step, 8)
            for sl in HALVES:
                last = v.tensor_tensor_scan(gro[:, 2, sl], gro[:, 0, sl], gro[:, 7, sl], 0.0, ALU.add, ALU.add)
            last.then_inc(scan_step, 1)
            dve.wait_ge(scan_step, 9)
            tt(gro[:, 3, :], gro[:, 1, :], gro[:, 2, :], ALU.subtract).then_inc(scan_step, 1)
            dve.wait_ge(scan_step, 10)
            for sl in HALVES:
                last = v.tensor_tensor_scan(gro[:, 4, sl], gro[:, 3, sl], gro[:, 7, sl], -3.0e38, ALU.max, ALU.add)
            last.then_inc(scan_step, 1)
            dve.wait_ge(scan_step, 11)
            ts(gro[:, 5, :], gro[:, 4, :], -1.0, None, ALU.mult)
            stt(gro[:, 6, :], gro[:, 2, :], -1.0, gro[:, 4, :], ALU.mult, ALU.subtract).then_inc(scan_step, 1)

            def log_weights(u):
                base = ASTEPS * u
                dve.wait_ge(first_step, base + 2)
                for k in range(2):
                    last = tt(g3(gexp[:, k * 512:(k + 1) * 512], S), g3(TP[k][:], S), bc(st_a[:, k * 8:(k + 1) * 8], S), ALU.add)
                last.then_inc(first_step, 1)
                dve.wait_ge(first_step, base + 3)
                stt(g3(gexp[:], S), g3(gexp[:], S), 0.0, mid(causal[:], 16), ALU.min, ALU.add).then_inc(first_step, 1)

            def weighted_scores(u):
                dve.wait_ge(first_step, ASTEPS * u + 5)
                dve.wait_ge(scored, u + 1)
                for h in range(XH):
                    e = gexp[:].rearrange("p (k h s) -> p k h s", k=4, h=XH)[:, :, h, :]
                    last = stt(e, g3(SCX[h][:, 0:256], S), float(XD) ** -0.5, e, ALU.mult, ALU.mult)
                last.then_inc(first_step, 1)

            def second_part(u, following=None, first=False):
                base = BSTEPS * u
                dve.wait_ge(mixed_mm, u + 1)
                for k in range(2):
                    last = ts(ST[3][:, k * 8:(k + 1) * 8], g3(OT[k][:, 0:264], 33)[:, :, 32], -1.0, None, ALU.mult)
                last.then_inc(second_step, 1)
                dve.wait_ge(second_step, base + 1)
                for k in range(2):
                    last = tt(ST[3][:, k * 8:(k + 1) * 8], g3(OT[k][:, 0:264], 33)[:, :, 32], ST[3][:, k * 8:(k + 1) * 8], ALU.max)
                last.then_inc(second_step, 1)
                dve.wait_ge(second_step, base + 2)
                tt(ST[3], ST[3], st_em[:], ALU.max).then_inc(second_step, 1)
                dve.wait_ge(second_step, base + 3)
                ts(ST[3], ST[3], 1e-6, None, ALU.add).then_inc(second_step, 1)
                dve.wait_ge(second_step, base + 4)
                v.reciprocal(ST[3], ST[3]).then_inc(second_step, 1)
                dve.wait_ge(second_step, base + 5)
                for k in range(2):
                    last = tt(g3(hmix[:, k * 256:(k + 1) * 256], XD), g3(OT[k][:, 0:264], 33)[:, :, 0:32],
                              bc(ST[3][:, k * 8:(k + 1) * 8], XD), ALU.mult)
                last.then_inc(second_step, 1)
                dve.wait_ge(second_step, base + 6)
                v.tensor_reduce(ST[4], g3(hmix[:], XD), AX_X, ALU.add).then_inc(second_step, 1)
                dve.wait_ge(second_step, base + 7)
                ts(ST[4], ST[4], 1.0 / XD, None, ALU.mult).then_inc(mixed, 1)
                dve.wait_ge(mixed, u + 1)
                tt(g3(hmix[:], XD), g3(hmix[:], XD), bc(ST[4], XD), ALU.subtract).then_inc(second_step, 1)
                if following is not None:
                    log_weights(following)
                dve.wait_ge(second_step, base + 9)
                v.tensor_reduce(ST[5], g3(psq[:], XD), AX_X, ALU.add).then_inc(second_step, 1)
                dve.wait_ge(second_step, base + 12)
                tt(g3(hmix[:], XD), g3(hmix[:], XD), bc(ST[5], XD), ALU.mult).then_inc(second_step, 1)
                dve.wait_ge(second_step, base + 13)
                tt(g3(hmix[:], D), g3(hmix[:], D), mid(onorm[:], 4), ALU.mult).then_inc(second_step, 1)
                x1 = xtok[:, bass.ds(u * 512, 512)]
                dve.wait_ge(second_step, base + 14)
                tt(x1, x1, hmix[:], ALU.add).then_inc(second_step, 1)
                if following is not None:
                    weighted_scores(following)
                ln_sums(second_step, base + BNORM, x1, free=None if first else (x1_mm, u))
                ln_scale(second_step, base + BNORM)

            log_weights(0)
            weighted_scores(0)
            second_part(0, following=1, first=True)
            with dve.Fori(1, UNITS - 1) as u:
                second_part(u, following=u + 1)
            second_part(UNITS - 1)

            def split_lo(L, *chunks):
                for i in chunks:
                    dve.wait_ge(whi_done, 6 * L + i + 1)
                    sl = slice(WCOL[i], WCOL[i] + 512)
                    tt(w_lo[:, sl], w_raw[:, sl], w_hi[:, sl].bitcast(F32), ALU.subtract).then_inc(wlo_done, 1)

            def stationary_lo(n, par, local):
                dve.wait_ge(xs_half, n + 1)
                lo, hi = views(local, 128)
                half = slice(par * 128, par * 128 + 128)
                tt(xs_lo[0:64, half], lo, xs_hi[0:64, half].bitcast(F32), ALU.subtract)
                tt(late(xs_lo[:, half]), hi, late(xs_hi[:, half].bitcast(F32)), ALU.subtract).then_inc(xs_ready, 1)

            def sum_squares(n, i, first):
                dve.wait_ge(qk_sq, 4 * n + i + 1)
                if i == 0 and not first:
                    dve.wait_ge(newton, 12 * n)
                v.tensor_reduce(ss[:, 8 * i:8 * i + 8], g3(sq[:, i % 2, :], DH), AX_X, ALU.add).then_inc(ss_red, 1)

            def norm_op(n, k, first):
                y, a, b = nwt[:, 0, :], nwt[:, 1, :], nwt[:, 2, :]
                if k == 0:
                    dve.wait_ge(ss_red, 4 * n + 4)
                    op = ts(ss[:], ss[:], 1e-24, None, ALU.max)
                else:
                    dve.wait_ge(newton, 12 * n + k)
                    if k == 1:
                        op = ts(seed[:], ss[:].bitcast(I32), 1, None, ALU.logical_shift_right)
                    elif k == 2:
                        op = ts(y.bitcast(I32), seed[:], -1.0, MAGIC, ALU.mult, ALU.add)
                    elif k % 3 == 0:
                        op = tt(a, y, y, ALU.mult)
                    elif k % 3 == 1:
                        op = stt(b, a, -0.5, ss[:], ALU.mult, ALU.mult)
                    else:
                        op = stt(rinv[:] if k == 11 else y, b, 1.5, y, ALU.add, ALU.mult)
                op.then_inc(newton, 1)

            def unit_qk(n, i, first):
                if i == 0:
                    dve.wait_ge(newton, 12 * n + 12)
                    dve.wait_ge(qkv_evac, 6 * n + 4)
                if i == 0 and not first:
                    dve.wait_ge(t_done, 4 * n)
                tt(g3(qn[:, i, :], DH), g3(raw[:, i, :], DH), bc(rinv[:, 8 * i:8 * i + 8], DH), ALU.mult).then_inc(qn_ready, 1)

            def sine_qk(n, i, first):
                dve.wait_ge(qn_ready, 4 * n + i + 1)
                if i == 0 and not first:
                    dve.wait_ge(rot_ready, 4 * n)
                o = (2 * (i % 2) + 1) * DH
                swapped = qn[:, i, :].rearrange("p (h t d) -> p h t d", t=2, d=32)[:, :, ::-1, :]
                tab = tabs[:, o:o + DH].rearrange("p (t d) -> p t d", t=2).unsqueeze(1).broadcast_to([128, 8, 2, 32])
                tt(ur[:, i, :].rearrange("p (h t d) -> p h t d", t=2, d=32), swapped, tab, ALU.mult).then_inc(u_ready, 1)

            def row_max(m, g):
                dve.wait_ge(s_mm, 2 * m + g + 1)
                v.tensor_reduce(smax[:, g, :], g3(SC[g][:], S), AX_X, ALU.max).then_inc(s_max, 1)

            def row_shift(m, g, first):
                dve.wait_ge(s_max, 2 * m + g + 1)
                if not first:
                    dve.wait_ge(pt_mm, 2 * m + g - 1)
                tt(g3(es[:, g, :], S), g3(SC[g][:], S), bc(smax[:, g, :], S), ALU.subtract).then_inc(s_sub, 1)

            def row_sum(m, g):
                dve.wait_ge(e_exp, 2 * m + g + 1)
                v.tensor_reduce(ssum[:, g, :], g3(es[:, g, :], S), AX_X, ALU.add).then_inc(e_sum, 1)

            def row_inverse(m, g, first):
                dve.wait_ge(e_sum, 2 * m + g + 1)
                if not first:
                    dve.wait_ge(pn_ready, 2 * m + g - 1)
                v.reciprocal(sinv[:, g, :], ssum[:, g, :]).then_inc(e_inv, 1)

            def residual(w, local):
                dve.wait_ge(wo_mm, w + 1)
                cols = bass.ds(local * 128, 128) if not isinstance(local, int) else slice(local * 128, local * 128 + 128)
                tt(xT[:, cols], OT[0][:, 0:128], xT[:, cols], ALU.add).then_inc(resid, 1)

            def ffn_scale(f):
                dve.wait_ge(frs_done, f + 1)
                tt(fxn[:], SC[1][:, 0:256], frs[:], ALU.mult).then_inc(fn_step, 1)

            def ffn_gain(f):
                dve.wait_ge(fn_step, f + 1)
                ts(fxn[:], fxn[:], vecs[:, 0:1], vecs[:, 1:2], ALU.mult, ALU.add).then_inc(fxn_ready, 1)

            def ffn_hidden(f):
                for c in (0, 1, 2):
                    dve.wait_ge(gelu_done, 3 * f + c + 1)
                    if c == 0:
                        dve.wait_ge(w1_mm, 3 * f + 3)
                    rows = slice(0, FCH[c])
                    src = TP[1][rows, c * 256:(c + 1) * 256] if c < 2 else OT[1][rows, 256:512]
                    stt(fh[rows, c, :], src, vecs[rows, 3 + c:4 + c], fh[rows, c, :], ALU.add, ALU.mult).then_inc(h_ready, 1)

            def ffn_residual(f, q):
                dve.wait_ge(w2_mm, f + 1)
                cols = bass.ds(q * 256, 256) if not isinstance(q, int) else slice(q * 256, q * 256 + 256)
                stt(xT[:, cols], SC[0][:, 0:256], vecs[:, 2:3], xT[:, cols], ALU.add, ALU.add).then_inc(ffn_done, 1)

            def new_tables(L, n):
                dve.wait_ge(t_done, 4 * n)
                tt(tabs[:], rot_base[:], scales[:, bass.ds(L, 1), :, :].rearrange("p o a b -> p (o a b)"),
                   ALU.mult).then_inc(tabs_ready, 1)
                dve.wait_ge(tabs_ready, L + 1)

            def step(n, par, a=True, b=True, w=None, up=None, down=None, down_q=None, nxt=None, first=False, b_first=False,
                     tables=None, split=None):
                m = n - 1

                def norm_ops(*ops):
                    if a:
                        for k in ops:
                            norm_op(n, k, first)

                if down is not None:
                    ffn_hidden(down)
                if w is not None:
                    residual(n - 3, w)
                if a:
                    sum_squares(n, 0, first)
                if a:
                    sum_squares(n, 1, first)
                if down is not None:
                    ffn_residual(down, down_q)
                if a:
                    sum_squares(n, 2, first)
                if a:
                    sum_squares(n, 3, first)
                norm_ops(0, 1, 2, 3, 4, 5, 6, 7, 8)
                if b:
                    row_max(m, 0)
                norm_ops(9)
                if b:
                    row_shift(m, 0, b_first)
                norm_ops(10, 11)
                if tables is not None:
                    new_tables(tables, n)
                if a:
                    unit_qk(n, 0, first)
                if up is not None:
                    ffn_scale(up)
                if a:
                    unit_qk(n, 1, first)
                if b:
                    row_sum(m, 0)
                if up is not None:
                    ffn_gain(up)
                if a:
                    sine_qk(n, 0, first)
                if b:
                    row_inverse(m, 0, b_first)
                if nxt is not None:
                    stationary_lo(n + 1, 1 - par, nxt)
                if split is not None:
                    split_lo(split, 0, 1)
                if b:
                    row_max(m, 1)
                if b:
                    row_shift(m, 1, b_first)
                if a:
                    sine_qk(n, 1, first)
                    unit_qk(n, 2, first)
                if split is not None:
                    split_lo(split, 2, 3)
                if b:
                    row_sum(m, 1)
                if a:
                    unit_qk(n, 3, first)
                if b:
                    row_inverse(m, 1, b_first)
                if a:
                    sine_qk(n, 2, first)
                    sine_qk(n, 3, first)
                if split is not None:
                    split_lo(split, 4, 5)

            dve.wait_ge(x1_kept, UNITS)
            dve.wait_ge(tabs_ready, 1)
            stationary_lo(0, 0, 0)
            split_lo(0, 0, 1, 2, 3, 4, 5)
            step(0, 0, b=False, first=True, nxt=1)
            step(1, 1, b_first=True, nxt=2)
            step(2, 0, nxt=3)
            step(3, 1, w=0, nxt=4)
            with dve.Fori(2, NQUAD - 1) as q:
                step(2 * q, 0, w=2 * q - 3, up=q - 2, nxt=2 * q + 1)
                step(2 * q + 1, 1, w=2 * q - 2, down=q - 2, down_q=q - 2, nxt=2 * q + 2)
            with dve.Fori(1, DEPTH) as L:
                n, g = NTILE * L, NQUAD * L
                step(n - 2, 0, w=NTILE - 5, up=g - 3, nxt=NTILE - 1)
                step(n - 1, 1, w=NTILE - 4, down=g - 3, down_q=NQUAD - 3, split=L, nxt=0)
                step(n, 0, w=NTILE - 3, up=g - 2, tables=L, nxt=1)
                step(n + 1, 1, w=NTILE - 2, down=g - 2, down_q=NQUAD - 2, nxt=2)
                step(n + 2, 0, w=NTILE - 1, up=g - 1, nxt=3)
                step(n + 3, 1, w=0, down=g - 1, down_q=NQUAD - 1, nxt=4)
                dve.wait_ge(ffn_done, g)
                ts(vecs[:], vecs_all[:, bass.ds(L * NVEC, NVEC)], 1.0, None, ALU.mult).then_inc(vec_ready, 1)
                with dve.Fori(2, NQUAD - 1) as q:
                    n, g = NTILE * L + 2 * q, NQUAD * L + q
                    step(n, 0, w=2 * q - 3, up=g - 2, nxt=2 * q + 1)
                    step(n + 1, 1, w=2 * q - 2, down=g - 2, down_q=q - 2, nxt=2 * q + 2)
            n, g = DEPTH * NTILE, DEPTH * NQUAD
            step(n - 2, 0, w=NTILE - 5, up=g - 3, nxt=NTILE - 1)
            step(n - 1, 1, w=NTILE - 4, down=g - 3, down_q=NQUAD - 3)
            step(n, 0, a=False, w=NTILE - 3, up=g - 2)
            step(n + 1, 1, a=False, b=False, w=NTILE - 2, down=g - 2, down_q=NQUAD - 2)
            residual(n - 1, NTILE - 1)
            ffn_scale(g - 1)
            ffn_gain(g - 1)
            ffn_hidden(g - 1)
            ffn_residual(g - 1, NQUAD - 1)
            for k in range(UNITS):
                dve.wait_ge(end_mm, k + 1)
                sl = slice(k * 512, (k + 1) * 512)
                tt(xtok[:, sl], QKV[k % 2][:], xtok[:, sl], ALU.add).then_inc(end_add, 1)


_ARRAYS = ["x", "ctx", "wgate", "bgate", "outnorm", "wqkv", "qscale", "kscale", "wo", "w1", "w2", "vec", "rot", "band", "causal"]


def kernel(**inputs):
    import numpy as _np
    import concourse.bacc as _bacc
    from concourse import mybir as _mybir
    from concourse.bass_utils import run_bass_kernel_spmd as _run

    i = {k: _np.asarray(v) for k, v in inputs.items()}
    f32 = _np.float32
    a = {"x": i["x"].reshape(NTOK, D), "ctx": i["ctx_1024"].reshape(NTOK, D)}
    a["wgate"] = _np.concatenate([i["L0_xattn_igate_kernel"], i["L0_xattn_fgate_kernel"]], 1)
    a["bgate"] = _np.concatenate([i["L0_xattn_igate_bias"], i["L0_xattn_fgate_bias"]])
    a["outnorm"] = i["L0_xattn_outnorm_scale"]
    a["wqkv"] = i["L0_ffn_Wqkv"]
    a["qscale"], a["kscale"] = i["L0_ffn_q_scale"], i["L0_ffn_k_scale"]
    a["wo"] = i["L0_ffn_Wo"].reshape(DEPTH, 8, 128, D).transpose(0, 2, 1, 3)
    a["w1"] = i["L0_ffn_W1"]
    w2 = _np.zeros((DEPTH, 384, D), f32)
    w2[:, :FF] = i["L0_ffn_W2"]
    a["w2"] = w2.reshape(DEPTH, 3, 128, D).transpose(0, 2, 1, 3)
    vec = _np.zeros((DEPTH, NVEC, 128), f32)
    vec[:, 0], vec[:, 1], vec[:, 2] = i["L0_ffn_ln_g"], i["L0_ffn_ln_b"], i["L0_ffn_b2"]
    for part in range(2):
        for c in range(3):
            vec[:, 3 + 3 * part + c, :FCH[c]] = i["L0_ffn_b1"][:, part * FF + c * 128:part * FF + c * 128 + FCH[c]]
    a["vec"] = vec.transpose(2, 0, 1).reshape(128, DEPTH * NVEC)
    a["rot"], a["band"], a["causal"] = constants()

    nc = _bacc.Bacc("TRN2", target_bir_lowering=False, num_devices=1)
    arrays, args = {}, []
    for name in _ARRAYS:
        arr = _np.ascontiguousarray(a[name])
        arrays[f"in_{name}"] = arr
        args.append(nc.dram_tensor(f"in_{name}", arr.shape, _mybir.dt.from_np(arr.dtype), kind="ExternalInput").ap())
    args.append(nc.dram_tensor("out_x", (NTOK, D), _mybir.dt.float32, kind="ExternalOutput").ap())
    transformer_program(nc, *args)
    r = _run(nc, [arrays], core_ids=[0])
    return r.results[0]["out_x"].reshape(NSEQ, S, D)
```
